# Optimizing a Trainium2 kernel written in Bass

```python
import numpy as np
import jax
import jax.numpy as jnp

def _softmax(x, axis=-1):
    return jax.nn.softmax(x, axis=axis)

def _gelu(x):
    return jax.nn.gelu(x, approximate=True)

def _silu(x):
    return jax.nn.silu(x)

def _sigmoid(x):
    return jax.nn.sigmoid(x)

def _layernorm(x, axis=-1, eps=1e-05):
    m = jnp.mean(x, axis=axis, keepdims=True)
    v = jnp.var(x, axis=axis, keepdims=True)
    return (x - m) / jnp.sqrt(v + eps)

def _scatter_add(tgt, idx, src, axis=0):
    return tgt.at[idx].add(src)

def _segment_sum(src, seg, n):
    return jax.ops.segment_sum(src, seg, n)
kernel_name = 'mk_seq_postln_d2_jaxref_r8_a16beb'

def setup_inputs(seed: int=0):
    np.random.seed(seed)
    _w = jnp.asarray

    def _L0_attn_setup():
        import jax, jax.numpy as jnp
        import numpy as np
        ROPE_BASE = 1250
        B, L, D, NH = (2, 256, 128, 16)
        HD = D // NH

        def apply_rope(inputs, positions, base_frequency):
            head_dim = inputs.shape[-1]
            fraction = 2 * jnp.arange(0, head_dim // 2) / head_dim
            timescale = base_frequency ** fraction
            sinusoid = positions[..., None] / timescale[None, None, :]
            sinusoid = sinusoid[..., None, :]
            sin, cos = (jnp.sin(sinusoid), jnp.cos(sinusoid))
            first, second = jnp.split(inputs, 2, axis=-1)
            out = jnp.concatenate([first * cos - second * sin, second * cos + first * sin], axis=-1)
            return out.astype(inputs.dtype)
        key = jax.random.key(seed)
        ks = jax.random.split(key, 5)
        s = 0.02
        return {'x': jax.random.normal(ks[0], (B, L, D), jnp.float32), 'wq_w': jax.random.normal(ks[1], (D, D), jnp.float32) * s, 'wq_b': jnp.zeros((D,), jnp.float32), 'wk_w': jax.random.normal(ks[2], (D, D), jnp.float32) * s, 'wk_b': jnp.zeros((D,), jnp.float32), 'wv_w': jax.random.normal(ks[3], (D, D), jnp.float32) * s, 'wv_b': jnp.zeros((D,), jnp.float32), 'wo_w': jax.random.normal(ks[4], (D, D), jnp.float32) * s, 'wo_b': jnp.zeros((D,), jnp.float32)}
    _L0_attn_in = _L0_attn_setup()

    def _L0_ffn_setup():
        import jax, jax.numpy as jnp
        import numpy as np
        DIM = 128
        DEPTH = 2
        HEADS = 8
        DIM_HEAD = 64
        WINDOW = 64
        INNER = HEADS * DIM_HEAD
        HID = int(DIM * 4 * 2 / 3)
        B, N = (2, 1024)
        QK_SCALE = 8.0

        def shift_token(t):
            t1, t2 = jnp.split(t, 2, axis=-1)
            t2 = jnp.pad(t2, ((0, 0), (1, 0), (0, 0)))[:, :-1]
            return jnp.concatenate([t1, t2], axis=-1)

        def l2norm(t):
            return t / jnp.clip(jnp.linalg.norm(t, axis=-1, keepdims=True), 1e-12)

        def rotate_half(x):
            x1, x2 = jnp.split(x, 2, axis=-1)
            return jnp.concatenate([-x2, x1], axis=-1)

        def rotary_xpos(q, k):
            n = q.shape[-2]
            half_idx = jnp.arange(0, DIM_HEAD, 2, dtype=jnp.float32)
            inv_freq = 1.0 / 10000.0 ** (half_idx / DIM_HEAD)
            t = jnp.arange(n, dtype=jnp.float32)
            freqs = t[:, None] * inv_freq[None, :]
            freqs = jnp.concatenate([freqs, freqs], axis=-1)
            base = (half_idx + 0.4 * DIM_HEAD) / (1.4 * DIM_HEAD)
            power = (t - n // 2) / float(WINDOW // 2)
            scale = base[None, :] ** power[:, None]
            scale = jnp.concatenate([scale, scale], axis=-1)
            cos, sin = (jnp.cos(freqs), jnp.sin(freqs))
            q = q * cos * scale + rotate_half(q) * sin * scale
            k = k * cos / scale + rotate_half(k) * sin / scale
            return (q, k)

        def local_attention(q, k, v):
            b, h, n, d = q.shape
            w = n // WINDOW
            bq = q.reshape(b, h, w, WINDOW, d) * QK_SCALE
            bk = k.reshape(b, h, w, WINDOW, d)
            bv = v.reshape(b, h, w, WINDOW, d)

            def look_around(t):
                p = jnp.pad(t, ((0, 0), (0, 0), (1, 0), (0, 0), (0, 0)))
                return jnp.concatenate([p[:, :, :w], p[:, :, 1:]], axis=3)
            bk, bv = (look_around(bk), look_around(bv))
            bt = jnp.arange(n).reshape(w, WINDOW)
            btp = jnp.pad(bt, ((1, 0), (0, 0)), constant_values=-1)
            btk = jnp.concatenate([btp[:w], btp[1:]], axis=1)
            sim = jnp.einsum('bhwid,bhwjd->bhwij', bq, bk)
            i = bt[:, :, None]
            j = btk[:, None, :]
            mask = (i < j) | (i > j + WINDOW) | (j == -1)
            sim = jnp.where(mask, -jnp.finfo(sim.dtype).max, sim)
            attn = jax.nn.softmax(sim, axis=-1)
            out = jnp.einsum('bhwij,bhwjd->bhwid', attn, bv)
            return out.reshape(b, h, n, d)

        def _layer(x, wqkv, qs, ksc, wo, lg, lb, w1, b1, w2, b2):
            b, n, _ = x.shape
            h = shift_token(x)
            qkv = h @ wqkv
            q, k, v = jnp.split(qkv, 3, axis=-1)
            to_heads = lambda t: t.reshape(b, n, HEADS, DIM_HEAD).transpose(0, 2, 1, 3)
            q, k, v = (to_heads(q), to_heads(k), to_heads(v))
            q = l2norm(q) * qs
            k = l2norm(k) * ksc
            q, k = rotary_xpos(q, k)
            o = local_attention(q, k, v)
            o = o.transpose(0, 2, 1, 3).reshape(b, n, INNER)
            x = x + o @ wo
            h = shift_token(x)
            mu = h.mean(-1, keepdims=True)
            var = h.var(-1, keepdims=True)
            h = (h - mu) / jnp.sqrt(var + 1e-05) * lg + lb
            h = h @ w1 + b1
            a, g = jnp.split(h, 2, axis=-1)
            h = a * jax.nn.gelu(g, approximate=False)
            x = x + h @ w2 + b2
            return x
        key = jax.random.key(seed)
        ks = jax.random.split(key, 6)
        return {'x': jax.random.normal(ks[0], (B, N, DIM), jnp.float32), 'wqkv': jax.random.normal(ks[1], (DEPTH, DIM, 3 * INNER), jnp.float32) * 0.02, 'q_scale': jnp.ones((DEPTH, DIM_HEAD), jnp.float32), 'k_scale': jnp.ones((DEPTH, DIM_HEAD), jnp.float32), 'wo': jax.random.normal(ks[2], (DEPTH, INNER, DIM), jnp.float32) * 0.02, 'ln_g': jnp.ones((DEPTH, DIM), jnp.float32), 'ln_b': jnp.zeros((DEPTH, DIM), jnp.float32), 'w1': jax.random.normal(ks[3], (DEPTH, DIM, 2 * HID), jnp.float32) * 0.02, 'b1': jnp.zeros((DEPTH, 2 * HID), jnp.float32), 'w2': jax.random.normal(ks[4], (DEPTH, HID, DIM), jnp.float32) * 0.02, 'b2': jnp.zeros((DEPTH, DIM), jnp.float32)}
    _L0_ffn_in = _L0_ffn_setup()

    def _L1_attn_setup():
        import jax, jax.numpy as jnp
        import numpy as np
        B, S, D, H = (4, 256, 128, 16)
        DH = D // H
        key = jax.random.key(seed)
        ks = jax.random.split(key, 5)
        std = 1.0 / np.sqrt(D)
        return {'x': jax.random.normal(ks[0], (B, S, D), dtype=jnp.float32), 'mask': jnp.ones((S, S), dtype=bool), 'Wq': jax.random.normal(ks[1], (D, D), dtype=jnp.float32) * std, 'Wk': jax.random.normal(ks[2], (D, D), dtype=jnp.float32) * std, 'Wv': jax.random.normal(ks[3], (D, D), dtype=jnp.float32) * std, 'Wout': jax.random.normal(ks[4], (D, D), dtype=jnp.float32) * std}
    _L1_attn_in = _L1_attn_setup()

    def _L1_ffn_setup():
        import jax, jax.numpy as jnp
        import numpy as np
        EPS = 1e-05

        def _layernorm(x, w, b):
            mu = jnp.mean(x, axis=-1, keepdims=True)
            var = jnp.mean((x - mu) ** 2, axis=-1, keepdims=True)
            return (x - mu) * jax.lax.rsqrt(var + EPS) * w + b

        def _rope_tables(T, D, base=10000.0):
            inv_freq = 1.0 / base ** (jnp.arange(0, D, 2, dtype=jnp.float32) / D)
            t = jnp.arange(T, dtype=jnp.float32)
            freqs = jnp.einsum('i,j->ij', t, inv_freq)
            emb = jnp.concatenate([freqs, freqs], axis=-1)
            return (jnp.cos(emb), jnp.sin(emb))

        def _rotate_half(x):
            x1, x2 = (x[..., :x.shape[-1] // 2], x[..., x.shape[-1] // 2:])
            return jnp.concatenate([-x2, x1], axis=-1)

        def _attn(x, ln_w, ln_b, conv_w, attn_w, proj_w, n_head):
            B, T, C = x.shape
            D = C // n_head
            h = _layernorm(x, ln_w, ln_b)
            hc = jnp.transpose(h, (0, 2, 1))
            hc = jnp.pad(hc, ((0, 0), (0, 0), (2, 0)))
            hc = jax.lax.conv_general_dilated(hc, conv_w, window_strides=(1,), padding='VALID', dimension_numbers=('NCH', 'OIH', 'NCH'), feature_group_count=C)
            h = jnp.transpose(hc, (0, 2, 1))
            qkv = h @ attn_w
            q, k, v = jnp.split(qkv, 3, axis=-1)
            q = q.reshape(B, T, n_head, D)
            k = k.reshape(B, T, n_head, D)
            v = v.reshape(B, T, n_head, D)
            cos, sin = _rope_tables(T, D)
            cos = cos[None, :, None, :]
            sin = sin[None, :, None, :]
            q = q * cos + _rotate_half(q) * sin
            k = k * cos + _rotate_half(k) * sin
            scores = jnp.einsum('bqhd,bkhd->bhqk', q, k) / jnp.sqrt(jnp.float32(D))
            causal = jnp.tril(jnp.ones((T, T), dtype=bool))
            scores = jnp.where(causal, scores, jnp.float32(-1e+30))
            p = jax.nn.softmax(scores, axis=-1)
            y = jnp.einsum('bhqk,bkhd->bqhd', p, v).reshape(B, T, C)
            return y @ proj_w

        def _moe(x, ln_w, ln_b, router_w, expert_wv, expert_proj):
            h = _layernorm(x, ln_w, ln_b)
            logits = h @ router_w
            expert_idx = jnp.argmax(logits, axis=-1)
            E = router_w.shape[-1]
            out = jnp.zeros_like(x)
            for e in range(E):
                gv = h @ expert_wv[e]
                gate_raw, value = jnp.split(gv, 2, axis=-1)
                y = gate_raw * jax.nn.sigmoid(gate_raw) * value @ expert_proj[e]
                out = out + jnp.where((expert_idx == e)[..., None], y, 0.0)
            return out
        C, H, E, B, T = (128, 16, 4, 4, 128)
        Dff = 4 * C
        key = jax.random.key(seed)
        ks = jax.random.split(key, 8)
        s = 0.02
        return {'x': jax.random.normal(ks[0], (B, T, C), dtype=jnp.float32), 'ln1_w': jnp.ones((C,), jnp.float32), 'ln1_b': jnp.zeros((C,), jnp.float32), 'ln2_w': jnp.ones((C,), jnp.float32), 'ln2_b': jnp.zeros((C,), jnp.float32), 'conv_w': jax.random.normal(ks[1], (C, 1, 3), dtype=jnp.float32) * 0.1, 'attn_w': jax.random.normal(ks[2], (C, 3 * C), dtype=jnp.float32) * s, 'proj_w': jax.random.normal(ks[3], (C, C), dtype=jnp.float32) * s, 'router_w': jax.random.normal(ks[4], (C, E), dtype=jnp.float32) * s, 'expert_wv': jax.random.normal(ks[5], (E, C, 2 * Dff), dtype=jnp.float32) * s, 'expert_proj': jax.random.normal(ks[6], (E, Dff, C), dtype=jnp.float32) * s}
    _L1_ffn_in = _L1_ffn_setup()
    _d = {'L0_attn_x': _L0_attn_in['x'], 'L0_attn_wq_w': _L0_attn_in['wq_w'], 'L0_attn_wq_b': _L0_attn_in['wq_b'], 'L0_attn_wk_w': _L0_attn_in['wk_w'], 'L0_attn_wk_b': _L0_attn_in['wk_b'], 'L0_attn_wv_w': _L0_attn_in['wv_w'], 'L0_attn_wv_b': _L0_attn_in['wv_b'], 'L0_attn_wo_w': _L0_attn_in['wo_w'], 'L0_attn_wo_b': _L0_attn_in['wo_b'], 'L0_ffn_wqkv': _L0_ffn_in['wqkv'], 'L0_ffn_q_scale': _L0_ffn_in['q_scale'], 'L0_ffn_k_scale': _L0_ffn_in['k_scale'], 'L0_ffn_wo': _L0_ffn_in['wo'], 'L0_ffn_ln_g': _L0_ffn_in['ln_g'], 'L0_ffn_ln_b': _L0_ffn_in['ln_b'], 'L0_ffn_w1': _L0_ffn_in['w1'], 'L0_ffn_b1': _L0_ffn_in['b1'], 'L0_ffn_w2': _L0_ffn_in['w2'], 'L0_ffn_b2': _L0_ffn_in['b2'], 'L1_attn_mask': _L1_attn_in['mask'], 'L1_attn_Wq': _L1_attn_in['Wq'], 'L1_attn_Wk': _L1_attn_in['Wk'], 'L1_attn_Wv': _L1_attn_in['Wv'], 'L1_attn_Wout': _L1_attn_in['Wout'], 'L1_ffn_ln1_w': _L1_ffn_in['ln1_w'], 'L1_ffn_ln1_b': _L1_ffn_in['ln1_b'], 'L1_ffn_ln2_w': _L1_ffn_in['ln2_w'], 'L1_ffn_ln2_b': _L1_ffn_in['ln2_b'], 'L1_ffn_conv_w': _L1_ffn_in['conv_w'], 'L1_ffn_attn_w': _L1_ffn_in['attn_w'], 'L1_ffn_proj_w': _L1_ffn_in['proj_w'], 'L1_ffn_router_w': _L1_ffn_in['router_w'], 'L1_ffn_expert_wv': _L1_ffn_in['expert_wv'], 'L1_ffn_expert_proj': _L1_ffn_in['expert_proj']}
    _x0 = _d['L0_attn_x']
    _d['L0_attn_x'] = jax.random.normal(jax.random.fold_in(jax.random.key(seed), 1), (8, 512, 128), dtype=_x0.dtype)
    del _x0
    return _d

def reference(L0_attn_x, L0_attn_wq_w, L0_attn_wq_b, L0_attn_wk_w, L0_attn_wk_b, L0_attn_wv_w, L0_attn_wv_b, L0_attn_wo_w, L0_attn_wo_b, L0_ffn_wqkv, L0_ffn_q_scale, L0_ffn_k_scale, L0_ffn_wo, L0_ffn_ln_g, L0_ffn_ln_b, L0_ffn_w1, L0_ffn_b1, L0_ffn_w2, L0_ffn_b2, L1_attn_mask, L1_attn_Wq, L1_attn_Wk, L1_attn_Wv, L1_attn_Wout, L1_ffn_ln1_w, L1_ffn_ln1_b, L1_ffn_ln2_w, L1_ffn_ln2_b, L1_ffn_conv_w, L1_ffn_attn_w, L1_ffn_proj_w, L1_ffn_router_w, L1_ffn_expert_wv, L1_ffn_expert_proj):

    def _L0_attn_ref(x, wq_w, wq_b, wk_w, wk_b, wv_w, wv_b, wo_w, wo_b):
        import jax, jax.numpy as jnp
        import numpy as np
        ROPE_BASE = 1250
        B, L, D, NH = (2, 256, 128, 16)
        HD = D // NH

        def apply_rope(inputs, positions, base_frequency):
            head_dim = inputs.shape[-1]
            fraction = 2 * jnp.arange(0, head_dim // 2) / head_dim
            timescale = base_frequency ** fraction
            sinusoid = positions[..., None] / timescale[None, None, :]
            sinusoid = sinusoid[..., None, :]
            sin, cos = (jnp.sin(sinusoid), jnp.cos(sinusoid))
            first, second = jnp.split(inputs, 2, axis=-1)
            out = jnp.concatenate([first * cos - second * sin, second * cos + first * sin], axis=-1)
            return out.astype(inputs.dtype)
        b, l, _ = x.shape
        q = (x @ wq_w + wq_b).reshape(b, l, NH, HD)
        k = (x @ wk_w + wk_b).reshape(b, l, NH, HD)
        v = (x @ wv_w + wv_b).reshape(b, l, NH, HD)
        pos = jnp.arange(l)
        q = apply_rope(q, pos, ROPE_BASE)
        k = apply_rope(k, pos, ROPE_BASE)
        q = q.transpose(0, 2, 1, 3)
        k = k.transpose(0, 2, 1, 3)
        v = v.transpose(0, 2, 1, 3)
        scale = jnp.sqrt(jnp.asarray(HD, q.dtype))
        scores = jnp.einsum('bnqh,bnkh->bnqk', q, k) / scale
        causal = jnp.tril(jnp.ones((l, l), bool))
        scores = jnp.where(causal, scores, jnp.finfo(scores.dtype).min)
        attn = jax.nn.softmax(scores, axis=-1)
        ctx = jnp.einsum('bnqk,bnkh->bnqh', attn, v)
        ctx = ctx.transpose(0, 2, 1, 3).reshape(b, l, D)
        return ctx @ wo_w + wo_b

    def _L0_ffn_ref(x, wqkv, q_scale, k_scale, wo, ln_g, ln_b, w1, b1, w2, b2):
        import jax, jax.numpy as jnp
        import numpy as np
        DIM = 128
        DEPTH = 2
        HEADS = 8
        DIM_HEAD = 64
        WINDOW = 64
        INNER = HEADS * DIM_HEAD
        HID = int(DIM * 4 * 2 / 3)
        B, N = (2, 1024)
        QK_SCALE = 8.0

        def shift_token(t):
            t1, t2 = jnp.split(t, 2, axis=-1)
            t2 = jnp.pad(t2, ((0, 0), (1, 0), (0, 0)))[:, :-1]
            return jnp.concatenate([t1, t2], axis=-1)

        def l2norm(t):
            return t / jnp.clip(jnp.linalg.norm(t, axis=-1, keepdims=True), 1e-12)

        def rotate_half(x):
            x1, x2 = jnp.split(x, 2, axis=-1)
            return jnp.concatenate([-x2, x1], axis=-1)

        def rotary_xpos(q, k):
            n = q.shape[-2]
            half_idx = jnp.arange(0, DIM_HEAD, 2, dtype=jnp.float32)
            inv_freq = 1.0 / 10000.0 ** (half_idx / DIM_HEAD)
            t = jnp.arange(n, dtype=jnp.float32)
            freqs = t[:, None] * inv_freq[None, :]
            freqs = jnp.concatenate([freqs, freqs], axis=-1)
            base = (half_idx + 0.4 * DIM_HEAD) / (1.4 * DIM_HEAD)
            power = (t - n // 2) / float(WINDOW // 2)
            scale = base[None, :] ** power[:, None]
            scale = jnp.concatenate([scale, scale], axis=-1)
            cos, sin = (jnp.cos(freqs), jnp.sin(freqs))
            q = q * cos * scale + rotate_half(q) * sin * scale
            k = k * cos / scale + rotate_half(k) * sin / scale
            return (q, k)

        def local_attention(q, k, v):
            b, h, n, d = q.shape
            w = n // WINDOW
            bq = q.reshape(b, h, w, WINDOW, d) * QK_SCALE
            bk = k.reshape(b, h, w, WINDOW, d)
            bv = v.reshape(b, h, w, WINDOW, d)

            def look_around(t):
                p = jnp.pad(t, ((0, 0), (0, 0), (1, 0), (0, 0), (0, 0)))
                return jnp.concatenate([p[:, :, :w], p[:, :, 1:]], axis=3)
            bk, bv = (look_around(bk), look_around(bv))
            bt = jnp.arange(n).reshape(w, WINDOW)
            btp = jnp.pad(bt, ((1, 0), (0, 0)), constant_values=-1)
            btk = jnp.concatenate([btp[:w], btp[1:]], axis=1)
            sim = jnp.einsum('bhwid,bhwjd->bhwij', bq, bk)
            i = bt[:, :, None]
            j = btk[:, None, :]
            mask = (i < j) | (i > j + WINDOW) | (j == -1)
            sim = jnp.where(mask, -jnp.finfo(sim.dtype).max, sim)
            attn = jax.nn.softmax(sim, axis=-1)
            out = jnp.einsum('bhwij,bhwjd->bhwid', attn, bv)
            return out.reshape(b, h, n, d)

        def _layer(x, wqkv, qs, ksc, wo, lg, lb, w1, b1, w2, b2):
            b, n, _ = x.shape
            h = shift_token(x)
            qkv = h @ wqkv
            q, k, v = jnp.split(qkv, 3, axis=-1)
            to_heads = lambda t: t.reshape(b, n, HEADS, DIM_HEAD).transpose(0, 2, 1, 3)
            q, k, v = (to_heads(q), to_heads(k), to_heads(v))
            q = l2norm(q) * qs
            k = l2norm(k) * ksc
            q, k = rotary_xpos(q, k)
            o = local_attention(q, k, v)
            o = o.transpose(0, 2, 1, 3).reshape(b, n, INNER)
            x = x + o @ wo
            h = shift_token(x)
            mu = h.mean(-1, keepdims=True)
            var = h.var(-1, keepdims=True)
            h = (h - mu) / jnp.sqrt(var + 1e-05) * lg + lb
            h = h @ w1 + b1
            a, g = jnp.split(h, 2, axis=-1)
            h = a * jax.nn.gelu(g, approximate=False)
            x = x + h @ w2 + b2
            return x
        for l in range(DEPTH):
            x = _layer(x, wqkv[l], q_scale[l], k_scale[l], wo[l], ln_g[l], ln_b[l], w1[l], b1[l], w2[l], b2[l])
        return x

    def _L1_attn_ref(x, mask, Wq, Wk, Wv, Wout):
        import jax, jax.numpy as jnp
        import numpy as np
        B, S, D, H = (4, 256, 128, 16)
        DH = D // H
        n, s, d = x.shape
        scale = 1.0 / np.sqrt(DH).astype(np.float32)
        q = (x @ Wq).reshape(n, s, H, DH)
        k = (x @ Wk).reshape(n, s, H, DH)
        v = (x @ Wv).reshape(n, s, H, DH)
        attn = jnp.einsum('nqhd,nkhd->nqkh', q, k) * scale
        attn = jax.nn.softmax(attn, axis=-2)
        z = jnp.einsum('nqkh,nkhd->nqhd', attn, v).reshape(n, s, d)
        z = jnp.einsum('nqd,de->nqe', z, Wout)
        return x + z

    def _L1_ffn_ref(x, ln1_w, ln1_b, ln2_w, ln2_b, conv_w, attn_w, proj_w, router_w, expert_wv, expert_proj):
        import jax, jax.numpy as jnp
        import numpy as np
        EPS = 1e-05

        def _layernorm(x, w, b):
            mu = jnp.mean(x, axis=-1, keepdims=True)
            var = jnp.mean((x - mu) ** 2, axis=-1, keepdims=True)
            return (x - mu) * jax.lax.rsqrt(var + EPS) * w + b

        def _rope_tables(T, D, base=10000.0):
            inv_freq = 1.0 / base ** (jnp.arange(0, D, 2, dtype=jnp.float32) / D)
            t = jnp.arange(T, dtype=jnp.float32)
            freqs = jnp.einsum('i,j->ij', t, inv_freq)
            emb = jnp.concatenate([freqs, freqs], axis=-1)
            return (jnp.cos(emb), jnp.sin(emb))

        def _rotate_half(x):
            x1, x2 = (x[..., :x.shape[-1] // 2], x[..., x.shape[-1] // 2:])
            return jnp.concatenate([-x2, x1], axis=-1)

        def _attn(x, ln_w, ln_b, conv_w, attn_w, proj_w, n_head):
            B, T, C = x.shape
            D = C // n_head
            h = _layernorm(x, ln_w, ln_b)
            hc = jnp.transpose(h, (0, 2, 1))
            hc = jnp.pad(hc, ((0, 0), (0, 0), (2, 0)))
            hc = jax.lax.conv_general_dilated(hc, conv_w, window_strides=(1,), padding='VALID', dimension_numbers=('NCH', 'OIH', 'NCH'), feature_group_count=C)
            h = jnp.transpose(hc, (0, 2, 1))
            qkv = h @ attn_w
            q, k, v = jnp.split(qkv, 3, axis=-1)
            q = q.reshape(B, T, n_head, D)
            k = k.reshape(B, T, n_head, D)
            v = v.reshape(B, T, n_head, D)
            cos, sin = _rope_tables(T, D)
            cos = cos[None, :, None, :]
            sin = sin[None, :, None, :]
            q = q * cos + _rotate_half(q) * sin
            k = k * cos + _rotate_half(k) * sin
            scores = jnp.einsum('bqhd,bkhd->bhqk', q, k) / jnp.sqrt(jnp.float32(D))
            causal = jnp.tril(jnp.ones((T, T), dtype=bool))
            scores = jnp.where(causal, scores, jnp.float32(-1e+30))
            p = jax.nn.softmax(scores, axis=-1)
            y = jnp.einsum('bhqk,bkhd->bqhd', p, v).reshape(B, T, C)
            return y @ proj_w

        def _moe(x, ln_w, ln_b, router_w, expert_wv, expert_proj):
            h = _layernorm(x, ln_w, ln_b)
            logits = h @ router_w
            expert_idx = jnp.argmax(logits, axis=-1)
            E = router_w.shape[-1]
            out = jnp.zeros_like(x)
            for e in range(E):
                gv = h @ expert_wv[e]
                gate_raw, value = jnp.split(gv, 2, axis=-1)
                y = gate_raw * jax.nn.sigmoid(gate_raw) * value @ expert_proj[e]
                out = out + jnp.where((expert_idx == e)[..., None], y, 0.0)
            return out
        n_head = 16
        x = x + _attn(x, ln1_w, ln1_b, conv_w, attn_w, proj_w, n_head)
        x = x + _moe(x, ln2_w, ln2_b, router_w, expert_wv, expert_proj)
        return x
    x = L0_attn_x
    x = _layernorm(x + _L0_attn_ref(x, L0_attn_wq_w, L0_attn_wq_b, L0_attn_wk_w, L0_attn_wk_b, L0_attn_wv_w, L0_attn_wv_b, L0_attn_wo_w, L0_attn_wo_b), axis=-1)
    x = _layernorm(x + _L0_ffn_ref(x, L0_ffn_wqkv, L0_ffn_q_scale, L0_ffn_k_scale, L0_ffn_wo, L0_ffn_ln_g, L0_ffn_ln_b, L0_ffn_w1, L0_ffn_b1, L0_ffn_w2, L0_ffn_b2), axis=-1)
    x = _layernorm(x + _L1_attn_ref(x, L1_attn_mask, L1_attn_Wq, L1_attn_Wk, L1_attn_Wv, L1_attn_Wout), axis=-1)
    x = _layernorm(x + _L1_ffn_ref(x, L1_ffn_ln1_w, L1_ffn_ln1_b, L1_ffn_ln2_w, L1_ffn_ln2_b, L1_ffn_conv_w, L1_ffn_attn_w, L1_ffn_proj_w, L1_ffn_router_w, L1_ffn_expert_wv, L1_ffn_expert_proj), axis=-1)
    return x

_drawn_inputs = setup_inputs


def setup_inputs(seed=0):
    import zlib

    import numpy as np

    out = dict(_drawn_inputs(seed))
    spreads = {'L0_attn_wq_b': (0.0, 0.8),
     'L0_attn_wk_b': (0.0, 0.8),
     'L0_attn_wv_b': (0.0, 0.304),
     'L0_attn_wo_b': (0.0, 0.1),
     'L0_ffn_q_scale': (1.0, 0.6),
     'L0_ffn_k_scale': (1.0, 0.6),
     'L0_ffn_ln_g': (1.0, 0.6),
     'L0_ffn_ln_b': (0.0, 0.8),
     'L0_ffn_b1': (0.0, 0.8),
     'L0_ffn_b2': (0.0, 0.1),
     'L1_ffn_ln1_w': (1.0, 0.6),
     'L1_ffn_ln1_b': (0.0, 0.8),
     'L1_ffn_ln2_w': (1.0, 0.6),
     'L1_ffn_ln2_b': (0.0, 0.8)}
    factors = {'L0_attn_wq_w': 8.0,
     'L0_attn_wk_w': 8.0,
     'L0_attn_wv_w': 8.0,
     'L0_ffn_wqkv': 3.091,
     'L0_ffn_wo': 3.156,
     'L0_ffn_w1': 6.208,
     'L0_ffn_w2': 6.087,
     'L1_ffn_conv_w': 8.0,
     'L1_ffn_attn_w': 8.0,
     'L1_ffn_proj_w': 8.0,
     'L1_ffn_router_w': 8.0,
     'L1_ffn_expert_wv': 8.0,
     'L1_ffn_expert_proj': 8.0}
    for name, (base, spread) in spreads.items():
        noise = np.random.default_rng([zlib.crc32(name.encode()), seed]).standard_normal(out[name].shape)
        drawn = base * np.exp(spread * noise) if base else spread * noise
        out[name] = jnp.asarray(drawn.astype(out[name].dtype))
    for name, factor in factors.items():
        out[name] = (out[name] * factor).astype(out[name].dtype)
    return out
```

```python
import concourse.bass as bass
from concourse import mybir
from contextlib import ExitStack

B, L, C = 8, 512, 128
P = 128
NT = L // P
H, HD = 16, 8
HG = 4
NG = H // HG
SLOT = 32
MSLOT = 3 * HD
LH, LD, WIN = 8, 64, 64
BAND = P + WIN
HID = 341
HB = [128, 128, HID - 256]
NE, FF = 4, 512
EPS = 1e-5
NEG = -1.0e30


def network_kernel(nc: bass.Bass, ins, consts, out: bass.AP):
    fp32, fp32r, bf16 = mybir.dt.float32, mybir.dt.float32r, mybir.dt.bfloat16
    ALU = mybir.AluOpType
    ACT = mybir.ActivationFunctionType
    X = mybir.AxisListType.X

    ctx = ExitStack()
    with ctx:
        def sb(name, shape, dt=fp32):
            return ctx.enter_context(nc.sbuf_tensor(name, shape, dt))

        class Signal:

            def __init__(self, name, per_batch):
                self.sem, self.per = ctx.enter_context(nc.semaphore(name)), per_batch

            def at(self, b, n):
                return b * self.per + n

        ident = sb("ident", [P, P])
        ident_h = sb("ident_h", [P, P], bf16)
        shift = sb("shift", [P, 2, P])
        mask_h = sb("mask_h", [P, 2 * P + 3 * BAND], bf16)
        causal_qk = mask_h[:, 0:P]
        causal_kq = mask_h[:, P:2 * P]
        band_qk = mask_h[:, 2 * P:2 * P + BAND]
        band_q0 = mask_h[:, 2 * P + BAND:2 * P + 2 * BAND]
        band_kq = mask_h[:, 2 * P + 2 * BAND:2 * P + 3 * BAND]
        sel = sb("sel", [LH, LH * P], fp32r)
        rope = {s: sb(f"rope_{s}", [P, NT, 2, HD]) for s in "AD"}
        wqkv = {s: sb(f"wqkv_{s}", [P, 3 * C]) for s in "ACD"}
        wout = {s: sb(f"wout_{s}", [P, C]) for s in "ACD"}
        bqkv = sb("bqkv", [P, 3 * C])
        bout = sb("bout", [P, C])
        lw_qkv = sb("lw_qkv", [P, 2, 3 * LH * LD])
        lw_o = sb("lw_o", [P, 2, 4, C])
        lw_1 = sb("lw_1", [P, 2, 2 * HID])
        lw_2 = sb("lw_2", [P, 2, 3, C])
        lb_1 = sb("lb_1", [P, 2, 2, 3])
        lb_2 = sb("lb_2", [P, 2, C])
        l_gb = sb("l_gb", [P, 2, 2])
        l_scale = sb("l_scale", [P, 2, 2, 2, LD])
        tab = sb("tab", [P, 2, NT, 2, 2, LD])
        ln1 = sb("ln1", [P, 2])
        ln2 = sb("ln2", [P, 2])
        conv = sb("conv", [P, 3])
        router = sb("router", [P, NE])
        e_wv = sb("e_wv", [P, NE, 2 * FF])
        e_pr = sb("e_pr", [P, NE, FF // P, C])
        m_half = sb("m_half", [P, 4 * LH * 2])

        xin = sb("xin", [P, NT, C])
        xa = sb("xa", [P, NT, C])
        xb = sb("xb", [P, NT, C])
        xc = sb("xc", [P, NT, C])
        y = sb("y", [P, NT, C])
        l_x = sb("l_x", [P, 2, NT, C])
        l_m = sb("l_m", [P, NT, C])
        hn = sb("hn", [P, NT, C])
        xT = sb("xT", [P, L])
        xsT = sb("xsT", [P, L])
        hT = sb("hT", [P, L + 2])
        cT = sb("cT", [P, 2, L])
        stack = sb("stack", [P, NT, 2, H, SLOT], fp32r)
        vaug = sb("vaug", [P, NT, H, HD + 1])
        stats = sb("stats", [P, NT, 2, 6])
        held = sb("held", [P, 1])
        mv = sb("mv", [P, NT, 2])
        rstd = sb("rstd", [P, NT])
        l_v = sb("l_v", [P, NT, LH, LD + 1])
        moe = sb("moe", [P, NT, C])
        yo = sb("yo", [P, NT, C])

        with ExitStack() as shared:
            def over(name, shape, dt=fp32):
                return shared.enter_context(nc.sbuf_tensor(name, shape, dt))

            xpos = over("xpos", [P, NT, 2, 2, LD])
            sel_f = over("sel_f", [LH, LH * P])
            mask_f = over("mask_f", [P, 2 * P + 3 * BAND])
            qk = over("qk", [P, NT, 2 * H, HD])
            qk_c = over("qk_c", [P, NT, 2 * H, HD])
            qk_s = over("qk_s", [P, NT, 2 * H, HD])
            KT = over("KT", [P, NG, L], fp32r)
            QT = over("QT", [P, NG, L], fp32r)
            QM = over("QM", [P, NG, L], fp32r)
            prob = over("prob", [P, 2, NT, L])
            rden = over("rden", [P, NT, H])
            heads = over("heads", [P, NT, C])
            headsT = over("headsT", [P, L])
        with ExitStack() as shared:
            sq = over("sq", [P, 2, 2 * LH * LD])
            l_c = over("l_c", [P, NT, 2 * LH, LD])
            l_s = over("l_s", [P, 2, 2 * LH, LD])
            ssum = over("ssum", [P, NT, 2 * LH])
            rn = over("rn", [P, NT, 2 * LH])
            l_T = over("l_T", [P, 8, L])
            nm = over("nm", [P, NT, LH])
            nmT = over("nmT", [LH, L], fp32r)
            l_p = over("l_p", [P, 2, NT, BAND])
            l_rd = over("l_rd", [P, 2, NT])
            l_o = l_s[:, :, :, :].rearrange("p a h d -> p (a h d)").rearrange("p (t n) -> p t n", t=NT)
            l_oT = l_T[:, 0:4]
            gel = l_T[:, 4:7]
            hidT = over("hidT", [P, 3, L])
        with ExitStack() as shared:
            sil = over("sil", [P, 2, L])
            eact = over("eact", [P, 2, FF // P, L])
            lg = over("lg", [P, NT, NE])
            lmax = over("lmax", [P, NT])
            free = over("free", [P, NT])
            pick = over("pick", [P, NT, NE])

        ps = ctx.enter_context(nc.psum_tensor("ps", [P, 8, 512], fp32))

        def bank(i):
            return ps[:, i, :]

        stack_f = stack[:, :, :, :, :].bitcast(fp32)

        loaded = ctx.enter_context(nc.semaphore("weights_loaded"))
        consts_ready = ctx.enter_context(nc.semaphore("consts_ready"))
        x_in = Signal("x_in", 16)
        x_out = Signal("x_out", 16)
        y_final = Signal("y_final", 1)
        xin_used = Signal("xin_used", 1)
        dstep = Signal("dve_step", 0)
        pstep = Signal("pool_step", 0)
        S = {}

        def signals(stages, **per):
            for k, n in per.items():
                whole = Signal(f"{k}_{stages}", n * len(stages))
                for i, s in enumerate(stages):
                    S[s + k] = Part(whole, i * n)

        class Part:
            def __init__(self, whole, offset):
                self.sem, self.whole, self.offset = whole.sem, whole, offset

            def at(self, b, n):
                return self.whole.at(b, self.offset + n)

        signals("AC", xT_ps=1)
        signals("ACD", xT=1, qkv_ps=4, stacked=1, dup=1, kq_ps=8, kq=8, sc_ps=H * NT, mx=H * NT,
                qm_ps=NG, qm=NG, st_ps=H * NT, ex=H * NT, pv=H, ctx=1, cT_ps=1, cT=1, o_ps=1)
        signals("01", xT_ps=1, xT=1, qkv_ps=NT, sq=NT, v=NT, roped=NT, ssum=1, rn=1, nrm=NT, T_ps=8, T=8,
                sc_ps=LH, mx=LH, nm_ps=1, nmT=1, st_ps=LH, ex=LH, pv=LH, o=LH, oT_ps=4, oT=4, o_ps=1,
                lm=1, sh_ps=1, g_ps=3, gel=3, hid=3, f_ps=1, lx=1)
        signals("01NM", hn=1, hT_ps=1)
        signals("01M", hT=1)
        signals("A01BCNMF", var=1, rstd=1)
        signals("ABC", res=1)
        signals("M", lg_ps=1, g_ps=16, sil=16, act=16, e_ps=NE, acc=NE)

        block = ctx.enter_context(nc.Block())
        CAUSAL = {"A": True, "C": False, "D": True}
        SRC = {"A": xin, "C": xb, "D": None}
        SCALE = float(HD) ** -0.5
        LSCALE = 8.0

        def first(s, i):
            return i * P if CAUSAL[s] else 0

        n_loads = [0]

        @block.sync
        def _(sp):
            def load(dst, src):
                sp.dma_start(dst, src).then_inc(loaded, 16)
                n_loads[0] += 1

            def row(ap):
                n = ap.shape[0]
                return ap.rearrange("(a n) -> a n", a=1).broadcast_to([P, n])

            load(ident[:, :], consts["ident"])
            load(mask_f[:, :], consts["masks"])
            load(shift[:, :, :], consts["shift"])
            load(sel_f[:, :], consts["sel"])
            load(rope["A"][:, :, :, :], consts["rope_A"])
            load(rope["D"][:, :, :, :], consts["rope_D"])
            load(xpos[:, :, :, :, :], consts["xpos"])
            for i, n in enumerate(("wq", "wk", "wv")):
                load(wqkv["A"][:, i * C:(i + 1) * C], ins[f"L0_attn_{n}_w"])
                load(bqkv[:, i * C:(i + 1) * C], row(ins[f"L0_attn_{n}_b"]))
            load(wout["A"][:, :], ins["L0_attn_wo_w"])
            load(bout[:, :], row(ins["L0_attn_wo_b"]))
            for i, n in enumerate(("Wq", "Wk", "Wv")):
                load(wqkv["C"][:, i * C:(i + 1) * C], ins[f"L1_attn_{n}"])
            load(wout["C"][:, :], ins["L1_attn_Wout"])
            load(wqkv["D"][:, :], ins["L1_ffn_attn_w"])
            load(wout["D"][:, :], ins["L1_ffn_proj_w"])
            load(lw_qkv[:, :, :], ins["L0_ffn_wqkv"].rearrange("l c n -> c l n"))
            for l in range(2):
                load(lw_o[:, l], ins["L0_ffn_wo"][l].rearrange("(k c) n -> c k n", c=P))
                load(lw_2[:, l, 0:2], ins["L0_ffn_w2"][l, 0:256].rearrange("(k c) n -> c k n", c=P))
                load(lw_2[0:HB[2], l, 2], ins["L0_ffn_w2"][l, 256:HID])
                load(lb_2[:, l], row(ins["L0_ffn_b2"][l]))
                for half in range(2):
                    for j, n in enumerate(HB):
                        c0 = half * HID + j * P
                        load(lb_1[0:n, l, half, j:j + 1], ins["L0_ffn_b1"][l, c0:c0 + n].rearrange("(c a) -> c a", a=1))
                load(l_gb[:, l, 0:1], ins["L0_ffn_ln_g"][l].rearrange("(c a) -> c a", a=1))
                load(l_gb[:, l, 1:2], ins["L0_ffn_ln_b"][l].rearrange("(c a) -> c a", a=1))
                for i, n in enumerate(("q", "k")):
                    v = ins[f"L0_ffn_{n}_scale"][l]
                    load(l_scale[:, l, 0, i, :], row(v))
                    load(l_scale[:, l, 1, i, 0:LD // 2], row(v[LD // 2:LD]))
                    load(l_scale[:, l, 1, i, LD // 2:LD], row(v[0:LD // 2]))
            load(lw_1[:, :, :], ins["L0_ffn_w1"].rearrange("l c n -> c l n"))
            for t, n in ((ln1, "ln1"), (ln2, "ln2")):
                load(t[:, 0:1], ins[f"L1_ffn_{n}_w"].rearrange("(c a) -> c a", a=1))
                load(t[:, 1:2], ins[f"L1_ffn_{n}_b"].rearrange("(c a) -> c a", a=1))
            load(conv[:, :], ins["L1_ffn_conv_w"].rearrange("c a k -> c (a k)"))
            load(router[:, :], ins["L1_ffn_router_w"])
            load(e_wv[:, :, :], ins["L1_ffn_expert_wv"].rearrange("e c n -> c e n"))
            for e in range(NE):
                load(e_pr[:, e], ins["L1_ffn_expert_proj"][e].rearrange("(k c) n -> c k n", c=P))
            sp.dma_start(xin[:, :, :], ins["L0_attn_x"][0].rearrange("(t p) c -> p t c", p=P)).then_inc(x_in.sem, 16)
            with sp.Fori(0, B - 1) as b:
                sp.wait_ge(xin_used.sem, xin_used.at(b, 1))
                sp.dma_start(xin[:, :, :], ins["L0_attn_x"][bass.ds(b + 1, 1)].rearrange("o (t p) c -> p (o t) c", p=P)).then_inc(x_in.sem, 16)
                sp.wait_ge(y_final.sem, y_final.at(b, 1))
                sp.dma_start(out[bass.ds(b, 1)].rearrange("o (t p) c -> p (o t) c", p=P), yo[:, :, :]).then_inc(x_out.sem, 16)
            sp.wait_ge(y_final.sem, B)
            sp.dma_start(out[B - 1].rearrange("(t p) c -> p t c", p=P), yo[:, :, :]).then_inc(x_out.sem, 16)
            sp.wait_ge(x_out.sem, 16 * (B + 1))

        LOADS = 16 * n_loads[0]

        @block.tensor
        def _(pe):
            pe.wait_ge(loaded, LOADS)
            pe.wait_ge(consts_ready, 3)

            def transpose4(src, dst):
                for t in range(NT):
                    last = nc.tensor.transpose(dst[:, t * P:(t + 1) * P], src[:, t, :], ident[:, :])
                return last

            def attention(b, s):
                if s == "D":
                    srcT = cT[:, 1, :]
                else:
                    if s == "A":
                        pe.wait_ge(x_in.sem, x_in.at(b, 16))
                    else:
                        pe.wait_ge(S["Bres"].sem, S["Bres"].at(b, 1))
                    transpose4(SRC[s], bank(0)).then_inc(S[s + "xT_ps"].sem, 1)
                    srcT = xT
                w = S[s + "xT"]
                pe.wait_ge(w.sem, w.at(b, 1))
                for t in range(NT):
                    nc.tensor.matmul(ps[:, 1 + t, 0:3 * C], srcT[:, t * P:(t + 1) * P], wqkv[s][:, :],
                                     start=True, stop=True).then_inc(S[s + "qkv_ps"].sem, 1)
                pe.wait_ge(S[s + "stacked"].sem, S[s + "stacked"].at(b, 1))
                pe.wait_ge(S[s + "dup"].sem, S[s + "dup"].at(b, 1))
                for n in range(8):
                    g, which = n // 2, 1 - n % 2
                    for t in range(NT):
                        last = nc.tensor.transpose(ps[:, n, t * P:(t + 1) * P],
                                                   stack_f[:, t, which, g * HG:(g + 1) * HG, :].rearrange("p h s -> p (h s)"),
                                                   ident[:, :])
                    last.then_inc(S[s + "kq_ps"].sem, 1)

                def shifted(g):
                    pe.wait_ge(S[s + "mx"].sem, S[s + "mx"].at(b, (g + 1) * HG * NT))
                    if g >= 1:
                        pe.wait_ge(S[s + "qm"].sem, S[s + "qm"].at(b, g))
                    for t in range(NT):
                        last = nc.tensor.transpose(ps[:, 5, t * P:(t + 1) * P],
                                                   stack_f[:, t, 0, g * HG:(g + 1) * HG, :].rearrange("p h s -> p (h s)"),
                                                   ident[:, :])
                    last.then_inc(S[s + "qm_ps"].sem, 1)

                def keys_first(h):
                    g, r = h // HG, h % HG * SLOT
                    if h % HG == 0:
                        pe.wait_ge(S[s + "qm"].sem, S[s + "qm"].at(b, g + 1))
                    for i in range(NT):
                        n = h * NT + i
                        if n >= 3:
                            pe.wait_ge(S[s + "ex"].sem, S[s + "ex"].at(b, n - 2))
                        q0 = first(s, i)
                        m = nc.tensor.matmul(ps[:, 2 + n % 3, 0:L - q0], KT[r:r + SLOT, g, i * P:(i + 1) * P],
                                             QM[r:r + SLOT, g, q0:L], start=True, stop=True)
                        if CAUSAL[s]:
                            m = nc.tensor.matmul(ps[:, 2 + n % 3, 0:P], ident_h[:, :], causal_kq,
                                                 start=False, stop=True, skip_group_check=True)
                        m.then_inc(S[s + "st_ps"].sem, 1)

                def weigh(h):
                    pe.wait_ge(S[s + "ex"].sem, S[s + "ex"].at(b, (h + 1) * NT))
                    for i in range(NT):
                        js = range(i + 1) if CAUSAL[s] else range(NT)
                        for j in js:
                            o = (i % 2) * H * (HD + 1) + h * (HD + 1)
                            m = nc.tensor.matmul(ps[:, 6 + i // 2, o:o + HD + 1], prob[:, h % 2, j, i * P:(i + 1) * P],
                                                 vaug[:, j, h, :], start=(j == 0), stop=(j == js[-1]))
                    m.then_inc(S[s + "pv"].sem, 1)

                pe.wait_ge(S[s + "kq"].sem, S[s + "kq"].at(b, 8))
                for h in range(HG):
                    scores(b, s, h)
                for g in range(NG):
                    shifted(g)
                    for k in range(HG):
                        h = g * HG + k
                        keys_first(h)
                        if g + 1 < NG:
                            scores(b, s, h + HG)
                        if h >= 1:
                            weigh(h - 1)
                weigh(H - 1)
                pe.wait_ge(S[s + "ctx"].sem, S[s + "ctx"].at(b, 1))
                transpose4(heads, bank(0)).then_inc(S[s + "cT_ps"].sem, 1)
                pe.wait_ge(S[s + "cT"].sem, S[s + "cT"].at(b, 1))
                for t in range(NT):
                    last = nc.tensor.matmul(ps[:, 1, t * P:(t + 1) * P], headsT[:, t * P:(t + 1) * P], wout[s][:, :],
                                            start=True, stop=True)
                last.then_inc(S[s + "o_ps"].sem, 1)

            def scores(b, s, h):
                g, r = h // HG, h % HG * SLOT
                for i in range(NT):
                    n = h * NT + i
                    if n >= 2:
                        pe.wait_ge(S[s + "mx"].sem, S[s + "mx"].at(b, n - 1))
                    N = (i + 1) * P if CAUSAL[s] else L
                    m = nc.tensor.matmul(ps[:, n % 2, 0:N], QT[r:r + MSLOT, g, i * P:(i + 1) * P],
                                         KT[r:r + MSLOT, g, 0:N], start=True, stop=True)
                    if CAUSAL[s]:
                        m = nc.tensor.matmul(ps[:, n % 2, i * P:(i + 1) * P], ident_h[:, :], causal_qk,
                                             start=False, stop=True, skip_group_check=True)
                    m.then_inc(S[s + "sc_ps"].sem, 1)

            def local_layer(b, l):
                s = str(l)
                if l == 0:
                    pe.wait_ge(S["Ares"].sem, S["Ares"].at(b, 1))
                    src = xa
                else:
                    pe.wait_ge(S["0lx"].sem, S["0lx"].at(b, 1))
                    src = l_x[:, 0]
                transpose4(src, bank(0)).then_inc(S[s + "xT_ps"].sem, 1)
                pe.wait_ge(S[s + "xT"].sem, S[s + "xT"].at(b, 1))
                for t in range(NT):
                    if t >= 2:
                        pe.wait_ge(S[s + "roped"].sem, S[s + "roped"].at(b, t - 1))
                        pe.wait_ge(S[s + "v"].sem, S[s + "v"].at(b, t - 1))
                        pe.wait_ge(S[s + "sq"].sem, S[s + "sq"].at(b, t - 1))
                    for n in range(3):
                        m = nc.tensor.matmul(ps[:, 1 + t % 2 * 3 + n, :], xsT[:, t * P:(t + 1) * P],
                                             lw_qkv[:, l, n * 512:(n + 1) * 512], start=True, stop=True)
                    m.then_inc(S[s + "qkv_ps"].sem, 1)
                for n in range(8):
                    if n == 0:
                        pe.wait_ge(S[s + "nrm"].sem, S[s + "nrm"].at(b, NT))
                        pe.wait_ge(S[s + "v"].sem, S[s + "v"].at(b, NT))
                    for t in range(NT):
                        m = nc.tensor.transpose(ps[:, n, t * P:(t + 1) * P],
                                                l_c[:, t, 2 * n:2 * n + 2, :].rearrange("p h d -> p (h d)"), ident[:, :])
                    m.then_inc(S[s + "T_ps"].sem, 1)
                pe.wait_ge(S[s + "T"].sem, S[s + "T"].at(b, 8))
                for h in range(LH):
                    r, k = h % 2 * LD, h // 2
                    if h >= 2:
                        pe.wait_ge(S[s + "mx"].sem, S[s + "mx"].at(b, h - 1))
                    for t in range(NT):
                        o = ps[:, h % 2 * 2 + t // 2, t % 2 * BAND:(t % 2 + 1) * BAND]
                        k0 = max(t * P - WIN, 0)
                        N = (t + 1) * P - k0
                        nc.tensor.matmul(o, ident_h[:, :], band_qk if t else band_q0, start=True, stop=True)
                        m = nc.tensor.matmul(o[:, BAND - N:BAND], l_T[r:r + LD, k, t * P:(t + 1) * P],
                                             l_T[r:r + LD, 4 + k, k0:(t + 1) * P], start=False, stop=True,
                                             skip_group_check=True)
                    m.then_inc(S[s + "sc_ps"].sem, 1)
                pe.wait_ge(S[s + "mx"].sem, S[s + "mx"].at(b, LH))
                for t in range(NT):
                    m = nc.tensor.transpose(ps[0:LH, 0, t * P:(t + 1) * P], nm[:, t, :], ident[:, :])
                m.then_inc(S[s + "nm_ps"].sem, 1)
                pe.wait_ge(S[s + "nmT"].sem, S[s + "nmT"].at(b, 1))

                def weigh(h):
                    pe.wait_ge(S[s + "ex"].sem, S[s + "ex"].at(b, h + 1))
                    if h >= 2:
                        pe.wait_ge(S[s + "o"].sem, S[s + "o"].at(b, h - 1))
                    for t in range(NT):
                        o = ps[:, 4 + h % 2, t * (LD + 1):(t + 1) * (LD + 1)]
                        m = nc.tensor.matmul(o, l_p[:, h % 2, t, 0:P], l_v[:, t, h, :], start=True, stop=True)
                        if t:
                            m = nc.tensor.matmul(o[0:WIN], l_p[:, h % 2, t - 1, P:BAND], l_v[:, t - 1, h, :],
                                                 start=False, stop=True, skip_group_check=True)
                    m.then_inc(S[s + "pv"].sem, 1)

                for h in range(LH):
                    r, k = h % 2 * LD, h // 2
                    if h >= 2:
                        pe.wait_ge(S[s + "ex"].sem, S[s + "ex"].at(b, h - 1))
                    for t in range(NT):
                        q1 = min(t * P + BAND, L)
                        N = q1 - t * P
                        o = ps[:, h % 2 * 2 + t // 2, t % 2 * BAND:t % 2 * BAND + N]
                        nc.tensor.matmul(o, ident_h[:, :], band_kq[:, 0:N], start=True, stop=False)
                        nc.tensor.matmul(o, sel[:, h * P:(h + 1) * P], nmT[:, t * P:q1], start=False, stop=False)
                        m = nc.tensor.matmul(o, l_T[r:r + LD, 4 + k, t * P:(t + 1) * P], l_T[r:r + LD, k, t * P:q1],
                                             start=False, stop=True)
                    m.then_inc(S[s + "st_ps"].sem, 1)
                    if h >= 1:
                        weigh(h - 1)
                weigh(LH - 1)
                pe.wait_ge(S[s + "o"].sem, S[s + "o"].at(b, LH))
                for k in range(4):
                    for t in range(NT):
                        m = nc.tensor.transpose(ps[:, k, t * P:(t + 1) * P], l_o[:, t, k * P:(k + 1) * P], ident[:, :])
                    m.then_inc(S[s + "oT_ps"].sem, 1)
                pe.wait_ge(S[s + "oT"].sem, S[s + "oT"].at(b, 4))
                for t in range(NT):
                    for k in range(4):
                        m = nc.tensor.matmul(ps[:, 4, t * P:(t + 1) * P], l_oT[:, k, t * P:(t + 1) * P], lw_o[:, l, k, :],
                                             start=(k == 0), stop=(k == 3))
                m.then_inc(S[s + "o_ps"].sem, 1)
                pe.wait_ge(S[s + "lm"].sem, S[s + "lm"].at(b, 1))
                for t in range(NT):
                    o = ps[:, 5, t * 64:(t + 1) * 64]
                    m = nc.tensor.matmul(o, shift[:, 0, :], l_m[:, t, 64:128], start=True, stop=(t == 0))
                    if t:
                        m = nc.tensor.matmul(o, shift[:, 1, :], l_m[:, t - 1, 64:128], start=False, stop=True)
                m.then_inc(S[s + "sh_ps"].sem, 1)
                pe.wait_ge(S[s + "hn"].sem, S[s + "hn"].at(b, 1))
                transpose4(hn, bank(6)).then_inc(S[s + "hT_ps"].sem, 1)
                pe.wait_ge(S[s + "hT"].sem, S[s + "hT"].at(b, 1))
                for j in range(3):
                    for half in range(2):
                        c0 = half * HID + j * P
                        m = nc.tensor.matmul(ps[0:HB[j], 2 * j + half, :], lw_1[:, l, c0:c0 + HB[j]], hT[:, 2:L + 2],
                                             start=True, stop=True)
                    m.then_inc(S[s + "g_ps"].sem, 1)
                pe.wait_ge(S[s + "hid"].sem, S[s + "hid"].at(b, 3))
                for t in range(NT):
                    for j in range(3):
                        m = nc.tensor.matmul(ps[:, 7, t * P:(t + 1) * P], hidT[0:HB[j], j, t * P:(t + 1) * P],
                                             lw_2[0:HB[j], l, j, :], start=(j == 0), stop=(j == 2))
                m.then_inc(S[s + "f_ps"].sem, 1)

            def experts(b):
                pe.wait_ge(S["Mhn"].sem, S["Mhn"].at(b, 1))
                transpose4(hn, bank(0)).then_inc(S["MhT_ps"].sem, 1)
                pe.wait_ge(S["MhT"].sem, S["MhT"].at(b, 1))
                for t in range(NT):
                    m = nc.tensor.matmul(ps[:, 1, t * NE:(t + 1) * NE], hT[:, 2 + t * P:2 + (t + 1) * P], router[:, :],
                                         start=True, stop=True)
                m.then_inc(S["Mlg_ps"].sem, 1)

                def project(e):
                    pe.wait_ge(S["Mact"].sem, S["Mact"].at(b, 4 * e + 4))
                    if e >= 2:
                        pe.wait_ge(S["Macc"].sem, S["Macc"].at(b, e - 1))
                    for t in range(NT):
                        for j in range(4):
                            m = nc.tensor.matmul(ps[:, 6 + e % 2, t * P:(t + 1) * P],
                                                 eact[:, e % 2, j, t * P:(t + 1) * P], e_pr[:, e, j, :],
                                                 start=(j == 0), stop=(j == 3))
                    m.then_inc(S["Me_ps"].sem, 1)

                for e in range(NE):
                    for j in range(4):
                        n = e * 4 + j
                        if n >= 2:
                            pe.wait_ge(S["Mact"].sem, S["Mact"].at(b, n - 1))
                        nc.tensor.matmul(ps[:, 2 + n % 2 * 2, :], e_wv[:, e, j * P:(j + 1) * P], hT[:, 2:L + 2],
                                         start=True, stop=True)
                        nc.tensor.matmul(ps[:, 3 + n % 2 * 2, :], e_wv[:, e, FF + j * P:FF + (j + 1) * P],
                                         hT[:, 2:L + 2], start=True, stop=True).then_inc(S["Mg_ps"].sem, 1)
                        if e >= 1 and j == 1:
                            project(e - 1)
                project(NE - 1)

            with pe.Fori(0, B) as b:
                attention(b, "A")
                local_layer(b, 0)
                local_layer(b, 1)
                attention(b, "C")
                pe.wait_ge(S["Nhn"].sem, S["Nhn"].at(b, 1))
                transpose4(hn, bank(0)).then_inc(S["NhT_ps"].sem, 1)
                attention(b, "D")
                experts(b)

        @block.scalar
        def _(act):
            act.wait_ge(loaded, LOADS)

            def copy(dst, src):
                return nc.scalar.activation(dst, src, ACT.Copy)

            def attention(b, s):
                if s != "D":
                    act.wait_ge(S[s + "xT_ps"].sem, S[s + "xT_ps"].at(b, 1))
                    copy(xT[:, :], bank(0)).then_inc(S[s + "xT"].sem, 1)
                act.wait_ge(S[s + "stacked"].sem, S[s + "stacked"].at(b, 1))
                copy(stack[:, :, 0, :, 2 * HD:3 * HD], stack_f[:, :, 0, :, 0:HD])
                copy(stack[:, :, 1, :, HD:2 * HD], stack_f[:, :, 1, :, 0:HD]).then_inc(S[s + "dup"].sem, 1)
                for n in range(8):
                    act.wait_ge(S[s + "kq_ps"].sem, S[s + "kq_ps"].at(b, n + 1))
                    dst = (KT if n % 2 == 0 else QT)
                    copy(dst[:, n // 2, :], bank(n)).then_inc(S[s + "kq"].sem, 1)

                def queries(g):
                    act.wait_ge(S[s + "qm_ps"].sem, S[s + "qm_ps"].at(b, g + 1))
                    copy(QM[:, g, :], bank(5)).then_inc(S[s + "qm"].sem, 1)

                queries(0)
                for h in range(H):
                    for i in range(NT):
                        n = h * NT + i
                        act.wait_ge(S[s + "st_ps"].sem, S[s + "st_ps"].at(b, n + 1))
                        if i == 0 and h >= 2:
                            act.wait_ge(S[s + "pv"].sem, S[s + "pv"].at(b, h - 1))
                        q0 = first(s, i)
                        nc.scalar.activation(prob[:, h % 2, i, q0:L], ps[:, 2 + n % 3, 0:L - q0], ACT.Exp,
                                             scale=SCALE).then_inc(S[s + "ex"].sem, 1)
                    if h % HG == HG - 1 and h + 1 < H:
                        queries(h // HG + 1)
                act.wait_ge(S[s + "cT_ps"].sem, S[s + "cT_ps"].at(b, 1))
                copy(headsT[:, :], bank(0)).then_inc(S[s + "cT"].sem, 1)

            def local_layer(b, l):
                s = str(l)
                act.wait_ge(S[s + "xT_ps"].sem, S[s + "xT_ps"].at(b, 1))
                copy(xsT[0:64, :], ps[0:64, 0, :])
                copy(xsT[64:128, 1:L], ps[64:128, 0, 0:L - 1]).then_inc(S[s + "xT"].sem, 1)
                for t in range(NT):
                    act.wait_ge(S[s + "qkv_ps"].sem, S[s + "qkv_ps"].at(b, t + 1))
                    k = 1 + t % 2 * 3
                    if t >= 2:
                        act.wait_ge(S[s + "roped"].sem, S[s + "roped"].at(b, t - 1))
                    nc.scalar.activation(sq[:, t % 2, :], ps[:, k:k + 2, :].rearrange("p a n -> p (a n)"),
                                         ACT.Square).then_inc(S[s + "sq"].sem, 1)
                    copy(l_v[:, t, :, 0:LD], ps[:, k + 2, :].rearrange("p (h d) -> p h d", d=LD)).then_inc(S[s + "v"].sem, 1)
                for n in range(8):
                    act.wait_ge(S[s + "T_ps"].sem, S[s + "T_ps"].at(b, n + 1))
                    copy(l_T[:, n, :], bank(n)).then_inc(S[s + "T"].sem, 1)
                act.wait_ge(S[s + "nm_ps"].sem, S[s + "nm_ps"].at(b, 1))
                copy(nmT[:, :], ps[0:LH, 0, :]).then_inc(S[s + "nmT"].sem, 1)
                for h in range(LH):
                    act.wait_ge(S[s + "st_ps"].sem, S[s + "st_ps"].at(b, h + 1))
                    if h >= 2:
                        act.wait_ge(S[s + "pv"].sem, S[s + "pv"].at(b, h - 1))
                    pr = l_p[:, h % 2, :, :].rearrange("p t n -> p (t n)")
                    nc.scalar.activation(pr[:, 0:2 * BAND], ps[:, h % 2 * 2, 0:2 * BAND], ACT.Exp, scale=LSCALE)
                    nc.scalar.activation(pr[:, 2 * BAND:3 * BAND + P], ps[:, h % 2 * 2 + 1, 0:BAND + P], ACT.Exp,
                                         scale=LSCALE).then_inc(S[s + "ex"].sem, 1)
                for k in range(4):
                    act.wait_ge(S[s + "oT_ps"].sem, S[s + "oT_ps"].at(b, k + 1))
                    copy(l_oT[:, k, :], bank(k)).then_inc(S[s + "oT"].sem, 1)
                for j in range(3):
                    act.wait_ge(S[s + "g_ps"].sem, S[s + "g_ps"].at(b, j + 1))
                    n = HB[j]
                    nc.scalar.activation(gel[0:n, j, :], ps[0:n, 2 * j + 1, :], ACT.Gelu,
                                         bias=lb_1[0:n, l, 1, j:j + 1]).then_inc(S[s + "gel"].sem, 1)

            with act.Fori(0, B) as b:
                attention(b, "A")
                local_layer(b, 0)
                local_layer(b, 1)
                attention(b, "C")
                attention(b, "D")
                for n in range(16):
                    act.wait_ge(S["Mg_ps"].sem, S["Mg_ps"].at(b, n + 1))
                    if n >= 2:
                        act.wait_ge(S["Mact"].sem, S["Mact"].at(b, n - 1))
                    nc.scalar.activation(sil[:, n % 2, :], ps[:, 2 + n % 2 * 2, :], ACT.Silu).then_inc(S["Msil"].sem, 1)

        @block.gpsimd
        def _(pool):
            nc.gpsimd.memset(m_half[:, :], -0.5).then_inc(x_out.sem, 16)
            nc.gpsimd.memset(xsT[:, 0:1], 0.0)
            nc.gpsimd.memset(hT[:, 0:2], 0.0)
            nc.gpsimd.memset(stack_f[:, :, :, :, MSLOT:SLOT].rearrange("p t w h s -> p (t w h) s"), 0.0).then_inc(pstep.sem, 1)
            nc.gpsimd.memset(vaug[:, :, :, HD:HD + 1].rearrange("p t h s -> p (t h) s"), 1.0)
            nc.gpsimd.memset(l_v[:, :, :, LD:LD + 1].rearrange("p t h s -> p (t h) s"), 1.0)
            pool.wait_ge(pstep.sem, 1)
            nc.gpsimd.memset(stack_f[:, :, 1, :, MSLOT:MSLOT + 1], 1.0).then_inc(consts_ready, 1)
            pool.wait_ge(consts_ready, 3)

            with pool.Fori(0, B) as b:
                def norm_root(s):
                    pool.wait_ge(S[s + "var"].sem, S[s + "var"].at(b, 1))
                    nc.gpsimd.tensor_tensor(rstd[:, :], mv[:, :, 1], m_half[:, 0:NT], ALU.pow).then_inc(S[s + "rstd"].sem, 1)

                def local_root(s):
                    pool.wait_ge(S[s + "ssum"].sem, S[s + "ssum"].at(b, 1))
                    nc.gpsimd.tensor_tensor(rn[:, :, :].rearrange("p t h -> p (t h)"), ssum[:, :, :].rearrange("p t h -> p (t h)"),
                                            m_half[:, :], ALU.pow).then_inc(S[s + "rn"].sem, 1)

                norm_root("A")
                local_root("0")
                norm_root("0")
                local_root("1")
                norm_root("1")
                norm_root("B")
                norm_root("C")
                norm_root("N")
                norm_root("M")
                norm_root("F")

        STEPS = DVE_STEPS

        @block.vector
        def _(dve):
            dve.wait_ge(loaded, LOADS)
            nc.vector.tensor_copy(ident_h[:, :], ident[:, :])
            nc.vector.tensor_copy(mask_h[:, :], mask_f[:, :])
            for l in range(2):
                for cs in range(2):
                    for w in range(2):
                        nc.vector.tensor_tensor(tab[:, l, :, cs, w, :], xpos[:, :, cs, w, :],
                                                l_scale[:, l, cs, w, :].rearrange("p (a d) -> p a d", a=1).broadcast_to([P, NT, LD]),
                                                ALU.mult)
            nc.vector.tensor_copy(sel[:, :], sel_f[:, :]).then_inc(consts_ready, 2)
            dve.wait_ge(consts_ready, 3)

            with dve.Fori(0, B) as b:
                steps = [0]

                def settle(ins):
                    steps[0] += 1
                    ins.then_inc(dstep.sem, 1)
                    dve.wait_ge(dstep.sem, b * STEPS + steps[0])

                def statistics(src, s, upper=None):
                    for t in range(NT):
                        if upper is None:
                            last = nc.vector.bn_stats(stats[:, t, 0, :], src[:, t, :])
                        else:
                            nc.vector.bn_stats(stats[:, t, 0, :], src[:, t, 0:64])
                            last = nc.vector.bn_stats(stats[:, t, 1, :], upper[:, t * 64:(t + 1) * 64])
                    settle(last)
                    nc.vector.tensor_copy(held[:, :], ident[:, 0:1])
                    for t in range(NT):
                        w = stats[:, t, 0, :] if upper is None else stats[:, t, :, :].rearrange("p a n -> p (a n)")
                        last = nc.vector.bn_aggr(mv[:, t, :], w)
                    settle(last)
                    nc.vector.tensor_scalar(mv[:, :, 1], mv[:, :, 1], EPS, None, ALU.add).then_inc(S[s + "var"].sem, 1)
                    dve.wait_ge(S[s + "rstd"].sem, S[s + "rstd"].at(b, 1))

                def normalise(dst, src):
                    for t in range(NT):
                        last = nc.vector.tensor_scalar(dst[:, t, :], src[:, t, :], mv[:, t, 0:1], rstd[:, t:t + 1],
                                                       ALU.subtract, ALU.mult)
                    return last

                def four(i):
                    return ps[:, i, :].rearrange("p (t c) -> p t c", t=NT)

                def attention(s):
                    for t in range(NT):
                        dve.wait_ge(S[s + "qkv_ps"].sem, S[s + "qkv_ps"].at(b, t + 1))
                        o = qk[:, t, :, :].rearrange("p h d -> p (h d)")
                        v = ps[:, 1 + t, 2 * C:3 * C].rearrange("p (h d) -> p h d", d=HD)
                        if s == "A":
                            nc.vector.tensor_tensor(o, ps[:, 1 + t, 0:2 * C], bqkv[:, 0:2 * C], ALU.add)
                            last = nc.vector.tensor_tensor(vaug[:, t, :, 0:HD], v,
                                                           bqkv[:, 2 * C:3 * C].rearrange("p (h d) -> p h d", d=HD), ALU.add)
                        else:
                            nc.vector.tensor_copy(o, ps[:, 1 + t, 0:2 * C])
                            last = nc.vector.tensor_copy(vaug[:, t, :, 0:HD], v)
                    settle(last)
                    src = qk
                    if s in rope:
                        c = rope[s][:, :, 0:1, :].broadcast_to([P, NT, 2 * H, HD])
                        n = rope[s][:, :, 1:2, :].broadcast_to([P, NT, 2 * H, HD])
                        hf = HD // 2
                        nc.vector.tensor_tensor(qk_c[:, :, :, :], qk[:, :, :, :], c, ALU.mult)
                        nc.vector.tensor_tensor(qk_s[:, :, :, 0:hf], qk[:, :, :, hf:HD], n[:, :, :, 0:hf], ALU.mult)
                        settle(nc.vector.tensor_tensor(qk_s[:, :, :, hf:HD], qk[:, :, :, 0:hf], n[:, :, :, hf:HD], ALU.mult))
                        settle(nc.vector.tensor_tensor(qk_c[:, :, :, :], qk_c[:, :, :, :], qk_s[:, :, :, :], ALU.add))
                        src = qk_c
                    sv = stack[:, :, :, :, :].rearrange("p t w h s -> p (t w h) s")
                    settle(nc.vector.tensor_copy(sv[:, :, 0:HD], src[:, :, :, :].rearrange("p t h d -> p (t h) d")))
                    nc.vector.tensor_tensor(stack[:, :, 0, :, HD:2 * HD], src[:, :, 0:H, :], stack_f[:, :, 0, :, 0:HD], ALU.subtract)
                    nc.vector.tensor_tensor(stack[:, :, 1, :, 2 * HD:3 * HD], src[:, :, H:2 * H, :], stack_f[:, :, 1, :, 0:HD],
                                            ALU.subtract).then_inc(S[s + "stacked"].sem, 1)
                    for h in range(H):
                        for i in range(NT):
                            n = h * NT + i
                            dve.wait_ge(S[s + "sc_ps"].sem, S[s + "sc_ps"].at(b, n + 1))
                            N = (i + 1) * P if CAUSAL[s] else L
                            nc.vector.tensor_reduce(stack[:, i, 0, h, MSLOT:MSLOT + 1], ps[:, n % 2, 0:N], X, ALU.max,
                                                    negate=True).then_inc(S[s + "mx"].sem, 1)
                    dve.wait_ge(S[s + "pv"].sem, S[s + "pv"].at(b, H))
                    o = ps[:, 6:8, 0:2 * H * (HD + 1)].rearrange("p a (n e) -> p a n e", e=HD + 1)
                    rd = rden[:, :, :].rearrange("p (a c) h -> p a (c h)", a=2)
                    settle(nc.vector.reciprocal(rd, o[:, :, :, HD:HD + 1].rearrange("p a n e -> p a (n e)")))
                    nc.vector.tensor_tensor(heads[:, :, :].rearrange("p (a c) (h d) -> p a (c h) d", a=2, d=HD),
                                            o[:, :, :, 0:HD],
                                            rd.rearrange("p a (n e) -> p a n e", e=1).broadcast_to([P, 2, 2 * H, HD]),
                                            ALU.mult).then_inc(S[s + "ctx"].sem, 1)
                    dve.wait_ge(S[s + "o_ps"].sem, S[s + "o_ps"].at(b, 1))

                def local_layer(l):
                    s = str(l)
                    hf = LD // 2
                    for t in range(NT):
                        dve.wait_ge(S[s + "qkv_ps"].sem, S[s + "qkv_ps"].at(b, t + 1))
                        dve.wait_ge(S[s + "sq"].sem, S[s + "sq"].at(b, t + 1))
                        k = 1 + t % 2 * 3
                        z = ps[:, k:k + 2, :].rearrange("p w (h d) -> p w h d", d=LD)
                        cs = l_c[:, t, :, :].rearrange("p (w h) d -> p w h d", w=2)
                        sn = l_s[:, t % 2, :, :].rearrange("p (w h) d -> p w h d", w=2)
                        c = tab[:, l, t, 0, :, :].rearrange("p w (a d) -> p w a d", a=1).broadcast_to([P, 2, LH, LD])
                        n = tab[:, l, t, 1, :, :].rearrange("p w (a d) -> p w a d", a=1).broadcast_to([P, 2, LH, LD])
                        nc.vector.tensor_tensor(cs, z, c, ALU.mult)
                        nc.vector.tensor_tensor(sn[:, :, :, 0:hf], z[:, :, :, hf:LD], n[:, :, :, 0:hf], ALU.mult)
                        settle(nc.vector.tensor_tensor(sn[:, :, :, hf:LD], z[:, :, :, 0:hf], n[:, :, :, hf:LD], ALU.mult))
                        nc.vector.tensor_tensor(l_c[:, t, :, :], l_c[:, t, :, :], l_s[:, t % 2, :, :], ALU.add)
                        nc.vector.tensor_reduce(ssum[:, t, :], sq[:, t % 2, :].rearrange("p (h d) -> p h d", d=LD), X,
                                                ALU.add).then_inc(S[s + "roped"].sem, 1)
                    dve.wait_ge(S[s + "roped"].sem, S[s + "roped"].at(b, NT))
                    nc.vector.tensor_scalar(ssum[:, :, :], ssum[:, :, :], 1e-24, None, ALU.max).then_inc(S[s + "ssum"].sem, 1)
                    dve.wait_ge(S[s + "rn"].sem, S[s + "rn"].at(b, 1))
                    for t in range(NT):
                        nc.vector.tensor_tensor(l_c[:, t, :, :], l_c[:, t, :, :],
                                                rn[:, t, :].rearrange("p (h a) -> p h a", a=1).broadcast_to([P, 2 * LH, LD]),
                                                ALU.mult).then_inc(S[s + "nrm"].sem, 1)
                    for h in range(LH):
                        dve.wait_ge(S[s + "sc_ps"].sem, S[s + "sc_ps"].at(b, h + 1))
                        k = h % 2 * 2
                        nc.vector.tensor_reduce(nm[:, :, h].rearrange("p (a c) -> p a c", a=2),
                                                ps[:, k:k + 2, 0:2 * BAND].rearrange("p a (c n) -> p a c n", c=2), X, ALU.max,
                                                negate=True).then_inc(S[s + "mx"].sem, 1)
                    for h in range(LH):
                        dve.wait_ge(S[s + "pv"].sem, S[s + "pv"].at(b, h + 1))
                        o = ps[:, 4 + h % 2, 0:NT * (LD + 1)].rearrange("p (t e) -> p t e", t=NT)
                        settle(nc.vector.reciprocal(l_rd[:, h % 2, :].rearrange("p (t a) -> p t a", a=1), o[:, :, LD:LD + 1]))
                        nc.vector.tensor_tensor(l_o[:, :, h * LD:(h + 1) * LD], o[:, :, 0:LD],
                                                l_rd[:, h % 2, :].rearrange("p (t a) -> p t a", a=1).broadcast_to([P, NT, LD]),
                                                ALU.mult).then_inc(S[s + "o"].sem, 1)
                    src = xa if l == 0 else l_x[:, 0]
                    dve.wait_ge(S[s + "o_ps"].sem, S[s + "o_ps"].at(b, 1))
                    nc.vector.tensor_tensor(l_m[:, :, :], four(4), src[:, :, :], ALU.add).then_inc(S[s + "lm"].sem, 1)
                    dve.wait_ge(S[s + "sh_ps"].sem, S[s + "sh_ps"].at(b, 1))
                    statistics(l_m, s, upper=ps[:, 5, :])
                    for t in range(NT):
                        nc.vector.tensor_scalar(hn[:, t, 0:64], l_m[:, t, 0:64], mv[:, t, 0:1], rstd[:, t:t + 1],
                                                ALU.subtract, ALU.mult)
                        last = nc.vector.tensor_scalar(hn[:, t, 64:128], ps[:, 5, t * 64:(t + 1) * 64], mv[:, t, 0:1],
                                                       rstd[:, t:t + 1], ALU.subtract, ALU.mult)
                    last.then_inc(S[s + "hn"].sem, 1)
                    nc.vector.tensor_tensor(y[:, :, :], l_m[:, :, :],
                                            lb_2[:, l, :].rearrange("p (a c) -> p a c", a=1).broadcast_to([P, NT, C]), ALU.add)
                    dve.wait_ge(S[s + "hT_ps"].sem, S[s + "hT_ps"].at(b, 1))
                    nc.vector.tensor_scalar(hT[:, 2:L + 2], bank(6), l_gb[:, l, 0:1], l_gb[:, l, 1:2], ALU.mult,
                                            ALU.add).then_inc(S[s + "hT"].sem, 1)
                    for j in range(3):
                        n = HB[j]
                        dve.wait_ge(S[s + "gel"].sem, S[s + "gel"].at(b, j + 1))
                        nc.vector.scalar_tensor_tensor(hidT[0:n, j, :], ps[0:n, 2 * j, :], lb_1[0:n, l, 0, j:j + 1],
                                                       gel[0:n, j, :], ALU.add, ALU.mult).then_inc(S[s + "hid"].sem, 1)
                    dve.wait_ge(S[s + "f_ps"].sem, S[s + "f_ps"].at(b, 1))
                    nc.vector.tensor_tensor(l_x[:, l], four(7), y[:, :, :], ALU.add).then_inc(S[s + "lx"].sem, 1)
                    dve.wait_ge(S[s + "lx"].sem, S[s + "lx"].at(b, 1))

                def bc(v):
                    return v.rearrange("p (a c) -> p a c", a=1).broadcast_to([P, NT, C])

                attention("A")
                nc.vector.tensor_tensor(y[:, :, :], xin[:, :, :], bc(bout[:, :]), ALU.add).then_inc(xin_used.sem, 1)
                dve.wait_ge(xin_used.sem, xin_used.at(b, 1))
                settle(nc.vector.tensor_tensor(y[:, :, :], four(1), y[:, :, :], ALU.add))
                statistics(y, "A")
                normalise(xa, y).then_inc(S["Ares"].sem, 1)
                dve.wait_ge(S["Ares"].sem, S["Ares"].at(b, 1))
                local_layer(0)
                local_layer(1)
                settle(nc.vector.tensor_tensor(y[:, :, :], xa[:, :, :], l_x[:, 1], ALU.add))
                statistics(y, "B")
                normalise(xb, y).then_inc(S["Bres"].sem, 1)
                dve.wait_ge(S["Bres"].sem, S["Bres"].at(b, 1))
                attention("C")
                settle(nc.vector.scalar_tensor_tensor(y[:, :, :], xb[:, :, :], 2.0, four(1), ALU.mult, ALU.add))
                statistics(y, "C")
                normalise(xc, y).then_inc(S["Cres"].sem, 1)
                dve.wait_ge(S["Cres"].sem, S["Cres"].at(b, 1))
                statistics(xc, "N")
                normalise(hn, xc).then_inc(S["Nhn"].sem, 1)
                dve.wait_ge(S["NhT_ps"].sem, S["NhT_ps"].at(b, 1))
                settle(nc.vector.tensor_scalar(hT[:, 2:L + 2], bank(0), ln1[:, 0:1], ln1[:, 1:2], ALU.mult, ALU.add))
                settle(nc.vector.tensor_scalar(cT[:, 0, :], hT[:, 0:L], conv[:, 0:1], None, ALU.mult))
                settle(nc.vector.scalar_tensor_tensor(cT[:, 1, :], hT[:, 1:L + 1], conv[:, 1:2], cT[:, 0, :], ALU.mult, ALU.add))
                nc.vector.scalar_tensor_tensor(cT[:, 1, :], hT[:, 2:L + 2], conv[:, 2:3], cT[:, 1, :], ALU.mult,
                                               ALU.add).then_inc(S["DxT"].sem, 1)
                attention("D")
                settle(nc.vector.tensor_tensor(y[:, :, :], four(1), xc[:, :, :], ALU.add))
                statistics(y, "M")
                normalise(hn, y).then_inc(S["Mhn"].sem, 1)
                nc.vector.tensor_tensor(xb[:, :, :], xc[:, :, :], y[:, :, :], ALU.add)
                dve.wait_ge(S["MhT_ps"].sem, S["MhT_ps"].at(b, 1))
                nc.vector.tensor_scalar(hT[:, 2:L + 2], bank(0), ln2[:, 0:1], ln2[:, 1:2], ALU.mult, ALU.add).then_inc(S["MhT"].sem, 1)
                dve.wait_ge(S["Mlg_ps"].sem, S["Mlg_ps"].at(b, 1))
                settle(nc.vector.tensor_copy(lg[:, :, :], ps[:, 1, 0:NT * NE].rearrange("p (t e) -> p t e", e=NE)))
                settle(nc.vector.tensor_reduce(lmax[:, :], lg[:, :, :], X, ALU.max))
                for e in range(NE):
                    if e == 0:
                        settle(nc.vector.tensor_tensor(pick[:, :, 0], lg[:, :, 0], lmax[:, :], ALU.is_ge))
                        settle(nc.vector.tensor_scalar(free[:, :], pick[:, :, 0], -1.0, 1.0, ALU.mult, ALU.add))
                    else:
                        settle(nc.vector.tensor_tensor(pick[:, :, e], lg[:, :, e], lmax[:, :], ALU.is_ge))
                        settle(nc.vector.tensor_tensor(pick[:, :, e], pick[:, :, e], free[:, :], ALU.mult))
                        settle(nc.vector.tensor_tensor(free[:, :], free[:, :], pick[:, :, e], ALU.subtract))

                def gather(e):
                    dve.wait_ge(S["Me_ps"].sem, S["Me_ps"].at(b, e + 1))
                    if e >= 1:
                        dve.wait_ge(S["Macc"].sem, S["Macc"].at(b, e))
                    for t in range(NT):
                        last = nc.vector.scalar_tensor_tensor(moe[:, t, :], ps[:, 6 + e % 2, t * P:(t + 1) * P], pick[:, t, e:e + 1],
                                                              xb[:, t, :] if e == 0 else moe[:, t, :], ALU.mult, ALU.add)
                    last.then_inc(S["Macc"].sem, 1)

                for n in range(16):
                    e, j = n // 4, n % 4
                    dve.wait_ge(S["Msil"].sem, S["Msil"].at(b, n + 1))
                    if j == 0 and e >= 2:
                        dve.wait_ge(S["Me_ps"].sem, S["Me_ps"].at(b, e - 1))
                    nc.vector.tensor_tensor(eact[:, e % 2, j, :], ps[:, 3 + n % 2 * 2, :], sil[:, n % 2, :],
                                            ALU.mult).then_inc(S["Mact"].sem, 1)
                    if e >= 1 and j == 3:
                        gather(e - 1)
                gather(NE - 1)
                dve.wait_ge(S["Macc"].sem, S["Macc"].at(b, NE))
                statistics(moe, "F")
                dve.wait_ge(x_out.sem, x_out.at(b, 16))
                normalise(yo, moe).then_inc(y_final.sem, 1)
                assert steps[0] == STEPS, steps[0]


DVE_STEPS = 73


_OUTS = [((B, L, C), "float32")]


def constants():
    import numpy as np
    f = np.float32
    ar = np.arange
    i = ar(P)
    masks = np.zeros((P, 2 * P + 3 * BAND), f)
    masks[:, 0:P] = np.where(i[None, :] > i[:, None], NEG, 0)
    masks[:, P:2 * P] = np.where(i[:, None] > i[None, :], NEG, 0)
    k = ar(BAND)[None, :] - WIN
    q = i[:, None]
    ok = (k <= q) & (k >= q - WIN)
    masks[:, 2 * P:2 * P + BAND] = np.where(ok, 0, NEG)
    masks[:, 2 * P + BAND:2 * P + 2 * BAND] = np.where(ok & (k >= 0), 0, NEG)
    kk, qq = i[:, None], ar(BAND)[None, :]
    masks[:, 2 * P + 2 * BAND:] = np.where((qq >= kk) & (qq <= kk + WIN), 0, NEG)
    shift = np.zeros((P, 2, P), f)
    shift[i[:-1], 0, i[1:]] = 1
    shift[P - 1, 1, 0] = 1
    sel = np.zeros((LH, LH * P), f)
    for h in range(LH):
        sel[h, h * P:(h + 1) * P] = 1
    pos = ar(L).astype(f)

    def tiles(a):
        return np.ascontiguousarray(a.reshape((NT, P) + a.shape[1:]).swapaxes(0, 1).astype(f))

    def rope(angle):
        c, s = np.cos(angle).astype(f), np.sin(angle).astype(f)
        return tiles(np.stack([np.concatenate([c, c], -1), np.concatenate([-s, s], -1)], 1))

    frac = (2 * ar(HD // 2) / HD).astype(f)
    a_A = (pos[:, None] / np.power(f(1250), frac)[None, :]).astype(f)
    a_D = (pos[:, None] * (f(1) / np.power(f(10000), (ar(0, HD, 2).astype(f) / f(HD))))[None, :]).astype(f)
    half = ar(0, LD, 2).astype(f)
    inv = (f(1) / np.power(f(10000), half / f(LD))).astype(f)
    fr = (pos[:, None] * inv[None, :]).astype(f)
    base = ((half + f(0.4 * LD)) / f(1.4 * LD)).astype(f)
    power = ((pos - L // 2) / f(WIN // 2)).astype(f)
    sc = np.power(base[None, :], power[:, None]).astype(f)
    c, s = np.cos(fr).astype(f), np.sin(fr).astype(f)
    cc, ss, sc2 = np.concatenate([c, c], -1), np.concatenate([-s, s], -1), np.concatenate([sc, sc], -1)
    xpos = np.stack([np.stack([cc * sc2, cc / sc2], 1), np.stack([ss * sc2, ss / sc2], 1)], 1)
    return {"ident": np.eye(P, dtype=f), "masks": masks, "shift": shift, "sel": sel,
            "rope_A": rope(a_A), "rope_D": rope(a_D), "xpos": tiles(xpos)}


def kernel(**inputs):
    import numpy as _np
    import concourse.bacc as _bacc
    from concourse import mybir as _mybir
    from concourse.bass_utils import run_bass_kernel_spmd as _run

    nc = _bacc.Bacc("TRN2", target_bir_lowering=False, num_devices=1)
    arrays, ins, consts = {}, {}, {}
    for name, a in inputs.items():
        if name == "L1_attn_mask":
            continue
        a = _np.ascontiguousarray(a)
        arrays[f"in_{name}_dram"] = a
        ins[name] = nc.dram_tensor(f"in_{name}_dram", a.shape, _mybir.dt.from_np(a.dtype), kind="ExternalInput").ap()
    for name, a in constants().items():
        arrays[f"const_{name}_dram"] = a
        consts[name] = nc.dram_tensor(f"const_{name}_dram", a.shape, _mybir.dt.from_np(a.dtype), kind="ExternalInput").ap()
    shape, dtype = _OUTS[0]
    out = nc.dram_tensor("out_0_dram", shape, _mybir.dt.from_np(_np.dtype(dtype)), kind="ExternalOutput").ap()
    network_kernel(nc, ins, consts, out)
    r = _run(nc, [arrays], core_ids=[0])
    return r.results[0]["out_0_dram"]
```

```python
import concourse.bass as bass
from concourse import mybir
from contextlib import ExitStack

B, L, C = 8, 512, 128
P = 128
NT = L // P
H, HD = 16, 8
HG = 4
NG = H // HG
SLOT = 32
MSLOT = 3 * HD
LH, LD, WIN = 8, 64, 64
BAND = P + WIN
HID = 341
HB = [128, 128, HID - 256]
NE, FF = 4, 512
EPS = 1e-5
NEG = -1.0e30


def network_kernel(nc: bass.Bass, ins, consts, out: bass.AP):
    fp32, fp32r, bf16 = mybir.dt.float32, mybir.dt.float32r, mybir.dt.bfloat16
    ALU = mybir.AluOpType
    ACT = mybir.ActivationFunctionType
    X = mybir.AxisListType.X

    ctx = ExitStack()
    with ctx:
        def sb(name, shape, dt=fp32):
            return ctx.enter_context(nc.sbuf_tensor(name, shape, dt))

        class Signal:

            def __init__(self, name, per_batch):
                self.sem, self.per = ctx.enter_context(nc.semaphore(name)), per_batch

            def at(self, b, n):
                return b * self.per + n

        ident = sb("ident", [P, P])
        ident_h = sb("ident_h", [P, P], bf16)
        shift = sb("shift", [P, 2, P])
        mask_h = sb("mask_h", [P, 2 * P + 3 * BAND], bf16)
        causal_qk = mask_h[:, 0:P]
        causal_kq = mask_h[:, P:2 * P]
        band_qk = mask_h[:, 2 * P:2 * P + BAND]
        band_q0 = mask_h[:, 2 * P + BAND:2 * P + 2 * BAND]
        band_kq = mask_h[:, 2 * P + 2 * BAND:2 * P + 3 * BAND]
        pick_head = sb("pick_head", [LH, LH], fp32r)
        rope = {s: sb(f"rope_{s}", [P, NT, 2, HD]) for s in "AD"}
        wqkv = {s: sb(f"wqkv_{s}", [P, 3 * C]) for s in "ACD"}
        wout = {s: sb(f"wout_{s}", [P, C]) for s in "ACD"}
        bqkv = sb("bqkv", [P, 3 * C])
        bout = sb("bout", [P, C])
        lw_qkv = sb("lw_qkv", [P, 2, 3 * LH * LD])
        lw_o = sb("lw_o", [P, 2, 4, C])
        lw_1 = sb("lw_1", [P, 2, 2 * HID])
        lw_2 = sb("lw_2", [P, 2, 3, C])
        lb_1 = sb("lb_1", [P, 2, 2, 3])
        lb_2 = sb("lb_2", [P, 2, C])
        l_gb = sb("l_gb", [P, 2, 2])
        l_scale = sb("l_scale", [P, 2, 2, 2, LD])
        tab = sb("tab", [P, 2, NT, 2, 2, LD])
        ln1 = sb("ln1", [P, 2])
        ln2 = sb("ln2", [P, 2])
        conv = sb("conv", [P, 3])
        router = sb("router", [P, NE])
        e_wv = sb("e_wv", [P, NE, 2 * FF])
        e_pr = sb("e_pr", [P, NE, FF // P, C])
        one = sb("one", [P, 1])
        m_half = sb("m_half", [P, 2 * LH])

        xin = sb("xin", [P, NT, C])
        xa = sb("xa", [P, NT, C])
        xb = sb("xb", [P, NT, C])
        xc = sb("xc", [P, NT, C])
        yd = sb("yd", [P, NT, C])
        xd = sb("xd", [P, NT, C])
        yo = sb("yo", [P, NT, C])
        l_x = sb("l_x", [P, NT, C])
        l_m = sb("l_m", [P, NT, C])
        hn = [sb(f"hn{k}", [P, NT, C]) for k in range(2)]
        hT = [sb(f"hT{k}", [P, L + 2]) for k in range(2)]
        stats = [sb(f"stats{k}", [P, NT, 2, 6]) for k in range(2)]
        mv = [sb(f"mv{k}", [P, NT, 2]) for k in range(2)]
        rstd = [sb(f"rstd{k}", [P, NT]) for k in range(2)]
        held = sb("held", [P, 1])
        xT = sb("xT", [P, L])
        stack = sb("stack", [P, NT, 2, H, SLOT], fp32r)
        vaug = sb("vaug", [P, NT, H, SLOT])
        with ExitStack() as shared:
            def over(name, shape, dt=fp32):
                return shared.enter_context(nc.sbuf_tensor(name, shape, dt))

            xpos = over("xpos", [P, NT, 2, 2, LD])
            mask_f = over("mask_f", [P, 2 * P + 3 * BAND])
        KT = sb("KT", [P, NG, L], fp32r)
        QT = sb("QT", [P, NG, L], fp32r)
        QM = sb("QM", [P, 2, L], fp32r)
        prob = sb("prob", [P, 3, L])
        work = sb("work", [P, 3, NT * 2 * C])
        qk, qk_c, qk_s = (work[:, k, :].rearrange("p (t h d) -> p t h d", t=NT, d=HD) for k in range(3))
        oT = work[:, 0:2, :].rearrange("p a n -> p (a n)").rearrange("p (g n) -> p g n", g=NG)
        heads = work[:, 2, 0:NT * C].rearrange("p (t c) -> p t c", t=NT)
        headsT = work[:, 2, NT * C:2 * NT * C]
        rden = sb("rden", [P, NG, NT, HG])
        xsT = sb("xsT", [P, L])
        l_v = sb("l_v", [P, NT, LH, LD + 1])
        with ExitStack() as shared:
            sq = over("sq", [P, 2, LH * LD])
            l_c = over("l_c", [P, NT, 2 * LH, LD])
            l_s = over("l_s", [P, 2, LH, LD])
            ssum = over("ssum", [P, NT, 2 * LH])
            rn = over("rn", [P, NT, 2 * LH])
            l_T = over("l_T", [P, 8, L])
            nm = over("nm", [P, NT, LH])
            nmT = over("nmT", [LH, L], fp32r)
            l_p = over("l_p", [P, 4, 2 * BAND])
            l_rd = over("l_rd", [P, 2, NT])
            l_o = l_c[:, 0:2, :, :].rearrange("p a h d -> p (a h d)").rearrange("p (t n) -> p t n", t=NT)
            l_oT, hidT, gel = l_T[:, 0:4], l_T[:, 0:3], l_T[:, 4:7]
        with ExitStack() as shared:
            sil = over("sil", [P, 2, L])
            eact = over("eact", [P, 2, FF // P, L])
            lg = over("lg", [P, NT, NE])
            lmax = over("lmax", [P, NT])
            free = over("free", [P, NT])
            pick = over("pick", [P, NT, NE])

        ps = ctx.enter_context(nc.psum_tensor("ps", [P, 8, 512], fp32))

        def bank(i):
            return ps[:, i, :]

        def four(i):
            return ps[:, i, :].rearrange("p (t c) -> p t c", t=NT)

        SC, SK, PV, OT = 0, 2, 4, 5
        stack_f = stack[:, :, :, :, :].bitcast(fp32)

        loaded = ctx.enter_context(nc.semaphore("weights_loaded"))
        consts_ready = ctx.enter_context(nc.semaphore("consts_ready"))
        presets = ctx.enter_context(nc.semaphore("presets"))
        S = {}

        class Part:
            def __init__(self, whole, offset):
                self.sem, self.whole, self.offset = whole.sem, whole, offset

        def signals(stages, **per):
            for k, n in per.items():
                each = [n] * len(stages) if isinstance(n, int) else n
                whole = Signal(f"{k}_{stages}", sum(each))
                for i, s in enumerate(stages):
                    S[s, k] = Part(whole, sum(each[:i]))

        def sem(s, what):
            return S[s, what].sem

        def at(s, what, b, n):
            p = S[s, what]
            return p.sem, p.whole.at(b, p.offset + n)

        for stages in ("A", "CD"):
            signals(stages, xT=1, qkv_ps=NT, stacked=1, dup=1, kq_ps=8, kq=8, sc_ps=UNITS, mx=UNITS,
                    keys_ps=UNITS + NG, keys_out=UNITS + NG, pv=UNITS, ev=NG, ot_ps=NG, ctx=NG, cT_ps=1, cT=1,
                    o_ps=1, res=1)
        signals("A", xT_ps=1, used=1)
        signals("CN", xT_ps=1)
        signals("L", x=16)
        signals("S", y=1, stored=16)
        signals("01", xT_ps=1, xT=1, qkv_ps=3 * NT, sq=2 * NT, v=NT, roped=2 * NT, added=2 * NT, ssum=NT, rn=NT,
                nrm=NT, T_ps=8, T=8, sc_ps=2 * LH, mx=2 * LH, nm_ps=1, nmT=1, st_ps=2 * LH, ex=2 * LH, pv=LH, o=LH,
                oT_ps=4, oT=4, o_ps=1, lm=1, sh_ps=1, g_ps=6, gel=3, hid=3, f_ps=1, out=1)
        signals("01", hn=1, hT_ps=1, hT=1)
        signals("M", hn=1, hT_ps=1, hT=1)
        signals("M", lg_ps=1, lg=1, g_ps=16, v_ps=16, sil=16, act=16, e_ps=NE, acc=NE)
        signals("A", var=1, rstd=1, done=1)
        signals("01B", var=1, rstd=1)
        signals("B", done=1)
        signals("CND", var=[1, 1, 0], rstd=[1, 1, 0], done=[1, 1, 0])
        signals("MF", var=1, rstd=1)
        signals("A", step=STEPS["A"])
        signals("01B", step=[STEPS["0"], STEPS["1"], STEPS["B"]])
        signals("CND", step=[STEPS["C"], STEPS["N"], STEPS["D"]])
        signals("MF", step=[STEPS["M"], STEPS["F"]])

        block = ctx.enter_context(nc.Block())

        def first(s, j):
            return j * P if s in "AD" else 0

        def use(n):
            return n + min(NG, 1 + (n + 1) // 16)

        def turn(g):
            return 0 if g == 0 else 16 * g - 1 + g

        def slot(*streams):
            order = sorted(((k + 0.5) / n, i) for i, (_, n) in enumerate(streams) for k in range(n))
            for _, i in order:
                next(streams[i][0])
            for g, _ in streams:
                assert next(g, None) is None

        def batch_loop(eng, att, loc, exp):
            def iteration(i, new=True, mid=True, old=True):
                slot(*([(att(i, "A"), SEGS["A"])] if new else []), *([(exp(i - 2), SEGS["M"])] if old else []))
                slot(*([(att(i - 1, "C"), SEGS["C"])] if mid else []), *([(loc(i, 0), SEGS["0"])] if new else []))
                slot(*([(att(i - 1, "D"), SEGS["D"])] if mid else []), *([(loc(i, 1), SEGS["1"])] if new else []))

            iteration(0, mid=False, old=False)
            iteration(1, old=False)
            with eng.Fori(2, B) as i:
                iteration(i)
            iteration(B, new=False)
            iteration(B + 1, new=False, mid=False)

        n_loads = [0]

        @block.sync
        def _(sp):
            def load(dst, src):
                sp.dma_start(dst, src).then_inc(loaded, 16)
                n_loads[0] += 1

            def row(ap):
                n = ap.shape[0]
                return ap.rearrange("(a n) -> a n", a=1).broadcast_to([P, n])

            load(ident[:, :], consts["ident"])
            load(mask_f[:, :], consts["masks"])
            load(shift[:, :, :], consts["shift"])
            load(rope["A"][:, :, :, :], consts["rope_A"])
            load(rope["D"][:, :, :, :], consts["rope_D"])
            load(xpos[:, :, :, :, :], consts["xpos"])
            for i, n in enumerate(("wq", "wk", "wv")):
                load(wqkv["A"][:, i * C:(i + 1) * C], ins[f"L0_attn_{n}_w"])
                load(bqkv[:, i * C:(i + 1) * C], row(ins[f"L0_attn_{n}_b"]))
            load(wout["A"][:, :], ins["L0_attn_wo_w"])
            load(bout[:, :], row(ins["L0_attn_wo_b"]))
            for i, n in enumerate(("Wq", "Wk", "Wv")):
                load(wqkv["C"][:, i * C:(i + 1) * C], ins[f"L1_attn_{n}"])
            load(wout["C"][:, :], ins["L1_attn_Wout"])
            load(wqkv["D"][:, :], ins["L1_ffn_attn_w"])
            load(wout["D"][:, :], ins["L1_ffn_proj_w"])
            load(lw_qkv[:, :, :], ins["L0_ffn_wqkv"].rearrange("l c n -> c l n"))
            for l in range(2):
                load(lw_o[:, l], ins["L0_ffn_wo"][l].rearrange("(k c) n -> c k n", c=P))
                load(lw_2[:, l, 0:2], ins["L0_ffn_w2"][l, 0:256].rearrange("(k c) n -> c k n", c=P))
                load(lw_2[0:HB[2], l, 2], ins["L0_ffn_w2"][l, 256:HID])
                load(lb_2[:, l], row(ins["L0_ffn_b2"][l]))
                for half in range(2):
                    for j, n in enumerate(HB):
                        c0 = half * HID + j * P
                        load(lb_1[0:n, l, half, j:j + 1], ins["L0_ffn_b1"][l, c0:c0 + n].rearrange("(c a) -> c a", a=1))
                load(l_gb[:, l, 0:1], ins["L0_ffn_ln_g"][l].rearrange("(c a) -> c a", a=1))
                load(l_gb[:, l, 1:2], ins["L0_ffn_ln_b"][l].rearrange("(c a) -> c a", a=1))
                for i, n in enumerate(("q", "k")):
                    v = ins[f"L0_ffn_{n}_scale"][l]
                    load(l_scale[:, l, 0, i, :], row(v))
                    load(l_scale[:, l, 1, i, 0:LD // 2], row(v[LD // 2:LD]))
                    load(l_scale[:, l, 1, i, LD // 2:LD], row(v[0:LD // 2]))
            load(lw_1[:, :, :], ins["L0_ffn_w1"].rearrange("l c n -> c l n"))
            for t, n in ((ln1, "ln1"), (ln2, "ln2")):
                load(t[:, 0:1], ins[f"L1_ffn_{n}_w"].rearrange("(c a) -> c a", a=1))
                load(t[:, 1:2], ins[f"L1_ffn_{n}_b"].rearrange("(c a) -> c a", a=1))
            load(conv[:, :], ins["L1_ffn_conv_w"].rearrange("c a k -> c (a k)"))
            load(router[:, :], ins["L1_ffn_router_w"])
            load(e_wv[:, :, :], ins["L1_ffn_expert_wv"].rearrange("e c n -> c e n"))
            for e in range(NE):
                load(e_pr[:, e], ins["L1_ffn_expert_proj"][e].rearrange("(k c) n -> c k n", c=P))
            def x_of(b):
                return b.rearrange("o (t p) c -> p (o t) c", p=P)

            def load_x(b):
                sp.dma_start(xin[:, :, :], x_of(ins["L0_attn_x"][bass.ds(b, 1)])).then_inc(sem("L", "x"), 16)

            def store(b):
                sp.wait_ge(*at("S", "y", b, 1))
                sp.dma_start(x_of(out[bass.ds(b, 1)]), yo[:, :, :]).then_inc(sem("S", "stored"), 16)

            load_x(0)
            for b in range(2):
                sp.wait_ge(*at("A", "used", b, 1))
                load_x(b + 1)
            with sp.Fori(2, B - 1) as b:
                sp.wait_ge(*at("A", "used", b, 1))
                load_x(b + 1)
                store(b - 2)
            for b in range(B - 3, B):
                store(b)
            sp.wait_ge(*at("S", "stored", B, 16))

        LOADS = 16 * n_loads[0]

        @block.tensor
        def _(pe):
            pe.wait_ge(loaded, LOADS)
            pe.wait_ge(consts_ready, 3)

            def transpose4(src, dst):
                for t in range(NT):
                    last = nc.tensor.transpose(dst[:, t * P:(t + 1) * P], src[:, t, :], ident[:, :])
                return last

            def attention(b, s):
                causal = s != "C"
                if s == "A":
                    pe.wait_ge(*at("L", "x", b, 16))
                    transpose4(xin, bank(0)).then_inc(sem("A", "xT_ps"), 1)
                    yield
                elif s == "C":
                    pe.wait_ge(*at("B", "done", b, 1))
                    transpose4(xb, bank(0)).then_inc(sem("C", "xT_ps"), 1)
                    yield
                else:
                    yield
                    yield
                    pe.wait_ge(*at("N", "done", b, 1))
                    transpose4(hn[0], bank(0)).then_inc(sem("N", "xT_ps"), 1)
                    yield
                    yield
                for t in range(NT):
                    if t == 0:
                        pe.wait_ge(*at(s, "xT", b, 1))
                    nc.tensor.matmul(ps[:, t, 0:3 * C], xT[:, t * P:(t + 1) * P], wqkv[s][:, :],
                                     start=True, stop=True).then_inc(sem(s, "qkv_ps"), 1)
                    yield
                for _ in range(4):
                    yield
                for n in range(8):
                    g, which = n // 2, 1 - n % 2
                    if n == 0:
                        pe.wait_ge(*at(s, "stacked", b, 1))
                        pe.wait_ge(*at(s, "dup", b, 1))
                    if n >= 4:
                        pe.wait_ge(*at(s, "kq", b, n - 3))
                    for t in range(NT):
                        last = nc.tensor.transpose(ps[:, n % 4, t * P:(t + 1) * P],
                                                   stack_f[:, t, which, g * HG:(g + 1) * HG, :].rearrange("p h s -> p (h s)"),
                                                   ident[:, :])
                    last.then_inc(sem(s, "kq_ps"), 1)
                    yield

                def scores(n):
                    h, i = n // NT, n % NT
                    g, r = h // HG, h % HG * SLOT
                    if n == 0:
                        pe.wait_ge(*at(s, "kq", b, 8))
                    if n >= 2:
                        pe.wait_ge(*at(s, "mx", b, n - 1))
                    N = (i + 1) * P if causal else L
                    m = nc.tensor.matmul(ps[:, SC + n % 2, 0:N], QT[r:r + MSLOT, g, i * P:(i + 1) * P],
                                         KT[r:r + MSLOT, g, 0:N], start=True, stop=True)
                    if causal:
                        m = nc.tensor.matmul(ps[:, SC + n % 2, i * P:(i + 1) * P], ident_h[:, :], causal_qk,
                                             start=False, stop=True, skip_group_check=True)
                    m.then_inc(sem(s, "sc_ps"), 1)

                def shifted(g):
                    u = turn(g)
                    pe.wait_ge(*at(s, "mx", b, (g + 1) * 16))
                    if u >= 2:
                        pe.wait_ge(*at(s, "keys_out", b, u - 1))
                    for t in range(NT):
                        last = nc.tensor.transpose(ps[:, SK + u % 2, t * P:(t + 1) * P],
                                                   stack_f[:, t, 0, g * HG:(g + 1) * HG, :].rearrange("p h s -> p (h s)"),
                                                   ident[:, :])
                    last.then_inc(sem(s, "keys_ps"), 1)

                def keys_first(n):
                    h, j, u = n // NT, n % NT, use(n)
                    g, r = h // HG, h % HG * SLOT
                    pe.wait_ge(*at(s, "keys_out", b, max(u - 1, turn(g) + 1)))
                    q0 = first(s, j)
                    m = nc.tensor.matmul(ps[:, SK + u % 2, 0:L - q0], KT[r:r + SLOT, g, j * P:(j + 1) * P],
                                         QM[r:r + SLOT, g % 2, q0:L], start=True, stop=True)
                    if causal:
                        m = nc.tensor.matmul(ps[:, SK + u % 2, 0:P], ident_h[:, :], causal_kq,
                                             start=False, stop=True, skip_group_check=True)
                    m.then_inc(sem(s, "keys_ps"), 1)

                def weigh(n):
                    h, j = n // NT, n % NT
                    r, q0 = h % HG * SLOT, first(s, j)
                    pe.wait_ge(*at(s, "keys_out", b, use(n) + 1))
                    if n % 16 == 0 and n:
                        pe.wait_ge(*at(s, "ev", b, n // 16))
                    nc.tensor.matmul(ps[r:r + SLOT, PV, q0:L], vaug[:, j, h, :], prob[:, n % 3, q0:L],
                                     start=(j == 0), stop=True, skip_group_check=True).then_inc(sem(s, "pv"), 1)

                for n in range(LEAD):
                    scores(n)
                    if n == LEAD - 2:
                        shifted(0)
                    yield
                for n in range(UNITS):
                    keys_first(n)
                    if n + LEAD < UNITS:
                        scores(n + LEAD)
                    if n >= 1:
                        weigh(n - 1)
                    if n % 16 == 14 and n // 16 + 1 < NG:
                        shifted(n // 16 + 1)
                    yield
                weigh(UNITS - 1)
                yield
                for g in range(NG):
                    if g == 0:
                        pe.wait_ge(*at(s, "ev", b, NG))
                        pe.wait_ge(*at(s, "mx", b, UNITS))
                    for t in range(NT):
                        last = nc.tensor.transpose(ps[:, g, t * P:(t + 1) * P], oT[:, g, t * P:(t + 1) * P], ident[:, :])
                    last.then_inc(sem(s, "ot_ps"), 1)
                    yield
                pe.wait_ge(*at(s, "ctx", b, NG))
                transpose4(heads, bank(PV)).then_inc(sem(s, "cT_ps"), 1)
                yield
                pe.wait_ge(*at(s, "cT", b, 1))
                for t in range(NT):
                    last = nc.tensor.matmul(ps[:, 0, t * P:(t + 1) * P], headsT[:, t * P:(t + 1) * P], wout[s][:, :],
                                            start=True, stop=True)
                last.then_inc(sem(s, "o_ps"), 1)
                yield
                for _ in range(2):
                    yield
                pe.wait_ge(*at(s, "res", b, 1))
                yield

            def local_layer(b, l):
                s = str(l)
                if l == 0:
                    pe.wait_ge(*at("A", "done", b, 1))
                else:
                    pe.wait_ge(*at("0", "out", b, 1))
                transpose4(xa if l == 0 else l_x, bank(OT)).then_inc(sem(s, "xT_ps"), 1)
                yield
                for u in range(3 * NT):
                    t, p = u // 3, u % 3
                    if u == 0:
                        pe.wait_ge(*at(s, "xT", b, 1))
                    if t and p < 2:
                        pe.wait_ge(*at(s, "roped", b, 2 * (t - 1) + p + 1))
                        pe.wait_ge(*at(s, "sq", b, 2 * (t - 1) + p + 1))
                    elif t:
                        pe.wait_ge(*at(s, "v", b, t))
                    nc.tensor.matmul(bank(OT + p), xsT[:, t * P:(t + 1) * P], lw_qkv[:, l, p * 512:(p + 1) * 512],
                                     start=True, stop=True).then_inc(sem(s, "qkv_ps"), 1)
                    yield
                yield
                for n in range(8):
                    if n == 0:
                        pe.wait_ge(*at(s, "nrm", b, NT))
                        pe.wait_ge(*at(s, "v", b, NT))
                    if n >= 3:
                        pe.wait_ge(*at(s, "T", b, n - 2))
                    for t in range(NT):
                        m = nc.tensor.transpose(ps[:, OT + n % 3, t * P:(t + 1) * P],
                                                l_c[:, t, 2 * n:2 * n + 2, :].rearrange("p h d -> p (h d)"), ident[:, :])
                    m.then_inc(sem(s, "T_ps"), 1)
                    yield
                for m_ in range(2 * LH):
                    h = m_ // 2
                    r, k = h % 2 * LD, h // 2
                    if m_ == 0:
                        pe.wait_ge(*at(s, "T", b, 8))
                    if m_ >= 3:
                        pe.wait_ge(*at(s, "mx", b, m_ - 2))
                    for t in (m_ % 2 * 2, m_ % 2 * 2 + 1):
                        o = ps[:, OT + m_ % 3, t % 2 * BAND:(t % 2 + 1) * BAND]
                        k0 = max(t * P - WIN, 0)
                        N = (t + 1) * P - k0
                        nc.tensor.matmul(o, ident_h[:, :], band_qk if t else band_q0, start=True, stop=True)
                        m = nc.tensor.matmul(o[:, BAND - N:BAND], l_T[r:r + LD, k, t * P:(t + 1) * P],
                                             l_T[r:r + LD, 4 + k, k0:(t + 1) * P], start=False, stop=True,
                                             skip_group_check=True)
                    m.then_inc(sem(s, "sc_ps"), 1)
                    yield
                pe.wait_ge(*at(s, "mx", b, 2 * LH))
                for t in range(NT):
                    m = nc.tensor.transpose(ps[0:LH, OT, t * P:(t + 1) * P], nm[:, t, :], ident[:, :])
                m.then_inc(sem(s, "nm_ps"), 1)
                yield

                def weigh(h):
                    pe.wait_ge(*at(s, "ex", b, 2 * h + 2))
                    if h >= 1:
                        pe.wait_ge(*at(s, "o", b, h))
                    for t in range(NT):
                        o = ps[:, OT + 2, t * (LD + 1):(t + 1) * (LD + 1)]
                        pr = l_p[:, 2 * h % 4 + t // 2, t % 2 * BAND:(t % 2 + 1) * BAND]
                        m = nc.tensor.matmul(o, pr[:, 0:P], l_v[:, t, h, :], start=True, stop=True)
                        if t:
                            pr = l_p[:, 2 * h % 4 + (t - 1) // 2, (t - 1) % 2 * BAND:((t - 1) % 2 + 1) * BAND]
                            m = nc.tensor.matmul(o[0:WIN], pr[:, P:BAND], l_v[:, t - 1, h, :],
                                                 start=False, stop=True, skip_group_check=True)
                    m.then_inc(sem(s, "pv"), 1)

                for m_ in range(2 * LH):
                    h = m_ // 2
                    r, k = h % 2 * LD, h // 2
                    if m_ == 0:
                        pe.wait_ge(*at(s, "nmT", b, 1))
                    if m_ >= 2:
                        pe.wait_ge(*at(s, "ex", b, m_ - 1))
                    for t in (m_ % 2 * 2, m_ % 2 * 2 + 1):
                        q1 = min(t * P + BAND, L)
                        N = q1 - t * P
                        o = ps[:, OT + m_ % 2, t % 2 * BAND:t % 2 * BAND + N]
                        nc.tensor.matmul(o, ident_h[:, :], band_kq[:, 0:N], start=True, stop=False)
                        nc.tensor.matmul(o, pick_head[:, h:h + 1].broadcast_to([LH, P]), nmT[:, t * P:q1],
                                         start=False, stop=False)
                        m = nc.tensor.matmul(o, l_T[r:r + LD, 4 + k, t * P:(t + 1) * P], l_T[r:r + LD, k, t * P:q1],
                                             start=False, stop=True)
                    m.then_inc(sem(s, "st_ps"), 1)
                    if m_ % 2 and h >= 1:
                        weigh(h - 1)
                    yield
                weigh(LH - 1)
                yield
                for k in range(4):
                    if k == 0:
                        pe.wait_ge(*at(s, "o", b, LH))
                    if k >= 2:
                        pe.wait_ge(*at(s, "oT", b, k - 1))
                    for t in range(NT):
                        m = nc.tensor.transpose(ps[:, OT + k % 2, t * P:(t + 1) * P], l_o[:, t, k * P:(k + 1) * P],
                                                ident[:, :])
                    m.then_inc(sem(s, "oT_ps"), 1)
                    yield
                pe.wait_ge(*at(s, "oT", b, 4))
                for t in range(NT):
                    for k in range(4):
                        m = nc.tensor.matmul(ps[:, OT + 2, t * P:(t + 1) * P], l_oT[:, k, t * P:(t + 1) * P],
                                             lw_o[:, l, k, :], start=(k == 0), stop=(k == 3))
                m.then_inc(sem(s, "o_ps"), 1)
                yield
                pe.wait_ge(*at(s, "lm", b, 1))
                for t in range(NT):
                    o = ps[:, OT, t * 64:(t + 1) * 64]
                    m = nc.tensor.matmul(o, shift[:, 0, :], l_m[:, t, 64:128], start=True, stop=(t == 0))
                    if t:
                        m = nc.tensor.matmul(o, shift[:, 1, :], l_m[:, t - 1, 64:128], start=False, stop=True)
                m.then_inc(sem(s, "sh_ps"), 1)
                yield
                yield
                pe.wait_ge(*at(s, "hn", b, 1))
                transpose4(hn[1], bank(OT + 1)).then_inc(sem(s, "hT_ps"), 1)
                yield
                for u in range(6):
                    j, half = u // 2, 1 - u % 2
                    if u == 0:
                        pe.wait_ge(*at(s, "hT", b, 1))
                    if u in (3, 5):
                        pe.wait_ge(*at(s, "gel", b, (u - 3) // 2 + 1))
                    if u == 4:
                        pe.wait_ge(*at(s, "hid", b, 1))
                    c0 = half * HID + j * P
                    nc.tensor.matmul(ps[0:HB[j], OT + u % 3, :], lw_1[:, l, c0:c0 + HB[j]], hT[1][:, 2:L + 2],
                                     start=True, stop=True).then_inc(sem(s, "g_ps"), 1)
                    yield
                for t in range(NT):
                    if t == 0:
                        pe.wait_ge(*at(s, "hid", b, 3))
                    for j in range(3):
                        m = nc.tensor.matmul(ps[:, OT + 1, t * P:(t + 1) * P], hidT[0:HB[j], j, t * P:(t + 1) * P],
                                             lw_2[0:HB[j], l, j, :], start=(j == 0), stop=(j == 2))
                    if t == 3:
                        m.then_inc(sem(s, "f_ps"), 1)
                    if t % 2:
                        yield
                if l == 1:
                    yield
                    yield

            def experts(b):
                yield
                yield
                pe.wait_ge(*at("M", "hn", b, 1))
                transpose4(hn[1], bank(OT)).then_inc(sem("M", "hT_ps"), 1)
                yield
                pe.wait_ge(*at("M", "hT", b, 1))
                for t in range(NT):
                    m = nc.tensor.matmul(ps[:, OT + 1, t * NE:(t + 1) * NE], hT[1][:, 2 + t * P:2 + (t + 1) * P],
                                         router[:, :], start=True, stop=True)
                m.then_inc(sem("M", "lg_ps"), 1)
                yield

                def project(e, t):
                    if t == 0:
                        pe.wait_ge(*at("M", "act", b, 4 * e + 4))
                        if e:
                            pe.wait_ge(*at("M", "acc", b, e))
                    for j in range(4):
                        m = nc.tensor.matmul(ps[:, OT + 2, t * P:(t + 1) * P], eact[:, e % 2, j, t * P:(t + 1) * P],
                                             e_pr[:, e, j, :], start=(j == 0), stop=(j == 3))
                    if t == NT - 1:
                        m.then_inc(sem("M", "e_ps"), 1)

                for n in range(16):
                    e, j = n // 4, n % 4
                    if n:
                        pe.wait_ge(*at("M", "sil", b, n))
                    nc.tensor.matmul(bank(OT), e_wv[:, e, j * P:(j + 1) * P], hT[1][:, 2:L + 2],
                                     start=True, stop=True).then_inc(sem("M", "g_ps"), 1)
                    yield
                    if n:
                        pe.wait_ge(*at("M", "act", b, n))
                    else:
                        pe.wait_ge(*at("M", "lg", b, 1))
                    nc.tensor.matmul(bank(OT + 1), e_wv[:, e, FF + j * P:FF + (j + 1) * P], hT[1][:, 2:L + 2],
                                     start=True, stop=True).then_inc(sem("M", "v_ps"), 1)
                    yield
                    if e:
                        project(e - 1, j)
                        yield
                for t in range(NT):
                    project(NE - 1, t)
                    yield
                for _ in range(2):
                    yield

            batch_loop(pe, attention, local_layer, experts)

        @block.scalar
        def _(act):
            act.wait_ge(loaded, LOADS)

            def copy(dst, src):
                return nc.scalar.activation(dst, src, ACT.Copy)

            def attention(b, s):
                if s != "D":
                    act.wait_ge(*at(s, "xT_ps", b, 1))
                    copy(xT[:, :], bank(0)).then_inc(sem(s, "xT"), 1)
                    yield
                else:
                    for _ in range(4):
                        yield
                for _ in range(NT + 4):
                    yield
                for n in range(8):
                    act.wait_ge(*at(s, "kq_ps", b, n + 1))
                    copy((KT, QT)[n % 2][:, n // 2, :], bank(n % 4)).then_inc(sem(s, "kq"), 1)
                    yield

                def turned(g):
                    act.wait_ge(*at(s, "keys_ps", b, turn(g) + 1))
                    copy(QM[:, g % 2, :], bank(SK + turn(g) % 2)).then_inc(sem(s, "keys_out"), 1)

                def sums(g):
                    act.wait_ge(*at(s, "pv", b, 16 * (g + 1)))
                    copy(oT[:, g, :], bank(PV)).then_inc(sem(s, "ev"), 1)

                for n in range(LEAD):
                    if n == LEAD - 2:
                        turned(0)
                    yield
                for n in range(UNITS):
                    j, u = n % NT, use(n)
                    act.wait_ge(*at(s, "keys_ps", b, u + 1))
                    if n >= 3:
                        act.wait_ge(*at(s, "pv", b, n - 2))
                    q0 = first(s, j)
                    nc.scalar.activation(prob[:, n % 3, q0:L], ps[:, SK + u % 2, 0:L - q0], ACT.Exp,
                                         scale=float(HD) ** -0.5).then_inc(sem(s, "keys_out"), 1)
                    if n % 16 == 0 and n:
                        sums(n // 16 - 1)
                    if n % 16 == 14 and n // 16 + 1 < NG:
                        turned(n // 16 + 1)
                    yield
                sums(NG - 1)
                yield
                for g in range(NG):
                    yield
                act.wait_ge(*at(s, "cT_ps", b, 1))
                copy(headsT, bank(PV)).then_inc(sem(s, "cT"), 1)
                yield
                for _ in range(4):
                    yield

            def local_layer(b, l):
                s = str(l)
                act.wait_ge(*at(s, "xT_ps", b, 1))
                copy(xsT[0:64, :], ps[0:64, OT, :])
                copy(xsT[64:128, 1:L], ps[64:128, OT, 0:L - 1]).then_inc(sem(s, "xT"), 1)
                yield
                for u in range(3 * NT):
                    t, p = u // 3, u % 3
                    act.wait_ge(*at(s, "qkv_ps", b, u + 1))
                    if p < 2:
                        w = 2 * t + p
                        if w >= 2:
                            act.wait_ge(*at(s, "roped", b, w - 1))
                        nc.scalar.activation(sq[:, w % 2, :], bank(OT + p), ACT.Square).then_inc(sem(s, "sq"), 1)
                    else:
                        copy(l_v[:, t, :, 0:LD], bank(OT + 2).rearrange("p (h d) -> p h d", d=LD)).then_inc(sem(s, "v"), 1)
                    yield
                yield
                for n in range(8):
                    act.wait_ge(*at(s, "T_ps", b, n + 1))
                    copy(l_T[:, n, :], bank(OT + n % 3)).then_inc(sem(s, "T"), 1)
                    yield
                for _ in range(2 * LH):
                    yield
                act.wait_ge(*at(s, "nm_ps", b, 1))
                copy(nmT[:, :], ps[0:LH, OT, :]).then_inc(sem(s, "nmT"), 1)
                yield
                for m in range(2 * LH):
                    act.wait_ge(*at(s, "st_ps", b, m + 1))
                    if m >= 4:
                        act.wait_ge(*at(s, "pv", b, m // 2 - 1))
                    n = 2 * BAND if m % 2 == 0 else BAND + P
                    nc.scalar.activation(l_p[:, m % 4, 0:n], ps[:, OT + m % 2, 0:n], ACT.Exp,
                                         scale=8.0).then_inc(sem(s, "ex"), 1)
                    yield
                yield
                for k in range(4):
                    act.wait_ge(*at(s, "oT_ps", b, k + 1))
                    copy(l_oT[:, k, :], bank(OT + k % 2)).then_inc(sem(s, "oT"), 1)
                    yield
                for _ in range(4):
                    yield
                for u in range(6):
                    j = u // 2
                    if u % 2 == 0:
                        act.wait_ge(*at(s, "g_ps", b, u + 1))
                        n = HB[j]
                        nc.scalar.activation(gel[0:n, j, :], ps[0:n, OT + u % 3, :], ACT.Gelu,
                                             bias=lb_1[0:n, l, 1, j:j + 1]).then_inc(sem(s, "gel"), 1)
                    yield
                for _ in range(2 if l == 0 else 4):
                    yield

            def experts(b):
                for _ in range(4):
                    yield
                for n in range(16):
                    act.wait_ge(*at("M", "g_ps", b, n + 1))
                    if n >= 2:
                        act.wait_ge(*at("M", "act", b, n - 1))
                    nc.scalar.activation(sil[:, n % 2, :], bank(OT), ACT.Silu).then_inc(sem("M", "sil"), 1)
                    for _ in range(2 if n < 4 else 3):
                        yield
                for _ in range(NT + 2):
                    yield

            batch_loop(act, attention, local_layer, experts)

        @block.gpsimd
        def _(pool):
            nc.gpsimd.memset(m_half[:, :], -0.5).then_inc(sem("S", "stored"), 16)
            nc.gpsimd.memset(one[:, :], 1.0)
            nc.gpsimd.memset(xsT[:, 0:1], 0.0)
            for k in range(2):
                nc.gpsimd.memset(hT[k][:, 0:2], 0.0)
            nc.gpsimd.memset(stack_f[:, :, :, :, MSLOT:SLOT].rearrange("p t w h s -> p (t w h) s"), 0.0)
            nc.gpsimd.memset(vaug[:, :, :, :].rearrange("p t h s -> p (t h) s"), 0.0).then_inc(presets, 1)
            nc.gpsimd.memset(l_v[:, :, :, LD:LD + 1].rearrange("p t h s -> p (t h) s"), 1.0)
            pool.wait_ge(presets, 1)
            nc.gpsimd.memset(vaug[:, :, :, HD:HD + 1].rearrange("p t h s -> p (t h) s"), 1.0)
            nc.gpsimd.memset(stack_f[:, :, 1, :, MSLOT:MSLOT + 1], 1.0).then_inc(consts_ready, 1)
            pool.wait_ge(consts_ready, 3)

            def norm_root(b, s, k):
                pool.wait_ge(*at(s, "var", b, 1))
                nc.gpsimd.tensor_tensor(rstd[k][:, :], mv[k][:, :, 1], m_half[:, 0:NT], ALU.pow).then_inc(sem(s, "rstd"), 1)

            def attention(b, s):
                if s == "D":
                    norm_root(b, "N", 0)
                    for _ in range(4):
                        yield
                else:
                    yield
                for _ in range(NT + 3):
                    yield
                pool.wait_ge(*at(s, "stacked", b, 1))
                ones = one[:, :].rearrange("p (t h d) -> p t h d", t=1, h=1).broadcast_to([P, NT, H, HD])
                for side, to in ((0, 2 * HD), (1, HD)):
                    hi = stack_f[:, :, side, :, 0:HD]
                    last = nc.gpsimd.tensor_tensor(stack[:, :, side, :, to:to + HD], hi, ones, ALU.mult)
                last.then_inc(sem(s, "dup"), 1)
                yield
                for _ in range(8 + LEAD + UNITS + 1 + NG + 2 + 1):
                    yield
                if s != "D":
                    norm_root(b, s, 0)
                yield
                yield

            def local_layer(b, l):
                s = str(l)
                yield
                for u in range(3 * NT):
                    t, p = u // 3, u % 3
                    if p < 2:
                        w = 2 * t + p
                        pool.wait_ge(*at(s, "roped", b, w + 1))
                        half = l_c[:, t, p * LH:(p + 1) * LH, :]
                        nc.gpsimd.tensor_tensor(half, half, l_s[:, w % 2, :, :], ALU.add).then_inc(sem(s, "added"), 1)
                    else:
                        pool.wait_ge(*at(s, "ssum", b, t + 1))
                        nc.gpsimd.tensor_tensor(rn[:, t, :], ssum[:, t, :], m_half[:, 0:2 * LH], ALU.pow).then_inc(sem(s, "rn"), 1)
                        pool.wait_ge(*at(s, "rn", b, t + 1))
                        pool.wait_ge(*at(s, "added", b, 2 * t + 2))
                        nc.gpsimd.tensor_tensor(l_c[:, t, :, :], l_c[:, t, :, :],
                                                rn[:, t, :].rearrange("p (h a) -> p h a", a=1).broadcast_to([P, 2 * LH, LD]),
                                                ALU.mult).then_inc(sem(s, "nrm"), 1)
                    yield
                yield
                for _ in range(8 + 4 * LH + 2 + 4 + 1):
                    yield
                norm_root(b, s, 1)
                for _ in range(3 + 6 + 2):
                    yield
                if l == 1:
                    yield
                    norm_root(b, "B", 1)
                    yield
                yield

            def experts(b):
                norm_root(b, "M", 1)
                for _ in range(4 + 32 + 12 + NT):
                    yield
                yield
                norm_root(b, "F", 1)
                yield

            batch_loop(pool, attention, local_layer, experts)

        @block.vector
        def _(dve):
            dve.wait_ge(loaded, LOADS)
            nc.vector.tensor_copy(ident_h[:, :], ident[:, :])
            nc.vector.tensor_copy(pick_head[:, :], ident[0:LH, 0:LH])
            nc.vector.tensor_copy(mask_h[:, :], mask_f[:, :])
            for l in range(2):
                for cs in range(2):
                    for w in range(2):
                        last = nc.vector.tensor_tensor(tab[:, l, :, cs, w, :], xpos[:, :, cs, w, :],
                                                       l_scale[:, l, cs, w, :].rearrange("p (a d) -> p a d", a=1).broadcast_to([P, NT, LD]),
                                                       ALU.mult)
            last.then_inc(consts_ready, 2)
            dve.wait_ge(consts_ready, 3)

            class Steps:

                def __init__(self, b, s):
                    self.b, self.s, self.n = b, s, 0

                def settle(self, ins):
                    self.n += 1
                    ins.then_inc(sem(self.s, "step"), 1)
                    dve.wait_ge(*at(self.s, "step", self.b, self.n))

                def end(self):
                    assert self.n == STEPS[self.s], (self.s, self.n)

            def statistics(st, b, s, k, src, upper=None):
                for t in range(NT):
                    if upper is None:
                        last = nc.vector.bn_stats(stats[k][:, t, 0, :], src[:, t, :])
                    else:
                        nc.vector.bn_stats(stats[k][:, t, 0, :], src[:, t, 0:64])
                        last = nc.vector.bn_stats(stats[k][:, t, 1, :], upper[:, t * 64:(t + 1) * 64])
                st.settle(last)
                nc.vector.tensor_copy(held[:, :], ident[:, 0:1])
                for t in range(NT):
                    w = stats[k][:, t, 0, :] if upper is None else stats[k][:, t, :, :].rearrange("p a n -> p (a n)")
                    last = nc.vector.bn_aggr(mv[k][:, t, :], w)
                st.settle(last)
                nc.vector.tensor_scalar(mv[k][:, :, 1], mv[k][:, :, 1], EPS, None, ALU.add).then_inc(sem(s, "var"), 1)

            def normalise(b, s, k, dst, src):
                dve.wait_ge(*at(s, "rstd", b, 1))
                for t in range(NT):
                    last = nc.vector.tensor_scalar(dst[:, t, :], src[:, t, :], mv[k][:, t, 0:1], rstd[k][:, t:t + 1],
                                                   ALU.subtract, ALU.mult)
                return last

            def attention(b, s):
                st = Steps(b, s)
                if s == "D":
                    sn = Steps(b, "N")
                    statistics(sn, b, "N", 0, xc)
                    yield
                    normalise(b, "N", 0, hn[0], xc).then_inc(sem("N", "done"), 1)
                    yield
                    dve.wait_ge(*at("N", "xT_ps", b, 1))
                    sn.settle(nc.vector.tensor_scalar(hT[0][:, 2:L + 2], bank(0), ln1[:, 0:1], ln1[:, 1:2], ALU.mult, ALU.add))
                    yield
                    sn.settle(nc.vector.tensor_scalar(xT[:, :], hT[0][:, 0:L], conv[:, 0:1], None, ALU.mult))
                    sn.settle(nc.vector.scalar_tensor_tensor(xT[:, :], hT[0][:, 1:L + 1], conv[:, 1:2], xT[:, :], ALU.mult, ALU.add))
                    nc.vector.scalar_tensor_tensor(xT[:, :], hT[0][:, 2:L + 2], conv[:, 2:3], xT[:, :], ALU.mult,
                                                   ALU.add).then_inc(sem("D", "xT"), 1)
                    sn.end()
                    yield
                else:
                    yield
                for t in range(NT):
                    dve.wait_ge(*at(s, "qkv_ps", b, t + 1))
                    o = work[:, 0, t * 2 * C:(t + 1) * 2 * C]
                    v = ps[:, t, 2 * C:3 * C].rearrange("p (h d) -> p h d", d=HD)
                    if s == "A":
                        nc.vector.tensor_tensor(o, ps[:, t, 0:2 * C], bqkv[:, 0:2 * C], ALU.add)
                        last = nc.vector.tensor_tensor(vaug[:, t, :, 0:HD], v,
                                                       bqkv[:, 2 * C:3 * C].rearrange("p (h d) -> p h d", d=HD), ALU.add)
                    else:
                        nc.vector.tensor_copy(o, ps[:, t, 0:2 * C])
                        last = nc.vector.tensor_copy(vaug[:, t, :, 0:HD], v)
                    if t < NT - 1:
                        yield
                st.settle(last)
                yield
                src = qk
                if s in rope:
                    c = rope[s][:, :, 0:1, :].broadcast_to([P, NT, 2 * H, HD])
                    n = rope[s][:, :, 1:2, :].broadcast_to([P, NT, 2 * H, HD])
                    hf = HD // 2
                    nc.vector.tensor_tensor(qk_c, qk, c, ALU.mult)
                    nc.vector.tensor_tensor(qk_s[:, :, :, 0:hf], qk[:, :, :, hf:HD], n[:, :, :, 0:hf], ALU.mult)
                    st.settle(nc.vector.tensor_tensor(qk_s[:, :, :, hf:HD], qk[:, :, :, 0:hf], n[:, :, :, hf:HD], ALU.mult))
                yield
                if s in rope:
                    st.settle(nc.vector.tensor_tensor(qk_c, qk_c, qk_s, ALU.add))
                    src = qk_c
                yield
                sv = stack[:, :, :, :, :].rearrange("p t w h s -> p (t w h) s")
                st.settle(nc.vector.tensor_copy(sv[:, :, 0:HD], src.rearrange("p t h d -> p (t h) d")))
                yield
                nc.vector.tensor_tensor(stack[:, :, 0, :, HD:2 * HD], src[:, :, 0:H, :], stack_f[:, :, 0, :, 0:HD], ALU.subtract)
                nc.vector.tensor_tensor(stack[:, :, 1, :, 2 * HD:3 * HD], src[:, :, H:2 * H, :], stack_f[:, :, 1, :, 0:HD],
                                        ALU.subtract).then_inc(sem(s, "stacked"), 1)
                yield
                for _ in range(8):
                    yield

                def maximum(n):
                    h, i = n // NT, n % NT
                    dve.wait_ge(*at(s, "sc_ps", b, n + 1))
                    N = L if s == "C" else (i + 1) * P
                    nc.vector.tensor_reduce(stack[:, i, 0, h, MSLOT:MSLOT + 1], ps[:, SC + n % 2, 0:N], X, ALU.max,
                                            negate=True).then_inc(sem(s, "mx"), 1)

                for n in range(LEAD):
                    maximum(n)
                    yield
                for n in range(UNITS):
                    if n + LEAD < UNITS:
                        maximum(n + LEAD)
                    yield
                yield
                for g in range(NG):
                    dve.wait_ge(*at(s, "ot_ps", b, g + 1))
                    o = bank(g).rearrange("p (t h e) -> p t h e", t=NT, e=SLOT)
                    rd = rden[:, g, :, :].rearrange("p t (h a) -> p t h a", a=1)
                    st.settle(nc.vector.reciprocal(rd, o[:, :, :, HD:HD + 1]))
                    nc.vector.tensor_tensor(heads[:, :, g * HG * HD:(g + 1) * HG * HD].rearrange("p t (h d) -> p t h d", d=HD),
                                            o[:, :, :, 0:HD], rd.broadcast_to([P, NT, HG, HD]),
                                            ALU.mult).then_inc(sem(s, "ctx"), 1)
                    yield
                yield
                if s == "A":
                    nc.vector.tensor_tensor(xa[:, :, :], xin[:, :, :], tiled(bout[:, :]), ALU.add).then_inc(sem("A", "used"), 1)
                    dve.wait_ge(*at("A", "used", b, 1))
                yield
                dve.wait_ge(*at(s, "o_ps", b, 1))
                if s == "A":
                    nc.vector.tensor_tensor(xa[:, :, :], four(0), xa[:, :, :], ALU.add).then_inc(sem(s, "res"), 1)
                    x = xa
                elif s == "C":
                    nc.vector.scalar_tensor_tensor(xc[:, :, :], xb[:, :, :], 2.0, four(0), ALU.mult, ALU.add).then_inc(sem(s, "res"), 1)
                    x = xc
                else:
                    nc.vector.tensor_tensor(yd[:, :, :], four(0), xc[:, :, :], ALU.add).then_inc(sem("D", "res"), 1)
                yield
                if s != "D":
                    dve.wait_ge(*at(s, "res", b, 1))
                    statistics(st, b, s, 0, x)
                yield
                if s != "D":
                    normalise(b, s, 0, x, x).then_inc(sem(s, "done"), 1)
                    dve.wait_ge(*at(s, "done", b, 1))
                st.end()
                yield

            def tiled(v):
                return v.rearrange("p (a c) -> p a c", a=1).broadcast_to([P, NT, C])

            def local_layer(b, l):
                s = str(l)
                st = Steps(b, s)
                hf = LD // 2
                yield
                for u in range(3 * NT):
                    t, p = u // 3, u % 3
                    if p < 2:
                        w = 2 * t + p
                        dve.wait_ge(*at(s, "sq", b, w + 1))
                        z = bank(OT + p).rearrange("p (h d) -> p h d", d=LD)
                        c = tab[:, l, t, 0, p, :].rearrange("p (a d) -> p a d", a=1).broadcast_to([P, LH, LD])
                        n = tab[:, l, t, 1, p, :].rearrange("p (a d) -> p a d", a=1).broadcast_to([P, LH, LD])
                        if w >= 2:
                            dve.wait_ge(*at(s, "added", b, w - 1))
                        nc.vector.tensor_tensor(l_c[:, t, p * LH:(p + 1) * LH, :], z, c, ALU.mult)
                        nc.vector.tensor_tensor(l_s[:, w % 2, :, 0:hf], z[:, :, hf:LD], n[:, :, 0:hf], ALU.mult)
                        nc.vector.tensor_tensor(l_s[:, w % 2, :, hf:LD], z[:, :, 0:hf], n[:, :, hf:LD], ALU.mult)
                        nc.vector.tensor_reduce(ssum[:, t, p * LH:(p + 1) * LH], sq[:, w % 2, :].rearrange("p (h d) -> p h d", d=LD),
                                                X, ALU.add).then_inc(sem(s, "roped"), 1)
                    else:
                        dve.wait_ge(*at(s, "roped", b, 2 * t + 2))
                        nc.vector.tensor_scalar(ssum[:, t, :], ssum[:, t, :], 1e-24, None, ALU.max).then_inc(sem(s, "ssum"), 1)
                    yield
                yield
                for _ in range(8):
                    yield
                for m in range(2 * LH):
                    h, a = m // 2, m % 2
                    dve.wait_ge(*at(s, "sc_ps", b, m + 1))
                    nc.vector.tensor_reduce(nm[:, 2 * a:2 * a + 2, h], ps[:, OT + m % 3, 0:2 * BAND].rearrange("p (c n) -> p c n", c=2),
                                            X, ALU.max, negate=True).then_inc(sem(s, "mx"), 1)
                    yield
                yield

                def divided(h):
                    dve.wait_ge(*at(s, "pv", b, h + 1))
                    o = ps[:, OT + 2, 0:NT * (LD + 1)].rearrange("p (t e) -> p t e", t=NT)
                    rd = l_rd[:, h % 2, :].rearrange("p (t a) -> p t a", a=1)
                    st.settle(nc.vector.reciprocal(rd, o[:, :, LD:LD + 1]))
                    nc.vector.tensor_tensor(l_o[:, :, h * LD:(h + 1) * LD], o[:, :, 0:LD], rd.broadcast_to([P, NT, LD]),
                                            ALU.mult).then_inc(sem(s, "o"), 1)

                for m in range(2 * LH):
                    if m % 2 and m >= 3:
                        divided(m // 2 - 1)
                    yield
                divided(LH - 1)
                yield
                for _ in range(4):
                    yield
                dve.wait_ge(*at(s, "o_ps", b, 1))
                nc.vector.tensor_tensor(l_m[:, :, :], four(OT + 2), (xa if l == 0 else l_x)[:, :, :], ALU.add).then_inc(sem(s, "lm"), 1)
                yield
                dve.wait_ge(*at(s, "sh_ps", b, 1))
                statistics(st, b, s, 1, l_m, upper=bank(OT))
                yield
                dve.wait_ge(*at(s, "rstd", b, 1))
                for t in range(NT):
                    nc.vector.tensor_scalar(hn[1][:, t, 0:64], l_m[:, t, 0:64], mv[1][:, t, 0:1], rstd[1][:, t:t + 1],
                                            ALU.subtract, ALU.mult)
                    last = nc.vector.tensor_scalar(hn[1][:, t, 64:128], ps[:, OT, t * 64:(t + 1) * 64], mv[1][:, t, 0:1],
                                                   rstd[1][:, t:t + 1], ALU.subtract, ALU.mult)
                last.then_inc(sem(s, "hn"), 1)
                dst = l_x if l == 0 else xb
                st.settle(nc.vector.tensor_tensor(dst[:, :, :], l_m[:, :, :], tiled(lb_2[:, l, :]), ALU.add))
                yield
                dve.wait_ge(*at(s, "hT_ps", b, 1))
                nc.vector.tensor_scalar(hT[1][:, 2:L + 2], bank(OT + 1), l_gb[:, l, 0:1], l_gb[:, l, 1:2], ALU.mult,
                                        ALU.add).then_inc(sem(s, "hT"), 1)
                yield
                for u in range(6):
                    if u % 2:
                        j = u // 2
                        n = HB[j]
                        dve.wait_ge(*at(s, "g_ps", b, u + 1))
                        dve.wait_ge(*at(s, "gel", b, j + 1))
                        nc.vector.scalar_tensor_tensor(hidT[0:n, j, :], ps[0:n, OT + u % 3, :], lb_1[0:n, l, 0, j:j + 1],
                                                       gel[0:n, j, :], ALU.add, ALU.mult).then_inc(sem(s, "hid"), 1)
                    yield
                yield
                dve.wait_ge(*at(s, "f_ps", b, 1))
                nc.vector.tensor_tensor(dst[:, :, :], four(OT + 1), dst[:, :, :], ALU.add).then_inc(sem(s, "out"), 1)
                dve.wait_ge(*at(s, "out", b, 1))
                st.end()
                if l == 1:
                    st = Steps(b, "B")
                    yield
                    st.settle(nc.vector.tensor_tensor(xb[:, :, :], xa[:, :, :], xb[:, :, :], ALU.add))
                    statistics(st, b, "B", 1, xb)
                    yield
                    normalise(b, "B", 1, xb, xb).then_inc(sem("B", "done"), 1)
                    dve.wait_ge(*at("B", "done", b, 1))
                    st.end()
                yield

            def experts(b):
                st = Steps(b, "M")
                dve.wait_ge(*at("D", "res", b, 1))
                statistics(st, b, "M", 1, yd)
                yield
                normalise(b, "M", 1, hn[1], yd).then_inc(sem("M", "hn"), 1)
                nc.vector.tensor_tensor(xd[:, :, :], xc[:, :, :], yd[:, :, :], ALU.add)
                yield
                dve.wait_ge(*at("M", "hT_ps", b, 1))
                nc.vector.tensor_scalar(hT[1][:, 2:L + 2], bank(OT), ln2[:, 0:1], ln2[:, 1:2], ALU.mult, ALU.add).then_inc(sem("M", "hT"), 1)
                yield
                dve.wait_ge(*at("M", "lg_ps", b, 1))
                nc.vector.tensor_copy(lg[:, :, :], ps[:, OT + 1, 0:NT * NE].rearrange("p (t e) -> p t e", e=NE)).then_inc(sem("M", "lg"), 1)
                dve.wait_ge(*at("M", "lg", b, 1))
                st.settle(nc.vector.tensor_reduce(lmax[:, :], lg[:, :, :], X, ALU.max))
                for e in range(NE):
                    st.settle(nc.vector.tensor_tensor(pick[:, :, e], lg[:, :, e], lmax[:, :], ALU.is_ge))
                    if e == 0:
                        st.settle(nc.vector.tensor_scalar(free[:, :], pick[:, :, 0], -1.0, 1.0, ALU.mult, ALU.add))
                    else:
                        st.settle(nc.vector.tensor_tensor(pick[:, :, e], pick[:, :, e], free[:, :], ALU.mult))
                        st.settle(nc.vector.tensor_tensor(free[:, :], free[:, :], pick[:, :, e], ALU.subtract))
                yield

                def gather(e):
                    dve.wait_ge(*at("M", "e_ps", b, e + 1))
                    if e >= 1:
                        dve.wait_ge(*at("M", "acc", b, e))
                    for t in range(NT):
                        last = nc.vector.scalar_tensor_tensor(xd[:, t, :], ps[:, OT + 2, t * P:(t + 1) * P], pick[:, t, e:e + 1],
                                                              xd[:, t, :], ALU.mult, ALU.add)
                    last.then_inc(sem("M", "acc"), 1)

                for n in range(16):
                    e, j = n // 4, n % 4
                    yield
                    dve.wait_ge(*at("M", "v_ps", b, n + 1))
                    dve.wait_ge(*at("M", "sil", b, n + 1))
                    if j == 0 and e >= 2:
                        dve.wait_ge(*at("M", "e_ps", b, e - 1))
                    nc.vector.tensor_tensor(eact[:, e % 2, j, :], bank(OT + 1), sil[:, n % 2, :],
                                            ALU.mult).then_inc(sem("M", "act"), 1)
                    yield
                    if e >= 1:
                        if j == 3:
                            gather(e - 1)
                        yield
                for t in range(NT - 1):
                    yield
                gather(NE - 1)
                yield
                dve.wait_ge(*at("M", "acc", b, NE))
                st.end()
                st = Steps(b, "F")
                statistics(st, b, "F", 1, xd)
                yield
                dve.wait_ge(*at("S", "stored", b, 16))
                normalise(b, "F", 1, yo, xd).then_inc(sem("S", "y"), 1)
                st.end()
                yield

            batch_loop(dve, attention, local_layer, experts)


STEPS = {"A": 10, "0": 11, "1": 11, "B": 3, "C": 8, "N": 5, "D": 8, "M": 14, "F": 2}
UNITS = H * NT
LEAD = 20
_ATT = 1 + NT + 4 + 8 + LEAD + UNITS + 1 + NG + 2 + 3
_LOC = 1 + 3 * NT + 1 + 8 + 4 * LH + 2 + 4 + 1 + 3 + 6 + 2
SEGS = {"A": _ATT, "C": _ATT, "D": _ATT + 3, "0": _LOC, "1": _LOC + 2, "M": 4 + 32 + 12 + NT + 2}

_OUTS = [((B, L, C), "float32")]


def constants():
    import numpy as np
    f = np.float32
    ar = np.arange
    i = ar(P)
    masks = np.zeros((P, 2 * P + 3 * BAND), f)
    masks[:, 0:P] = np.where(i[None, :] > i[:, None], NEG, 0)
    masks[:, P:2 * P] = np.where(i[:, None] > i[None, :], NEG, 0)
    k = ar(BAND)[None, :] - WIN
    q = i[:, None]
    ok = (k <= q) & (k >= q - WIN)
    masks[:, 2 * P:2 * P + BAND] = np.where(ok, 0, NEG)
    masks[:, 2 * P + BAND:2 * P + 2 * BAND] = np.where(ok & (k >= 0), 0, NEG)
    kk, qq = i[:, None], ar(BAND)[None, :]
    masks[:, 2 * P + 2 * BAND:] = np.where((qq >= kk) & (qq <= kk + WIN), 0, NEG)
    shift = np.zeros((P, 2, P), f)
    shift[i[:-1], 0, i[1:]] = 1
    shift[P - 1, 1, 0] = 1
    pos = ar(L).astype(f)

    def tiles(a):
        return np.ascontiguousarray(a.reshape((NT, P) + a.shape[1:]).swapaxes(0, 1).astype(f))

    def rope(angle):
        c, s = np.cos(angle).astype(f), np.sin(angle).astype(f)
        return tiles(np.stack([np.concatenate([c, c], -1), np.concatenate([-s, s], -1)], 1))

    frac = (2 * ar(HD // 2) / HD).astype(f)
    a_A = (pos[:, None] / np.power(f(1250), frac)[None, :]).astype(f)
    a_D = (pos[:, None] * (f(1) / np.power(f(10000), (ar(0, HD, 2).astype(f) / f(HD))))[None, :]).astype(f)
    half = ar(0, LD, 2).astype(f)
    inv = (f(1) / np.power(f(10000), half / f(LD))).astype(f)
    fr = (pos[:, None] * inv[None, :]).astype(f)
    base = ((half + f(0.4 * LD)) / f(1.4 * LD)).astype(f)
    power = ((pos - L // 2) / f(WIN // 2)).astype(f)
    sc = np.power(base[None, :], power[:, None]).astype(f)
    c, s = np.cos(fr).astype(f), np.sin(fr).astype(f)
    cc, ss, sc2 = np.concatenate([c, c], -1), np.concatenate([-s, s], -1), np.concatenate([sc, sc], -1)
    xpos = np.stack([np.stack([cc * sc2, cc / sc2], 1), np.stack([ss * sc2, ss / sc2], 1)], 1)
    return {"ident": np.eye(P, dtype=f), "masks": masks, "shift": shift,
            "rope_A": rope(a_A), "rope_D": rope(a_D), "xpos": tiles(xpos)}


def kernel(**inputs):
    import numpy as _np
    import concourse.bacc as _bacc
    from concourse import mybir as _mybir
    from concourse.bass_utils import run_bass_kernel_spmd as _run

    nc = _bacc.Bacc("TRN2", target_bir_lowering=False, num_devices=1,
                     dynamic_dma_scratch_size=1024)
    arrays, ins, consts = {}, {}, {}
    for name, a in inputs.items():
        if name == "L1_attn_mask":
            continue
        a = _np.ascontiguousarray(a)
        arrays[f"in_{name}_dram"] = a
        ins[name] = nc.dram_tensor(f"in_{name}_dram", a.shape, _mybir.dt.from_np(a.dtype), kind="ExternalInput").ap()
    for name, a in constants().items():
        arrays[f"const_{name}_dram"] = a
        consts[name] = nc.dram_tensor(f"const_{name}_dram", a.shape, _mybir.dt.from_np(a.dtype), kind="ExternalInput").ap()
    shape, dtype = _OUTS[0]
    out = nc.dram_tensor("out_0_dram", shape, _mybir.dt.from_np(_np.dtype(dtype)), kind="ExternalOutput").ap()
    network_kernel(nc, ins, consts, out)
    r = _run(nc, [arrays], core_ids=[0])
    return r.results[0]["out_0_dram"]
```

```python
import concourse.bass as bass
from concourse import mybir
from contextlib import ExitStack

B, L, C = 8, 512, 128
P = 128
NT = L // P
H, HD = 16, 8
HG = 4
NG = H // HG
SLOT = 32
MSLOT = 3 * HD
LH, LD, WIN = 8, 64, 64
BAND = P + WIN
HID = 341
HB = [128, 128, HID - 256]
NE, FF = 4, 512
EPS = 1e-5
NEG = -1.0e30
STEPS = {"A": 10, "0": 11, "1": 11, "B": 3, "C": 8, "N": 4, "D": 8, "M": 14, "F": 2}
UNITS = H * NT
LEAD = 22
_UNITS = ([4.61] + [1] * (NT - 1) + [4, 3, 2, 2] + [1] * 8 + [1.4] * (LEAD // 2) + [1.3, 1.33] * (UNITS // 2)
          + [1.5] * (1 + NG) + [2, 1.74, 2, 4, 2])
_LOCAL = ([2] + [1.2] * 6 * NT + [3] + [1] * 8 + [1.2] * 2 * LH + [2] + [1.6] * 2 * LH + [2]
          + [1] * 4 + [3, 2.62, 4.75, 4] + [1] * 6 + [1.5, 3])
SEGS = {"A": [1] + _UNITS, "C": [0.81] + _UNITS, "D": [4, 4.28, 1.86, 3] + _UNITS, "0": _LOCAL, "1": _LOCAL + [5, 2],
        "M": [5, 3, 1.11, 6.54] + [1] * 20, "E": [1] * 24 + [0.98] * NT + [4.14, 1.67]}
SPANS = {"C": (0, 0.356), "D": (0.356, 0.727), "A": (0.727, 1), "E": (0, 0.135), "0": (0.135, 0.489), "1": (0.489, 0.863),
         "M": (0.863, 1)}


def network_kernel(nc: bass.Bass, ins, consts, out: bass.AP):
    fp32, fp32r, bf16 = mybir.dt.float32, mybir.dt.float32r, mybir.dt.bfloat16
    ALU = mybir.AluOpType
    ACT = mybir.ActivationFunctionType
    X = mybir.AxisListType.X

    ctx = ExitStack()
    with ctx:
        def sb(name, shape, dt=fp32):
            return ctx.enter_context(nc.sbuf_tensor(name, shape, dt))

        class Signal:

            def __init__(self, name, per_batch):
                self.sem, self.per = ctx.enter_context(nc.semaphore(name)), per_batch

            def at(self, b, n):
                return b * self.per + n

        ident = sb("ident", [P, P])
        ident_h = sb("ident_h", [P, P], bf16)
        shift = sb("shift", [P, 2, P])
        mask_h = sb("mask_h", [P, 2 * P + 3 * BAND], bf16)
        causal_qk = mask_h[:, 0:P]
        causal_kq = mask_h[:, P:2 * P]
        band_qk = mask_h[:, 2 * P:2 * P + BAND]
        band_q0 = mask_h[:, 2 * P + BAND:2 * P + 2 * BAND]
        band_kq = mask_h[:, 2 * P + 2 * BAND:2 * P + 3 * BAND]
        pick_head = sb("pick_head", [LH, LH], fp32r)
        rope = {s: sb(f"rope_{s}", [P, NT, 2, HD]) for s in "AD"}
        wqkv = {s: sb(f"wqkv_{s}", [P, 3 * C]) for s in "ACD"}
        wout = {s: sb(f"wout_{s}", [P, C]) for s in "ACD"}
        bqkv = sb("bqkv", [P, 3 * C])
        bout = sb("bout", [P, C])
        lw_qkv = sb("lw_qkv", [P, 2, 3 * LH * LD])
        lw_o = sb("lw_o", [P, 2, 4, C])
        lw_1 = sb("lw_1", [P, 2, 2 * HID])
        lw_2 = sb("lw_2", [P, 2, 3, C])
        lb_1 = sb("lb_1", [P, 2, 2, 3])
        lb_2 = sb("lb_2", [P, 2, C])
        l_gb = sb("l_gb", [P, 2, 2])
        l_scale = sb("l_scale", [P, 2, 2, 2, LD])
        tab = sb("tab", [P, 2, NT, 2, 2, LD])
        ln1 = sb("ln1", [P, 2])
        ln2 = sb("ln2", [P, 2])
        conv = sb("conv", [P, 3])
        router = sb("router", [P, NE])
        e_wv = sb("e_wv", [P, NE, 2 * FF])
        e_pr = sb("e_pr", [P, NE, FF // P, C])
        one = sb("one", [P, 1])
        m_half = sb("m_half", [P, 2 * LH])

        xin = sb("xin", [P, NT, C])
        xa = sb("xa", [P, NT, C])
        xb = sb("xb", [P, NT, C])
        xc = sb("xc", [P, NT, C])
        yd = sb("yd", [P, NT, C])
        yo = sb("yo", [P, NT, C])
        l_x = sb("l_x", [P, NT, C])
        l_m = sb("l_m", [P, NT, C])
        hn = [sb(f"hn{k}", [P, NT, C]) for k in range(2)]
        hT = [sb(f"hT{k}", [P, L + 2]) for k in range(2)]
        stats = [sb(f"stats{k}", [P, NT, 2, 6]) for k in range(2)]
        mv = [sb(f"mv{k}", [P, NT, 2]) for k in range(2)]
        rstd = [sb(f"rstd{k}", [P, NT]) for k in range(2)]
        held = sb("held", [P, 1])
        xT = sb("xT", [P, L])
        stack = sb("stack", [P, NT, 2, H, SLOT], fp32r)
        vaug = sb("vaug", [P, NT, H, SLOT])
        with ExitStack() as shared:
            def over(name, shape, dt=fp32):
                return shared.enter_context(nc.sbuf_tensor(name, shape, dt))

            xpos = over("xpos", [P, NT, 2, 2, LD])
            mask_f = over("mask_f", [P, 2 * P + 3 * BAND])
        KT = sb("KT", [P, NG, L], fp32r)
        QT = sb("QT", [P, NG, L], fp32r)
        QM = sb("QM", [P, 2, L], fp32r)
        prob = sb("prob", [P, 4, L])
        work = sb("work", [P, 3, NT * 2 * C])
        qk, qk_c, qk_s = (work[:, k, :].rearrange("p (t h d) -> p t h d", t=NT, d=HD) for k in range(3))
        oT = work[:, 0:2, :].rearrange("p a n -> p (a n)").rearrange("p (g n) -> p g n", g=NG)
        heads = work[:, 2, 0:NT * C].rearrange("p (t c) -> p t c", t=NT)
        headsT = work[:, 2, NT * C:2 * NT * C]
        rden = sb("rden", [P, NG, NT, HG])
        xsT = sb("xsT", [P, L])
        l_v = sb("l_v", [P, NT, LH, LD + 1])
        with ExitStack() as shared:
            sq = over("sq", [P, 2, LH * LD])
            l_c = over("l_c", [P, NT, 2 * LH, LD])
            l_s = over("l_s", [P, 2, LH, LD])
            ssum = over("ssum", [P, NT, 2 * LH])
            rn = over("rn", [P, NT, 2 * LH])
            l_T = over("l_T", [P, 8, L])
            nm = over("nm", [P, NT, LH])
            nmT = over("nmT", [LH, L], fp32r)
            l_p = over("l_p", [P, 4, 2 * BAND])
            l_rd = over("l_rd", [P, 2, NT])
            l_o = l_c[:, 0:2, :, :].rearrange("p a h d -> p (a h d)").rearrange("p (t n) -> p t n", t=NT)
            l_oT, hidT, gel = l_T[:, 0:4], l_T[:, 0:3], l_T[:, 4:7]
        with ExitStack() as shared:
            sil = over("sil", [P, 2, L])
            eact = over("eact", [P, 2, FF // P, L])
            lg = over("lg", [P, NT, NE])
            lmax = over("lmax", [P, NT])
            free = over("free", [P, NT])
            pick = over("pick", [P, NT, NE])

        ps = ctx.enter_context(nc.psum_tensor("ps", [P, 8, 512], fp32))

        def bank(i):
            return ps[:, i, :]

        def four(i):
            return ps[:, i, :].rearrange("p (t c) -> p t c", t=NT)

        SC, SK, PV, OT = 0, 2, 4, 5
        stack_f = stack[:, :, :, :, :].bitcast(fp32)

        loaded_first = ctx.enter_context(nc.semaphore("first_weights_loaded"))
        loaded = ctx.enter_context(nc.semaphore("other_weights_loaded"))
        consts_ready = ctx.enter_context(nc.semaphore("consts_ready"))
        presets = ctx.enter_context(nc.semaphore("presets"))
        S = {}

        class Part:
            def __init__(self, whole, offset):
                self.sem, self.whole, self.offset = whole.sem, whole, offset

        def signals(stages, **per):
            for k, n in per.items():
                each = [n] * len(stages) if isinstance(n, int) else n
                whole = Signal(f"{k}_{stages}", sum(each))
                for i, s in enumerate(stages):
                    S[s, k] = Part(whole, sum(each[:i]))

        def sem(s, what):
            return S[s, what].sem

        def at(s, what, b, n):
            p = S[s, what]
            return p.sem, p.whole.at(b, p.offset + n)

        for stages in ("A", "CD"):
            signals(stages, xT=1, qkv_ps=NT, stacked=1, dup=1, kq_ps=8, kq=8, sc_ps=UNITS, mx=UNITS,
                    keys_ps=UNITS + NG, keys_out=UNITS + NG, pv=UNITS, ev=NG, ot_ps=NG, ctx=NG, cT_ps=1, cT=1,
                    o_ps=1, res=1)
        signals("A", xT_ps=1, used=1)
        signals("CN", xT_ps=1)
        signals("N", hT=1)
        signals("L", x=16)
        signals("S", y=1, stored=16)
        signals("01", xT_ps=1, xT=1, qkv_ps=3 * NT, sq=2 * NT, v=NT, roped=2 * NT, added=2 * NT, ssum=NT, rn=NT,
                nrm=NT, T_ps=8, T=8, sc_ps=2 * LH, mx=2 * LH, nm_ps=1, nmT=1, st_ps=2 * LH, ex=2 * LH, pv=LH, o=LH,
                oT_ps=4, oT=4, o_ps=1, lm=1, sh_ps=1, g_ps=6, gel=3, hid=3, f_ps=1, out=1)
        signals("01", hn=1, hT_ps=1, hT=1)
        signals("M", hn=1, hT_ps=1, hT=1)
        signals("M", lg_ps=1, lg=1, g_ps=16, v_ps=16, sil=16, act=16, e_ps=NE, acc=NE)
        signals("A", var=1, rstd=1, done=1)
        signals("01B", var=1, rstd=1)
        signals("B", done=1)
        signals("CND", var=[1, 1, 0], rstd=[1, 1, 0], done=[1, 1, 0])
        signals("MF", var=1, rstd=1)
        signals("A", step=STEPS["A"])
        signals("01B", step=[STEPS["0"], STEPS["1"], STEPS["B"]])
        signals("CND", step=[STEPS["C"], STEPS["N"], STEPS["D"]])
        signals("MF", step=[STEPS["M"], STEPS["F"]])

        block = ctx.enter_context(nc.Block())

        def first(s, j):
            return j * P if s in "AD" else 0

        def unit(n):
            return n // 16 * HG + n % HG, n % 16 // HG, n // 16

        def use(n):
            return n + min(NG, 1 + (n + 2) // 16)

        def turn(g):
            return 0 if g == 0 else use(16 * g - 2) - 1

        def side_by_side(*stages):
            order = []
            for i, (_, name, begin, end) in enumerate(stages):
                w, done = SEGS[name], 0
                for k, share in enumerate(w):
                    order.append((begin + (end - begin) * (done + share / 2) / sum(w), i, k))
                    done += share
            for _, i, _ in sorted(order):
                next(stages[i][0])
            for g, *_ in stages:
                assert next(g, None) is None

        def batch_loop(eng, att, loc, exp):
            def stages(runs):
                side_by_side(*((g, name, *SPANS[name]) for g, name in runs))

            def last_attentions(b):
                return [(att(b, "C"), "C"), (att(b, "D"), "D")]

            def local(b):
                return [(loc(b, 0), "0"), (loc(b, 1), "1")]

            side_by_side((att(0, "A"), "A", 0, 1))
            eng.wait_ge(loaded, 16 * n_loads["rest"])
            side_by_side((att(1, "A"), "A", 0, 2), (loc(0, 0), "0", 0, 0.95), (loc(0, 1), "1", 0.95, 1.9))
            stages(last_attentions(0) + local(1) + [(att(2, "A"), "A"), (exp(0, 0), "M")])
            with eng.Fori(1, B - 2) as b:
                stages([(exp(b - 1, 1), "E")] + last_attentions(b) + local(b + 1)
                       + [(att(b + 2, "A"), "A"), (exp(b, 0), "M")])
            stages([(exp(B - 3, 1), "E")] + last_attentions(B - 2) + local(B - 1) + [(exp(B - 2, 0), "M")])
            stages([(exp(B - 2, 1), "E")] + last_attentions(B - 1) + [(exp(B - 1, 0), "M")])
            side_by_side((exp(B - 1, 1), "E", 0, 1))

        n_loads = {"first": 0, "rest": 0}

        @block.sync
        def _(sp):
            def load_first(dst, src):
                sp.dma_start(dst, src).then_inc(loaded_first, 16)
                n_loads["first"] += 1

            def load(dst, src):
                sp.dma_start(dst, src).then_inc(loaded, 16)
                n_loads["rest"] += 1

            def row(ap):
                n = ap.shape[0]
                return ap.rearrange("(a n) -> a n", a=1).broadcast_to([P, n])

            def x_of(b):
                return b.rearrange("o (t p) c -> p (o t) c", p=P)

            def load_x(b):
                sp.dma_start(xin[:, :, :], x_of(ins["L0_attn_x"][bass.ds(b, 1)])).then_inc(sem("L", "x"), 16)

            def store(b):
                sp.wait_ge(*at("S", "y", b, 1))
                sp.dma_start(x_of(out[bass.ds(b, 1)]), yo[:, :, :]).then_inc(sem("S", "stored"), 16)

            load_first(ident[:, :], consts["ident"])
            load_first(mask_f[:, :], consts["masks"])
            load_first(xpos[:, :, :, :, :], consts["xpos"])
            for l in range(2):
                for i, n in enumerate(("q", "k")):
                    v = ins[f"L0_ffn_{n}_scale"][l]
                    load_first(l_scale[:, l, 0, i, :], row(v))
                    load_first(l_scale[:, l, 1, i, 0:LD // 2], row(v[LD // 2:LD]))
                    load_first(l_scale[:, l, 1, i, LD // 2:LD], row(v[0:LD // 2]))
            for i, n in enumerate(("wq", "wk", "wv")):
                load_first(wqkv["A"][:, i * C:(i + 1) * C], ins[f"L0_attn_{n}_w"])
                load_first(bqkv[:, i * C:(i + 1) * C], row(ins[f"L0_attn_{n}_b"]))
            load_first(rope["A"][:, :, :, :], consts["rope_A"])
            load_first(wout["A"][:, :], ins["L0_attn_wo_w"])
            load_first(bout[:, :], row(ins["L0_attn_wo_b"]))
            load_x(0)
            load(shift[:, :, :], consts["shift"])
            load(rope["D"][:, :, :, :], consts["rope_D"])
            for i, n in enumerate(("Wq", "Wk", "Wv")):
                load(wqkv["C"][:, i * C:(i + 1) * C], ins[f"L1_attn_{n}"])
            load(wout["C"][:, :], ins["L1_attn_Wout"])
            load(wqkv["D"][:, :], ins["L1_ffn_attn_w"])
            load(wout["D"][:, :], ins["L1_ffn_proj_w"])
            load(lw_qkv[:, :, :], ins["L0_ffn_wqkv"].rearrange("l c n -> c l n"))
            for l in range(2):
                load(lw_o[:, l], ins["L0_ffn_wo"][l].rearrange("(k c) n -> c k n", c=P))
                load(lw_2[:, l, 0:2], ins["L0_ffn_w2"][l, 0:256].rearrange("(k c) n -> c k n", c=P))
                load(lw_2[0:HB[2], l, 2], ins["L0_ffn_w2"][l, 256:HID])
                load(lb_2[:, l], row(ins["L0_ffn_b2"][l]))
                for half in range(2):
                    for j, n in enumerate(HB):
                        c0 = half * HID + j * P
                        load(lb_1[0:n, l, half, j:j + 1], ins["L0_ffn_b1"][l, c0:c0 + n].rearrange("(c a) -> c a", a=1))
                load(l_gb[:, l, 0:1], ins["L0_ffn_ln_g"][l].rearrange("(c a) -> c a", a=1))
                load(l_gb[:, l, 1:2], ins["L0_ffn_ln_b"][l].rearrange("(c a) -> c a", a=1))
            load(lw_1[:, :, :], ins["L0_ffn_w1"].rearrange("l c n -> c l n"))
            for t, n in ((ln1, "ln1"), (ln2, "ln2")):
                load(t[:, 0:1], ins[f"L1_ffn_{n}_w"].rearrange("(c a) -> c a", a=1))
                load(t[:, 1:2], ins[f"L1_ffn_{n}_b"].rearrange("(c a) -> c a", a=1))
            load(conv[:, :], ins["L1_ffn_conv_w"].rearrange("c a k -> c (a k)"))
            load(router[:, :], ins["L1_ffn_router_w"])
            load(e_wv[:, :, :], ins["L1_ffn_expert_wv"].rearrange("e c n -> c e n"))
            for e in range(NE):
                load(e_pr[:, e], ins["L1_ffn_expert_proj"][e].rearrange("(k c) n -> c k n", c=P))

            for b in range(2):
                sp.wait_ge(*at("A", "used", b, 1))
                load_x(b + 1)
            with sp.Fori(2, B - 1) as b:
                sp.wait_ge(*at("A", "used", b, 1))
                load_x(b + 1)
                store(b - 2)
            for b in range(B - 3, B):
                store(b)
            sp.wait_ge(*at("S", "stored", B, 16))

        @block.tensor
        def _(pe):
            pe.wait_ge(loaded_first, 16 * n_loads["first"])
            pe.wait_ge(consts_ready, 3)

            def transpose4(src, dst):
                for t in range(NT):
                    last = nc.tensor.transpose(dst[:, t * P:(t + 1) * P], src[:, t, :], ident[:, :])
                return last

            def attention(b, s):
                causal = s != "C"
                if s == "A":
                    pe.wait_ge(*at("L", "x", b, 16))
                    transpose4(xin, bank(0)).then_inc(sem("A", "xT_ps"), 1)
                    yield
                elif s == "C":
                    pe.wait_ge(*at("B", "done", b, 1))
                    transpose4(xb, bank(0)).then_inc(sem("C", "xT_ps"), 1)
                    yield
                else:
                    yield
                    yield
                    pe.wait_ge(*at("N", "done", b, 1))
                    transpose4(hn[0], bank(0)).then_inc(sem("N", "xT_ps"), 1)
                    yield
                    yield
                for t in range(NT):
                    if t == 0:
                        pe.wait_ge(*at(s, "xT", b, 1))
                    nc.tensor.matmul(ps[:, t, 0:3 * C], xT[:, t * P:(t + 1) * P], wqkv[s][:, :],
                                     start=True, stop=True).then_inc(sem(s, "qkv_ps"), 1)
                    yield
                for _ in range(4):
                    yield
                for n in range(8):
                    g, which = n // 2, 1 - n % 2
                    if n == 0:
                        pe.wait_ge(*at(s, "stacked", b, 1))
                        pe.wait_ge(*at(s, "dup", b, 1))
                    if n >= 4:
                        pe.wait_ge(*at(s, "kq", b, n - 3))
                    for t in range(NT):
                        last = nc.tensor.transpose(ps[:, n % 4, t * P:(t + 1) * P],
                                                   stack_f[:, t, which, g * HG:(g + 1) * HG, :].rearrange("p h s -> p (h s)"),
                                                   ident[:, :])
                    last.then_inc(sem(s, "kq_ps"), 1)
                    yield

                def scores(n):
                    h, i, g = unit(n)
                    r = h % HG * SLOT
                    if n == 0:
                        pe.wait_ge(*at(s, "kq", b, 8))
                    if n >= 2:
                        pe.wait_ge(*at(s, "mx", b, n - 1))
                    N = (i + 1) * P if causal else L
                    return nc.tensor.matmul(ps[:, SC + n % 2, 0:N], QT[r:r + MSLOT, g, i * P:(i + 1) * P],
                                            KT[r:r + MSLOT, g, 0:N], start=True, stop=True)

                def scores_masked(n):
                    i = unit(n)[1]
                    return nc.tensor.matmul(ps[:, SC + n % 2, i * P:(i + 1) * P], ident_h[:, :], causal_qk,
                                            start=False, stop=True, skip_group_check=True)

                def shifted(g):
                    u = turn(g)
                    pe.wait_ge(*at(s, "mx", b, (g + 1) * 16))
                    if u >= 2:
                        pe.wait_ge(*at(s, "keys_out", b, u - 1))
                    for t in range(NT):
                        last = nc.tensor.transpose(ps[:, SK + u % 2, t * P:(t + 1) * P],
                                                   stack_f[:, t, 0, g * HG:(g + 1) * HG, :].rearrange("p h s -> p (h s)"),
                                                   ident[:, :])
                    last.then_inc(sem(s, "keys_ps"), 1)

                def keys_first(n):
                    h, j, g = unit(n)
                    r, u = h % HG * SLOT, use(n)
                    pe.wait_ge(*at(s, "keys_out", b, max(u - 1, turn(g) + 1)))
                    q0 = first(s, j)
                    return nc.tensor.matmul(ps[:, SK + u % 2, 0:L - q0], KT[r:r + SLOT, g, j * P:(j + 1) * P],
                                            QM[r:r + SLOT, g % 2, q0:L], start=True, stop=True)

                def keys_masked(n):
                    return nc.tensor.matmul(ps[:, SK + use(n) % 2, 0:P], ident_h[:, :], causal_kq,
                                            start=False, stop=True, skip_group_check=True)

                def both(n):
                    k, q = keys_first(n), scores(n + LEAD) if n + LEAD < UNITS else None
                    if causal:
                        k = keys_masked(n)
                    k.then_inc(sem(s, "keys_ps"), 1)
                    if q is not None:
                        if causal:
                            q = scores_masked(n + LEAD)
                        q.then_inc(sem(s, "sc_ps"), 1)

                def weigh(pair):
                    for n in pair:
                        h, j, g = unit(n)
                        r, q0 = h % HG * SLOT, first(s, j)
                        pe.wait_ge(*at(s, "keys_out", b, use(n) + 1))
                        if n % 16 == 0 and n:
                            pe.wait_ge(*at(s, "ev", b, g))
                        nc.tensor.matmul(ps[r:r + SLOT, PV, q0:L], vaug[:, j, h, :], prob[:, n % 4, q0:L],
                                         start=(j == 0), stop=True, skip_group_check=True).then_inc(sem(s, "pv"), 1)

                for n in range(0, LEAD, 2):
                    for k in (n, n + 1):
                        q = scores(k)
                        if causal:
                            q = scores_masked(k)
                        q.then_inc(sem(s, "sc_ps"), 1)
                    if n == 16:
                        shifted(0)
                    yield
                for n in range(0, UNITS, 2):
                    both(n)
                    yield
                    if n:
                        weigh((n - 2, n - 1))
                    both(n + 1)
                    if n % 16 == 12 and n // 16 + 1 < NG:
                        shifted(n // 16 + 1)
                    yield
                weigh((UNITS - 2, UNITS - 1))
                yield
                for g in range(NG):
                    if g == 0:
                        pe.wait_ge(*at(s, "ev", b, NG))
                        pe.wait_ge(*at(s, "mx", b, UNITS))
                    for t in range(NT):
                        last = nc.tensor.transpose(ps[:, g, t * P:(t + 1) * P], oT[:, g, t * P:(t + 1) * P], ident[:, :])
                    last.then_inc(sem(s, "ot_ps"), 1)
                    yield
                pe.wait_ge(*at(s, "ctx", b, NG))
                transpose4(heads, bank(PV)).then_inc(sem(s, "cT_ps"), 1)
                yield
                pe.wait_ge(*at(s, "cT", b, 1))
                for t in range(NT):
                    last = nc.tensor.matmul(ps[:, 0, t * P:(t + 1) * P], headsT[:, t * P:(t + 1) * P], wout[s][:, :],
                                            start=True, stop=True)
                last.then_inc(sem(s, "o_ps"), 1)
                yield
                for _ in range(2):
                    yield
                pe.wait_ge(*at(s, "res", b, 1))
                yield

            def local_layer(b, l):
                s = str(l)
                if l == 0:
                    pe.wait_ge(*at("A", "done", b, 1))
                else:
                    pe.wait_ge(*at("0", "out", b, 1))
                transpose4(xa if l == 0 else l_x, bank(OT)).then_inc(sem(s, "xT_ps"), 1)
                yield
                for u in range(3 * NT):
                    t, p = u // 3, u % 3
                    if u == 0:
                        pe.wait_ge(*at(s, "xT", b, 1))
                    if t and p < 2:
                        pe.wait_ge(*at(s, "roped", b, 2 * (t - 1) + p + 1))
                        pe.wait_ge(*at(s, "sq", b, 2 * (t - 1) + p + 1))
                    elif t:
                        pe.wait_ge(*at(s, "v", b, t))
                    nc.tensor.matmul(bank(OT + p), xsT[:, t * P:(t + 1) * P], lw_qkv[:, l, p * 512:(p + 1) * 512],
                                     start=True, stop=True).then_inc(sem(s, "qkv_ps"), 1)
                    yield
                    yield
                yield
                for n in range(8):
                    if n == 0:
                        pe.wait_ge(*at(s, "nrm", b, NT))
                        pe.wait_ge(*at(s, "v", b, NT))
                    if n >= 3:
                        pe.wait_ge(*at(s, "T", b, n - 2))
                    for t in range(NT):
                        m = nc.tensor.transpose(ps[:, OT + n % 3, t * P:(t + 1) * P],
                                                l_c[:, t, 2 * n:2 * n + 2, :].rearrange("p h d -> p (h d)"), ident[:, :])
                    m.then_inc(sem(s, "T_ps"), 1)
                    yield
                for m_ in range(2 * LH):
                    h = m_ // 2
                    r, k = h % 2 * LD, h // 2
                    if m_ == 0:
                        pe.wait_ge(*at(s, "T", b, 8))
                    if m_ >= 3:
                        pe.wait_ge(*at(s, "mx", b, m_ - 2))
                    for t in (m_ % 2 * 2, m_ % 2 * 2 + 1):
                        o = ps[:, OT + m_ % 3, t % 2 * BAND:(t % 2 + 1) * BAND]
                        k0 = max(t * P - WIN, 0)
                        N = (t + 1) * P - k0
                        nc.tensor.matmul(o, ident_h[:, :], band_qk if t else band_q0, start=True, stop=True)
                        m = nc.tensor.matmul(o[:, BAND - N:BAND], l_T[r:r + LD, k, t * P:(t + 1) * P],
                                             l_T[r:r + LD, 4 + k, k0:(t + 1) * P], start=False, stop=True,
                                             skip_group_check=True)
                    m.then_inc(sem(s, "sc_ps"), 1)
                    yield
                pe.wait_ge(*at(s, "mx", b, 2 * LH))
                for t in range(NT):
                    m = nc.tensor.transpose(ps[0:LH, OT, t * P:(t + 1) * P], nm[:, t, :], ident[:, :])
                m.then_inc(sem(s, "nm_ps"), 1)
                yield

                def weigh(h):
                    pe.wait_ge(*at(s, "ex", b, 2 * h + 2))
                    if h >= 1:
                        pe.wait_ge(*at(s, "o", b, h))
                    for t in range(NT):
                        o = ps[:, OT + 2, t * (LD + 1):(t + 1) * (LD + 1)]
                        pr = l_p[:, 2 * h % 4 + t // 2, t % 2 * BAND:(t % 2 + 1) * BAND]
                        m = nc.tensor.matmul(o, pr[:, 0:P], l_v[:, t, h, :], start=True, stop=True)
                        if t:
                            pr = l_p[:, 2 * h % 4 + (t - 1) // 2, (t - 1) % 2 * BAND:((t - 1) % 2 + 1) * BAND]
                            m = nc.tensor.matmul(o[0:WIN], pr[:, P:BAND], l_v[:, t - 1, h, :],
                                                 start=False, stop=True, skip_group_check=True)
                    m.then_inc(sem(s, "pv"), 1)

                for m_ in range(2 * LH):
                    h = m_ // 2
                    r, k = h % 2 * LD, h // 2
                    if m_ == 0:
                        pe.wait_ge(*at(s, "nmT", b, 1))
                    if m_ >= 2:
                        pe.wait_ge(*at(s, "ex", b, m_ - 1))
                    for t in (m_ % 2 * 2, m_ % 2 * 2 + 1):
                        q1 = min(t * P + BAND, L)
                        N = q1 - t * P
                        o = ps[:, OT + m_ % 2, t % 2 * BAND:t % 2 * BAND + N]
                        nc.tensor.matmul(o, ident_h[:, :], band_kq[:, 0:N], start=True, stop=False)
                        nc.tensor.matmul(o, pick_head[:, h:h + 1].broadcast_to([LH, P]), nmT[:, t * P:q1],
                                         start=False, stop=False)
                        m = nc.tensor.matmul(o, l_T[r:r + LD, 4 + k, t * P:(t + 1) * P], l_T[r:r + LD, k, t * P:q1],
                                             start=False, stop=True)
                    m.then_inc(sem(s, "st_ps"), 1)
                    if m_ % 2 and h >= 1:
                        weigh(h - 1)
                    yield
                weigh(LH - 1)
                yield
                for k in range(4):
                    if k == 0:
                        pe.wait_ge(*at(s, "o", b, LH))
                    if k >= 2:
                        pe.wait_ge(*at(s, "oT", b, k - 1))
                    for t in range(NT):
                        m = nc.tensor.transpose(ps[:, OT + k % 2, t * P:(t + 1) * P], l_o[:, t, k * P:(k + 1) * P],
                                                ident[:, :])
                    m.then_inc(sem(s, "oT_ps"), 1)
                    yield
                pe.wait_ge(*at(s, "oT", b, 4))
                for t in range(NT):
                    for k in range(4):
                        m = nc.tensor.matmul(ps[:, OT + 2, t * P:(t + 1) * P], l_oT[:, k, t * P:(t + 1) * P],
                                             lw_o[:, l, k, :], start=(k == 0), stop=(k == 3))
                m.then_inc(sem(s, "o_ps"), 1)
                yield
                pe.wait_ge(*at(s, "lm", b, 1))
                for t in range(NT):
                    o = ps[:, OT, t * 64:(t + 1) * 64]
                    m = nc.tensor.matmul(o, shift[:, 0, :], l_m[:, t, 64:128], start=True, stop=(t == 0))
                    if t:
                        m = nc.tensor.matmul(o, shift[:, 1, :], l_m[:, t - 1, 64:128], start=False, stop=True)
                m.then_inc(sem(s, "sh_ps"), 1)
                yield
                yield
                pe.wait_ge(*at(s, "hn", b, 1))
                transpose4(hn[1], bank(OT + 1)).then_inc(sem(s, "hT_ps"), 1)
                yield
                for u in range(6):
                    j, half = u // 2, 1 - u % 2
                    if u == 0:
                        pe.wait_ge(*at(s, "hT", b, 1))
                    if u in (3, 5):
                        pe.wait_ge(*at(s, "gel", b, (u - 3) // 2 + 1))
                    if u == 4:
                        pe.wait_ge(*at(s, "hid", b, 1))
                    c0 = half * HID + j * P
                    nc.tensor.matmul(ps[0:HB[j], OT + u % 3, :], lw_1[:, l, c0:c0 + HB[j]], hT[1][:, 2:L + 2],
                                     start=True, stop=True).then_inc(sem(s, "g_ps"), 1)
                    yield
                for t in range(NT):
                    if t == 0:
                        pe.wait_ge(*at(s, "hid", b, 3))
                    for j in range(3):
                        m = nc.tensor.matmul(ps[:, OT + 1, t * P:(t + 1) * P], hidT[0:HB[j], j, t * P:(t + 1) * P],
                                             lw_2[0:HB[j], l, j, :], start=(j == 0), stop=(j == 2))
                    if t == 3:
                        m.then_inc(sem(s, "f_ps"), 1)
                    if t % 2:
                        yield
                if l == 1:
                    yield
                    yield

            def experts(b, half):
                if half == 0:
                    yield
                    yield
                    pe.wait_ge(*at("M", "hn", b, 1))
                    transpose4(hn[1], bank(OT)).then_inc(sem("M", "hT_ps"), 1)
                    yield
                    pe.wait_ge(*at("M", "hT", b, 1))
                    for t in range(NT):
                        m = nc.tensor.matmul(ps[:, OT + 1, t * NE:(t + 1) * NE], hT[1][:, 2 + t * P:2 + (t + 1) * P],
                                             router[:, :], start=True, stop=True)
                    m.then_inc(sem("M", "lg_ps"), 1)
                    yield

                def project(e, t):
                    if t == 0:
                        pe.wait_ge(*at("M", "act", b, 4 * e + 4))
                        if e:
                            pe.wait_ge(*at("M", "acc", b, e))
                    for j in range(4):
                        m = nc.tensor.matmul(ps[:, OT + 2, t * P:(t + 1) * P], eact[:, e % 2, j, t * P:(t + 1) * P],
                                             e_pr[:, e, j, :], start=(j == 0), stop=(j == 3))
                    if t == NT - 1:
                        m.then_inc(sem("M", "e_ps"), 1)

                for n in range(8 * half, 8 * half + 8):
                    e, j = n // 4, n % 4
                    if n:
                        pe.wait_ge(*at("M", "sil", b, n))
                    nc.tensor.matmul(bank(OT), e_wv[:, e, j * P:(j + 1) * P], hT[1][:, 2:L + 2],
                                     start=True, stop=True).then_inc(sem("M", "g_ps"), 1)
                    yield
                    if n:
                        pe.wait_ge(*at("M", "act", b, n))
                    else:
                        pe.wait_ge(*at("M", "lg", b, 1))
                    nc.tensor.matmul(bank(OT + 1), e_wv[:, e, FF + j * P:FF + (j + 1) * P], hT[1][:, 2:L + 2],
                                     start=True, stop=True).then_inc(sem("M", "v_ps"), 1)
                    yield
                    if e:
                        project(e - 1, j)
                        yield
                if half == 1:
                    for t in range(NT):
                        project(NE - 1, t)
                        yield
                    for _ in range(2):
                        yield

            batch_loop(pe, attention, local_layer, experts)

        @block.scalar
        def _(act):
            act.wait_ge(loaded_first, 16 * n_loads["first"])

            def copy(dst, src):
                return nc.scalar.activation(dst, src, ACT.Copy)

            def attention(b, s):
                if s != "D":
                    act.wait_ge(*at(s, "xT_ps", b, 1))
                    copy(xT[:, :], bank(0)).then_inc(sem(s, "xT"), 1)
                    yield
                else:
                    yield
                    yield
                    act.wait_ge(*at("N", "xT_ps", b, 1))
                    nc.scalar.activation(hT[0][:, 2:L + 2], bank(0), ACT.Identity, scale=ln1[:, 0:1],
                                         bias=ln1[:, 1:2]).then_inc(sem("N", "hT"), 1)
                    yield
                    yield
                for _ in range(NT + 4):
                    yield
                for n in range(8):
                    act.wait_ge(*at(s, "kq_ps", b, n + 1))
                    copy((KT, QT)[n % 2][:, n // 2, :], bank(n % 4)).then_inc(sem(s, "kq"), 1)
                    yield

                def turned(g):
                    act.wait_ge(*at(s, "keys_ps", b, turn(g) + 1))
                    copy(QM[:, g % 2, :], bank(SK + turn(g) % 2)).then_inc(sem(s, "keys_out"), 1)

                def sums(g):
                    act.wait_ge(*at(s, "pv", b, 16 * (g + 1)))
                    copy(oT[:, g, :], bank(PV)).then_inc(sem(s, "ev"), 1)

                for n in range(0, LEAD, 2):
                    if n == 16:
                        turned(0)
                    yield
                for n in range(UNITS):
                    j, u = unit(n)[1], use(n)
                    act.wait_ge(*at(s, "keys_ps", b, u + 1))
                    if n >= 4:
                        act.wait_ge(*at(s, "pv", b, n - 3))
                    q0 = first(s, j)
                    nc.scalar.activation(prob[:, n % 4, q0:L], ps[:, SK + u % 2, 0:L - q0], ACT.Exp,
                                         scale=float(HD) ** -0.5).then_inc(sem(s, "keys_out"), 1)
                    if n % 16 == 1 and n > 1:
                        sums(n // 16 - 1)
                    if n % 16 == 13 and n // 16 + 1 < NG:
                        turned(n // 16 + 1)
                    yield
                sums(NG - 1)
                yield
                for g in range(NG):
                    yield
                act.wait_ge(*at(s, "cT_ps", b, 1))
                copy(headsT, bank(PV)).then_inc(sem(s, "cT"), 1)
                yield
                for _ in range(4):
                    yield

            def local_layer(b, l):
                s = str(l)
                act.wait_ge(*at(s, "xT_ps", b, 1))
                copy(xsT[0:64, :], ps[0:64, OT, :])
                copy(xsT[64:128, 1:L], ps[64:128, OT, 0:L - 1]).then_inc(sem(s, "xT"), 1)
                yield
                for u in range(3 * NT):
                    t, p = u // 3, u % 3
                    act.wait_ge(*at(s, "qkv_ps", b, u + 1))
                    if p < 2:
                        w = 2 * t + p
                        if w >= 2:
                            act.wait_ge(*at(s, "roped", b, w - 1))
                        nc.scalar.activation(sq[:, w % 2, :], bank(OT + p), ACT.Square).then_inc(sem(s, "sq"), 1)
                    else:
                        copy(l_v[:, t, :, 0:LD], bank(OT + 2).rearrange("p (h d) -> p h d", d=LD)).then_inc(sem(s, "v"), 1)
                    yield
                    yield
                yield
                for n in range(8):
                    act.wait_ge(*at(s, "T_ps", b, n + 1))
                    copy(l_T[:, n, :], bank(OT + n % 3)).then_inc(sem(s, "T"), 1)
                    yield
                for _ in range(2 * LH):
                    yield
                act.wait_ge(*at(s, "nm_ps", b, 1))
                copy(nmT[:, :], ps[0:LH, OT, :]).then_inc(sem(s, "nmT"), 1)
                yield
                for m in range(2 * LH):
                    act.wait_ge(*at(s, "st_ps", b, m + 1))
                    if m >= 4:
                        act.wait_ge(*at(s, "pv", b, m // 2 - 1))
                    n = 2 * BAND if m % 2 == 0 else BAND + P
                    nc.scalar.activation(l_p[:, m % 4, 0:n], ps[:, OT + m % 2, 0:n], ACT.Exp,
                                         scale=8.0).then_inc(sem(s, "ex"), 1)
                    yield
                yield
                for k in range(4):
                    act.wait_ge(*at(s, "oT_ps", b, k + 1))
                    copy(l_oT[:, k, :], bank(OT + k % 2)).then_inc(sem(s, "oT"), 1)
                    yield
                for _ in range(3):
                    yield
                act.wait_ge(*at(s, "hT_ps", b, 1))
                nc.scalar.activation(hT[1][:, 2:L + 2], bank(OT + 1), ACT.Identity, scale=l_gb[:, l, 0:1],
                                     bias=l_gb[:, l, 1:2]).then_inc(sem(s, "hT"), 1)
                yield
                for u in range(6):
                    j = u // 2
                    if u % 2 == 0:
                        act.wait_ge(*at(s, "g_ps", b, u + 1))
                        n = HB[j]
                        nc.scalar.activation(gel[0:n, j, :], ps[0:n, OT + u % 3, :], ACT.Gelu,
                                             bias=lb_1[0:n, l, 1, j:j + 1]).then_inc(sem(s, "gel"), 1)
                    yield
                for _ in range(2 if l == 0 else 4):
                    yield

            def experts(b, half):
                if half == 0:
                    yield
                    yield
                    act.wait_ge(*at("M", "hT_ps", b, 1))
                    nc.scalar.activation(hT[1][:, 2:L + 2], bank(OT), ACT.Identity, scale=ln2[:, 0:1],
                                         bias=ln2[:, 1:2]).then_inc(sem("M", "hT"), 1)
                    yield
                    yield
                for n in range(8 * half, 8 * half + 8):
                    act.wait_ge(*at("M", "g_ps", b, n + 1))
                    if n >= 2:
                        act.wait_ge(*at("M", "act", b, n - 1))
                    nc.scalar.activation(sil[:, n % 2, :], bank(OT), ACT.Silu).then_inc(sem("M", "sil"), 1)
                    for _ in range(2 if n < 4 else 3):
                        yield
                for _ in range(NT + 2 if half == 1 else 0):
                    yield

            batch_loop(act, attention, local_layer, experts)

        @block.gpsimd
        def _(pool):
            nc.gpsimd.memset(m_half[:, :], -0.5).then_inc(sem("S", "stored"), 16)
            nc.gpsimd.memset(one[:, :], 1.0)
            nc.gpsimd.memset(xsT[:, 0:1], 0.0)
            for k in range(2):
                nc.gpsimd.memset(hT[k][:, 0:2], 0.0)
            nc.gpsimd.memset(stack_f[:, :, :, :, MSLOT:SLOT].rearrange("p t w h s -> p (t w h) s"), 0.0)
            nc.gpsimd.memset(vaug[:, :, :, :].rearrange("p t h s -> p (t h) s"), 0.0).then_inc(presets, 1)
            nc.gpsimd.memset(l_v[:, :, :, LD:LD + 1].rearrange("p t h s -> p (t h) s"), 1.0)
            pool.wait_ge(presets, 1)
            nc.gpsimd.memset(vaug[:, :, :, HD:HD + 1].rearrange("p t h s -> p (t h) s"), 1.0)
            nc.gpsimd.memset(stack_f[:, :, 1, :, MSLOT:MSLOT + 1], 1.0).then_inc(consts_ready, 1)
            pool.wait_ge(consts_ready, 3)

            def norm_root(b, s, k):
                pool.wait_ge(*at(s, "var", b, 1))
                nc.gpsimd.tensor_tensor(rstd[k][:, :], mv[k][:, :, 1], m_half[:, 0:NT], ALU.pow).then_inc(sem(s, "rstd"), 1)

            def attention(b, s):
                if s == "D":
                    norm_root(b, "N", 0)
                    for _ in range(4):
                        yield
                else:
                    yield
                for _ in range(NT + 3):
                    yield
                pool.wait_ge(*at(s, "stacked", b, 1))
                ones = one[:, :].rearrange("p (t h d) -> p t h d", t=1, h=1).broadcast_to([P, NT, H, HD])
                for side, to in ((0, 2 * HD), (1, HD)):
                    hi = stack_f[:, :, side, :, 0:HD]
                    last = nc.gpsimd.tensor_tensor(stack[:, :, side, :, to:to + HD], hi, ones, ALU.mult)
                last.then_inc(sem(s, "dup"), 1)
                yield
                for _ in range(8 + LEAD // 2 + UNITS + 1 + NG + 2 + 1):
                    yield
                if s != "D":
                    norm_root(b, s, 0)
                yield
                yield

            def local_layer(b, l):
                s = str(l)
                yield
                for u in range(3 * NT):
                    t, p = u // 3, u % 3
                    if p < 2:
                        w = 2 * t + p
                        pool.wait_ge(*at(s, "roped", b, w + 1))
                        half = l_c[:, t, p * LH:(p + 1) * LH, :]
                        nc.gpsimd.tensor_tensor(half, half, l_s[:, w % 2, :, :], ALU.add).then_inc(sem(s, "added"), 1)
                    else:
                        pool.wait_ge(*at(s, "ssum", b, t + 1))
                        nc.gpsimd.tensor_tensor(rn[:, t, :], ssum[:, t, :], m_half[:, 0:2 * LH], ALU.pow).then_inc(sem(s, "rn"), 1)
                        pool.wait_ge(*at(s, "rn", b, t + 1))
                        pool.wait_ge(*at(s, "added", b, 2 * t + 2))
                        nc.gpsimd.tensor_tensor(l_c[:, t, :, :], l_c[:, t, :, :],
                                                rn[:, t, :].rearrange("p (h a) -> p h a", a=1).broadcast_to([P, 2 * LH, LD]),
                                                ALU.mult).then_inc(sem(s, "nrm"), 1)
                    yield
                    yield
                yield
                for _ in range(8 + 4 * LH + 2 + 4 + 1):
                    yield
                norm_root(b, s, 1)
                for _ in range(3 + 6 + 2):
                    yield
                if l == 1:
                    yield
                    norm_root(b, "B", 1)
                    yield
                yield

            def experts(b, half):
                if half == 0:
                    norm_root(b, "M", 1)
                    for _ in SEGS["M"]:
                        yield
                else:
                    for _ in SEGS["E"][:-1]:
                        yield
                    norm_root(b, "F", 1)
                    yield

            batch_loop(pool, attention, local_layer, experts)

        @block.vector
        def _(dve):
            dve.wait_ge(loaded_first, 16 * n_loads["first"])
            nc.vector.tensor_copy(ident_h[:, :], ident[:, :])
            nc.vector.tensor_copy(pick_head[:, :], ident[0:LH, 0:LH])
            nc.vector.tensor_copy(mask_h[:, :], mask_f[:, :])
            for l in range(2):
                for cs in range(2):
                    for w in range(2):
                        last = nc.vector.tensor_tensor(tab[:, l, :, cs, w, :], xpos[:, :, cs, w, :],
                                                       l_scale[:, l, cs, w, :].rearrange("p (a d) -> p a d", a=1).broadcast_to([P, NT, LD]),
                                                       ALU.mult)
            last.then_inc(consts_ready, 2)
            dve.wait_ge(consts_ready, 3)

            class Steps:

                def __init__(self, b, s):
                    self.b, self.s, self.n = b, s, 0

                def settle(self, ins):
                    self.n += 1
                    ins.then_inc(sem(self.s, "step"), 1)
                    dve.wait_ge(*at(self.s, "step", self.b, self.n))

                def end(self):
                    assert self.n == STEPS[self.s], (self.s, self.n)

            def statistics(st, b, s, k, src, upper=None):
                for t in range(NT):
                    if upper is None:
                        last = nc.vector.bn_stats(stats[k][:, t, 0, :], src[:, t, :])
                    else:
                        nc.vector.bn_stats(stats[k][:, t, 0, :], src[:, t, 0:64])
                        last = nc.vector.bn_stats(stats[k][:, t, 1, :], upper[:, t * 64:(t + 1) * 64])
                st.settle(last)
                nc.vector.tensor_copy(held[:, :], ident[:, 0:1])
                for t in range(NT):
                    w = stats[k][:, t, 0, :] if upper is None else stats[k][:, t, :, :].rearrange("p a n -> p (a n)")
                    last = nc.vector.bn_aggr(mv[k][:, t, :], w)
                st.settle(last)
                nc.vector.tensor_scalar(mv[k][:, :, 1], mv[k][:, :, 1], EPS, None, ALU.add).then_inc(sem(s, "var"), 1)

            def normalise(b, s, k, dst, src):
                dve.wait_ge(*at(s, "rstd", b, 1))
                for t in range(NT):
                    last = nc.vector.tensor_scalar(dst[:, t, :], src[:, t, :], mv[k][:, t, 0:1], rstd[k][:, t:t + 1],
                                                   ALU.subtract, ALU.mult)
                return last

            def attention(b, s):
                st = Steps(b, s)
                if s == "D":
                    sn = Steps(b, "N")
                    statistics(sn, b, "N", 0, xc)
                    yield
                    normalise(b, "N", 0, hn[0], xc).then_inc(sem("N", "done"), 1)
                    yield
                    yield
                    dve.wait_ge(*at("N", "hT", b, 1))
                    sn.settle(nc.vector.tensor_scalar(xT[:, :], hT[0][:, 0:L], conv[:, 0:1], None, ALU.mult))
                    sn.settle(nc.vector.scalar_tensor_tensor(xT[:, :], hT[0][:, 1:L + 1], conv[:, 1:2], xT[:, :], ALU.mult, ALU.add))
                    nc.vector.scalar_tensor_tensor(xT[:, :], hT[0][:, 2:L + 2], conv[:, 2:3], xT[:, :], ALU.mult,
                                                   ALU.add).then_inc(sem("D", "xT"), 1)
                    sn.end()
                    yield
                else:
                    yield
                for t in range(NT):
                    dve.wait_ge(*at(s, "qkv_ps", b, t + 1))
                    o = work[:, 0, t * 2 * C:(t + 1) * 2 * C]
                    v = ps[:, t, 2 * C:3 * C].rearrange("p (h d) -> p h d", d=HD)
                    if s == "A":
                        nc.vector.tensor_tensor(o, ps[:, t, 0:2 * C], bqkv[:, 0:2 * C], ALU.add)
                        last = nc.vector.tensor_tensor(vaug[:, t, :, 0:HD], v,
                                                       bqkv[:, 2 * C:3 * C].rearrange("p (h d) -> p h d", d=HD), ALU.add)
                    else:
                        nc.vector.tensor_copy(o, ps[:, t, 0:2 * C])
                        last = nc.vector.tensor_copy(vaug[:, t, :, 0:HD], v)
                    if t < NT - 1:
                        yield
                st.settle(last)
                yield
                src = qk
                if s in rope:
                    c = rope[s][:, :, 0:1, :].broadcast_to([P, NT, 2 * H, HD])
                    n = rope[s][:, :, 1:2, :].broadcast_to([P, NT, 2 * H, HD])
                    hf = HD // 2
                    nc.vector.tensor_tensor(qk_c, qk, c, ALU.mult)
                    nc.vector.tensor_tensor(qk_s[:, :, :, 0:hf], qk[:, :, :, hf:HD], n[:, :, :, 0:hf], ALU.mult)
                    st.settle(nc.vector.tensor_tensor(qk_s[:, :, :, hf:HD], qk[:, :, :, 0:hf], n[:, :, :, hf:HD], ALU.mult))
                yield
                if s in rope:
                    st.settle(nc.vector.tensor_tensor(qk_c, qk_c, qk_s, ALU.add))
                    src = qk_c
                yield
                sv = stack[:, :, :, :, :].rearrange("p t w h s -> p (t w h) s")
                st.settle(nc.vector.tensor_copy(sv[:, :, 0:HD], src.rearrange("p t h d -> p (t h) d")))
                yield
                nc.vector.tensor_tensor(stack[:, :, 0, :, HD:2 * HD], src[:, :, 0:H, :], stack_f[:, :, 0, :, 0:HD], ALU.subtract)
                nc.vector.tensor_tensor(stack[:, :, 1, :, 2 * HD:3 * HD], src[:, :, H:2 * H, :], stack_f[:, :, 1, :, 0:HD],
                                        ALU.subtract).then_inc(sem(s, "stacked"), 1)
                yield
                for _ in range(8):
                    yield

                def maximum(n):
                    h, i, _ = unit(n)
                    dve.wait_ge(*at(s, "sc_ps", b, n + 1))
                    N = L if s == "C" else (i + 1) * P
                    nc.vector.tensor_reduce(stack[:, i, 0, h, MSLOT:MSLOT + 1], ps[:, SC + n % 2, 0:N], X, ALU.max,
                                            negate=True).then_inc(sem(s, "mx"), 1)

                for n in range(0, LEAD, 2):
                    maximum(n)
                    maximum(n + 1)
                    yield
                for n in range(UNITS):
                    if n + LEAD < UNITS:
                        maximum(n + LEAD)
                    yield
                yield
                for g in range(NG):
                    dve.wait_ge(*at(s, "ot_ps", b, g + 1))
                    o = bank(g).rearrange("p (t h e) -> p t h e", t=NT, e=SLOT)
                    rd = rden[:, g, :, :].rearrange("p t (h a) -> p t h a", a=1)
                    st.settle(nc.vector.reciprocal(rd, o[:, :, :, HD:HD + 1]))
                    nc.vector.tensor_tensor(heads[:, :, g * HG * HD:(g + 1) * HG * HD].rearrange("p t (h d) -> p t h d", d=HD),
                                            o[:, :, :, 0:HD], rd.broadcast_to([P, NT, HG, HD]),
                                            ALU.mult).then_inc(sem(s, "ctx"), 1)
                    yield
                yield
                if s == "A":
                    nc.vector.tensor_tensor(xa[:, :, :], xin[:, :, :], tiled(bout[:, :]), ALU.add).then_inc(sem("A", "used"), 1)
                    dve.wait_ge(*at("A", "used", b, 1))
                yield
                dve.wait_ge(*at(s, "o_ps", b, 1))
                if s == "A":
                    nc.vector.tensor_tensor(xa[:, :, :], four(0), xa[:, :, :], ALU.add).then_inc(sem(s, "res"), 1)
                    x = xa
                elif s == "C":
                    nc.vector.scalar_tensor_tensor(xc[:, :, :], xb[:, :, :], 2.0, four(0), ALU.mult, ALU.add).then_inc(sem(s, "res"), 1)
                    x = xc
                else:
                    nc.vector.tensor_tensor(yd[:, :, :], four(0), xc[:, :, :], ALU.add).then_inc(sem("D", "res"), 1)
                yield
                if s != "D":
                    dve.wait_ge(*at(s, "res", b, 1))
                    statistics(st, b, s, 0, x)
                yield
                if s != "D":
                    normalise(b, s, 0, x, x).then_inc(sem(s, "done"), 1)
                    dve.wait_ge(*at(s, "done", b, 1))
                st.end()
                yield

            def tiled(v):
                return v.rearrange("p (a c) -> p a c", a=1).broadcast_to([P, NT, C])

            def local_layer(b, l):
                s = str(l)
                st = Steps(b, s)
                hf = LD // 2
                yield
                for u in range(3 * NT):
                    t, p = u // 3, u % 3
                    if p < 2:
                        w = 2 * t + p
                        dve.wait_ge(*at(s, "sq", b, w + 1))
                        z = bank(OT + p).rearrange("p (h d) -> p h d", d=LD)
                        c = tab[:, l, t, 0, p, :].rearrange("p (a d) -> p a d", a=1).broadcast_to([P, LH, LD])
                        n = tab[:, l, t, 1, p, :].rearrange("p (a d) -> p a d", a=1).broadcast_to([P, LH, LD])
                        if w >= 2:
                            dve.wait_ge(*at(s, "added", b, w - 1))
                        nc.vector.tensor_tensor(l_c[:, t, p * LH:(p + 1) * LH, :], z, c, ALU.mult)
                        nc.vector.tensor_tensor(l_s[:, w % 2, :, 0:hf], z[:, :, hf:LD], n[:, :, 0:hf], ALU.mult)
                        nc.vector.tensor_tensor(l_s[:, w % 2, :, hf:LD], z[:, :, 0:hf], n[:, :, hf:LD], ALU.mult)
                        yield
                        nc.vector.tensor_reduce(ssum[:, t, p * LH:(p + 1) * LH], sq[:, w % 2, :].rearrange("p (h d) -> p h d", d=LD),
                                                X, ALU.add).then_inc(sem(s, "roped"), 1)
                    else:
                        dve.wait_ge(*at(s, "roped", b, 2 * t + 2))
                        nc.vector.tensor_scalar(ssum[:, t, :], ssum[:, t, :], 1e-24, None, ALU.max).then_inc(sem(s, "ssum"), 1)
                        yield
                    yield
                yield
                for _ in range(8):
                    yield
                for m in range(2 * LH):
                    h, a = m // 2, m % 2
                    dve.wait_ge(*at(s, "sc_ps", b, m + 1))
                    nc.vector.tensor_reduce(nm[:, 2 * a:2 * a + 2, h], ps[:, OT + m % 3, 0:2 * BAND].rearrange("p (c n) -> p c n", c=2),
                                            X, ALU.max, negate=True).then_inc(sem(s, "mx"), 1)
                    yield
                yield

                def divided(h):
                    dve.wait_ge(*at(s, "pv", b, h + 1))
                    o = ps[:, OT + 2, 0:NT * (LD + 1)].rearrange("p (t e) -> p t e", t=NT)
                    rd = l_rd[:, h % 2, :].rearrange("p (t a) -> p t a", a=1)
                    st.settle(nc.vector.reciprocal(rd, o[:, :, LD:LD + 1]))
                    nc.vector.tensor_tensor(l_o[:, :, h * LD:(h + 1) * LD], o[:, :, 0:LD], rd.broadcast_to([P, NT, LD]),
                                            ALU.mult).then_inc(sem(s, "o"), 1)

                for m in range(2 * LH):
                    if m % 2 and m >= 3:
                        divided(m // 2 - 1)
                    yield
                divided(LH - 1)
                yield
                for _ in range(4):
                    yield
                dve.wait_ge(*at(s, "o_ps", b, 1))
                nc.vector.tensor_tensor(l_m[:, :, :], four(OT + 2), (xa if l == 0 else l_x)[:, :, :], ALU.add).then_inc(sem(s, "lm"), 1)
                yield
                dve.wait_ge(*at(s, "sh_ps", b, 1))
                statistics(st, b, s, 1, l_m, upper=bank(OT))
                yield
                dve.wait_ge(*at(s, "rstd", b, 1))
                for t in range(NT):
                    nc.vector.tensor_scalar(hn[1][:, t, 0:64], l_m[:, t, 0:64], mv[1][:, t, 0:1], rstd[1][:, t:t + 1],
                                            ALU.subtract, ALU.mult)
                    last = nc.vector.tensor_scalar(hn[1][:, t, 64:128], ps[:, OT, t * 64:(t + 1) * 64], mv[1][:, t, 0:1],
                                                   rstd[1][:, t:t + 1], ALU.subtract, ALU.mult)
                last.then_inc(sem(s, "hn"), 1)
                dst = l_x if l == 0 else xb
                st.settle(nc.vector.tensor_tensor(dst[:, :, :], l_m[:, :, :], tiled(lb_2[:, l, :]), ALU.add))
                yield
                yield
                for u in range(6):
                    if u % 2:
                        j = u // 2
                        n = HB[j]
                        dve.wait_ge(*at(s, "g_ps", b, u + 1))
                        dve.wait_ge(*at(s, "gel", b, j + 1))
                        nc.vector.scalar_tensor_tensor(hidT[0:n, j, :], ps[0:n, OT + u % 3, :], lb_1[0:n, l, 0, j:j + 1],
                                                       gel[0:n, j, :], ALU.add, ALU.mult).then_inc(sem(s, "hid"), 1)
                    yield
                yield
                dve.wait_ge(*at(s, "f_ps", b, 1))
                nc.vector.tensor_tensor(dst[:, :, :], four(OT + 1), dst[:, :, :], ALU.add).then_inc(sem(s, "out"), 1)
                dve.wait_ge(*at(s, "out", b, 1))
                st.end()
                if l == 1:
                    st = Steps(b, "B")
                    yield
                    st.settle(nc.vector.tensor_tensor(xb[:, :, :], xa[:, :, :], xb[:, :, :], ALU.add))
                    statistics(st, b, "B", 1, xb)
                    yield
                    normalise(b, "B", 1, xb, xb).then_inc(sem("B", "done"), 1)
                    dve.wait_ge(*at("B", "done", b, 1))
                    st.end()
                yield

            def experts(b, half):
                if half == 0:
                    st = Steps(b, "M")
                    dve.wait_ge(*at("D", "res", b, 1))
                    statistics(st, b, "M", 1, yd)
                    yield
                    normalise(b, "M", 1, hn[1], yd).then_inc(sem("M", "hn"), 1)
                    nc.vector.tensor_tensor(xc[:, :, :], xc[:, :, :], yd[:, :, :], ALU.add)
                    yield
                    yield
                    dve.wait_ge(*at("M", "lg_ps", b, 1))
                    nc.vector.tensor_copy(lg[:, :, :], ps[:, OT + 1, 0:NT * NE].rearrange("p (t e) -> p t e", e=NE)).then_inc(sem("M", "lg"), 1)
                    dve.wait_ge(*at("M", "lg", b, 1))
                    st.settle(nc.vector.tensor_reduce(lmax[:, :], lg[:, :, :], X, ALU.max))
                    for e in range(NE):
                        st.settle(nc.vector.tensor_tensor(pick[:, :, e], lg[:, :, e], lmax[:, :], ALU.is_ge))
                        if e == 0:
                            st.settle(nc.vector.tensor_scalar(free[:, :], pick[:, :, 0], -1.0, 1.0, ALU.mult, ALU.add))
                        else:
                            st.settle(nc.vector.tensor_tensor(pick[:, :, e], pick[:, :, e], free[:, :], ALU.mult))
                            st.settle(nc.vector.tensor_tensor(free[:, :], free[:, :], pick[:, :, e], ALU.subtract))
                    st.end()
                    yield

                def gather(e):
                    dve.wait_ge(*at("M", "e_ps", b, e + 1))
                    if e >= 1:
                        dve.wait_ge(*at("M", "acc", b, e))
                    for t in range(NT):
                        last = nc.vector.scalar_tensor_tensor(xc[:, t, :], ps[:, OT + 2, t * P:(t + 1) * P], pick[:, t, e:e + 1],
                                                              xc[:, t, :], ALU.mult, ALU.add)
                    last.then_inc(sem("M", "acc"), 1)

                for n in range(8 * half, 8 * half + 8):
                    e, j = n // 4, n % 4
                    yield
                    dve.wait_ge(*at("M", "v_ps", b, n + 1))
                    dve.wait_ge(*at("M", "sil", b, n + 1))
                    if j == 0 and e >= 2:
                        dve.wait_ge(*at("M", "e_ps", b, e - 1))
                    nc.vector.tensor_tensor(eact[:, e % 2, j, :], bank(OT + 1), sil[:, n % 2, :],
                                            ALU.mult).then_inc(sem("M", "act"), 1)
                    yield
                    if e >= 1:
                        if j == 3:
                            gather(e - 1)
                        yield
                if half == 0:
                    return
                for t in range(NT - 1):
                    yield
                gather(NE - 1)
                yield
                dve.wait_ge(*at("M", "acc", b, NE))
                st = Steps(b, "F")
                statistics(st, b, "F", 1, xc)
                yield
                dve.wait_ge(*at("S", "stored", b, 16))
                normalise(b, "F", 1, yo, xc).then_inc(sem("S", "y"), 1)
                st.end()
                yield

            batch_loop(dve, attention, local_layer, experts)


_OUTS = [((B, L, C), "float32")]


def constants():
    import numpy as np
    f = np.float32
    ar = np.arange
    i = ar(P)
    masks = np.zeros((P, 2 * P + 3 * BAND), f)
    masks[:, 0:P] = np.where(i[None, :] > i[:, None], NEG, 0)
    masks[:, P:2 * P] = np.where(i[:, None] > i[None, :], NEG, 0)
    k = ar(BAND)[None, :] - WIN
    q = i[:, None]
    ok = (k <= q) & (k >= q - WIN)
    masks[:, 2 * P:2 * P + BAND] = np.where(ok, 0, NEG)
    masks[:, 2 * P + BAND:2 * P + 2 * BAND] = np.where(ok & (k >= 0), 0, NEG)
    kk, qq = i[:, None], ar(BAND)[None, :]
    masks[:, 2 * P + 2 * BAND:] = np.where((qq >= kk) & (qq <= kk + WIN), 0, NEG)
    shift = np.zeros((P, 2, P), f)
    shift[i[:-1], 0, i[1:]] = 1
    shift[P - 1, 1, 0] = 1
    pos = ar(L).astype(f)

    def tiles(a):
        return np.ascontiguousarray(a.reshape((NT, P) + a.shape[1:]).swapaxes(0, 1).astype(f))

    def rope(angle):
        c, s = np.cos(angle).astype(f), np.sin(angle).astype(f)
        return tiles(np.stack([np.concatenate([c, c], -1), np.concatenate([-s, s], -1)], 1))

    frac = (2 * ar(HD // 2) / HD).astype(f)
    a_A = (pos[:, None] / np.power(f(1250), frac)[None, :]).astype(f)
    a_D = (pos[:, None] * (f(1) / np.power(f(10000), (ar(0, HD, 2).astype(f) / f(HD))))[None, :]).astype(f)
    half = ar(0, LD, 2).astype(f)
    inv = (f(1) / np.power(f(10000), half / f(LD))).astype(f)
    fr = (pos[:, None] * inv[None, :]).astype(f)
    base = ((half + f(0.4 * LD)) / f(1.4 * LD)).astype(f)
    power = ((pos - L // 2) / f(WIN // 2)).astype(f)
    sc = np.power(base[None, :], power[:, None]).astype(f)
    c, s = np.cos(fr).astype(f), np.sin(fr).astype(f)
    cc, ss, sc2 = np.concatenate([c, c], -1), np.concatenate([-s, s], -1), np.concatenate([sc, sc], -1)
    xpos = np.stack([np.stack([cc * sc2, cc / sc2], 1), np.stack([ss * sc2, ss / sc2], 1)], 1)
    return {"ident": np.eye(P, dtype=f), "masks": masks, "shift": shift,
            "rope_A": rope(a_A), "rope_D": rope(a_D), "xpos": tiles(xpos)}


def kernel(**inputs):
    import numpy as _np
    import concourse.bacc as _bacc
    from concourse import mybir as _mybir
    from concourse.bass_utils import run_bass_kernel_spmd as _run

    nc = _bacc.Bacc("TRN2", target_bir_lowering=False, num_devices=1,
                     dynamic_dma_scratch_size=1024)
    arrays, ins, consts = {}, {}, {}
    for name, a in inputs.items():
        if name == "L1_attn_mask":
            continue
        a = _np.ascontiguousarray(a)
        arrays[f"in_{name}_dram"] = a
        ins[name] = nc.dram_tensor(f"in_{name}_dram", a.shape, _mybir.dt.from_np(a.dtype), kind="ExternalInput").ap()
    for name, a in constants().items():
        arrays[f"const_{name}_dram"] = a
        consts[name] = nc.dram_tensor(f"const_{name}_dram", a.shape, _mybir.dt.from_np(a.dtype), kind="ExternalInput").ap()
    shape, dtype = _OUTS[0]
    out = nc.dram_tensor("out_0_dram", shape, _mybir.dt.from_np(_np.dtype(dtype)), kind="ExternalOutput").ap()
    network_kernel(nc, ins, consts, out)
    r = _run(nc, [arrays], core_ids=[0])
    return r.results[0]["out_0_dram"]
```
